# Optimizing a Trainium2 kernel written in Bass

```python
import numpy as np
import jax
import jax.numpy as jnp

def _softmax(x, axis=-1):
    return jax.nn.softmax(x, axis=axis)

def _gelu(x):
    return jax.nn.gelu(x, approximate=True)

def _silu(x):
    return jax.nn.silu(x)

def _sigmoid(x):
    return jax.nn.sigmoid(x)

def _layernorm(x, axis=-1, eps=1e-05):
    m = jnp.mean(x, axis=axis, keepdims=True)
    v = jnp.var(x, axis=axis, keepdims=True)
    return (x - m) / jnp.sqrt(v + eps)

def _scatter_add(tgt, idx, src, axis=0):
    return tgt.at[idx].add(src)

def _segment_sum(src, seg, n):
    return jax.ops.segment_sum(src, seg, n)
kernel_name = 'mk_adj_preln_d4_adj_r2_574c8e'

def setup_inputs(seed: int=0):
    np.random.seed(seed)
    _w = jnp.asarray

    def _rec_inputs():
        import jax
        import jax.numpy as jnp
        _gk = jax.random.key(seed)
        x = -9.806e-05 + 1 * jax.random.normal(jax.random.fold_in(_gk, 1), (4096, 128), jnp.float32)
        _w = (1.0 + jnp.arange(4096, dtype=jnp.float32)) ** (-0.5)
        _w = _w / _w.mean()
        _pij = jnp.clip(0.00390625 * _w[:, None] * _w[None, :], 0.0, 1.0)
        _a = jax.random.uniform(jax.random.fold_in(_gk, 2), (4096, 4096)) < _pij
        _a = jnp.logical_or(_a, jnp.eye(4096, dtype=bool))
        _af = _a.astype(jnp.float32)
        adj = _af
        return (x, adj)
    x, adj = _rec_inputs()

    def _L0_gnn_setup():
        import jax, jax.numpy as jnp
        import numpy as np
        N, IN_DIM, OUT_DIM, HEADS = (2048, 128, 32, 4)
        EDGE_PROB = 0.015
        key = jax.random.key(seed)
        k1, k2, k3, k4 = jax.random.split(key, 4)
        x = jax.random.normal(k1, (N, IN_DIM), dtype=jnp.float32)
        adj = (jax.random.uniform(k2, (N, N)) < EDGE_PROB).astype(jnp.float32)
        adj = jnp.maximum(adj, jnp.eye(N, dtype=jnp.float32))
        W = jax.random.normal(k3, (IN_DIM, OUT_DIM * HEADS), dtype=jnp.float32) / np.sqrt(IN_DIM).astype(np.float32)
        a = jax.random.normal(k4, (2 * OUT_DIM,), dtype=jnp.float32) / np.sqrt(2 * OUT_DIM).astype(np.float32)
        return {'x': x, 'adj': adj, 'W': W, 'a': a}
    _L0_gnn_all = _L0_gnn_setup()
    _L0_gnn_in = {k: v for k, v in _L0_gnn_all.items() if k in ('W', 'a')}
    del _L0_gnn_all

    def _L1_gnn_setup():
        import jax, jax.numpy as jnp
        import numpy as np
        key = jax.random.key(seed)
        k1, k2, k3, k4 = jax.random.split(key, 4)
        n, in_dim, out_dim = (8192, 128, 128)
        h = jax.random.normal(k1, (n, in_dim), dtype=jnp.float32)
        adj = jax.random.uniform(k2, (n, n), dtype=jnp.float32)
        W_self = jax.random.normal(k3, (in_dim, out_dim), dtype=jnp.float32) * (1.0 / np.sqrt(in_dim))
        W_neigh = jax.random.normal(k4, (in_dim, out_dim), dtype=jnp.float32) * (1.0 / np.sqrt(in_dim))
        return {'h': h, 'adj': adj, 'W_self': W_self, 'W_neigh': W_neigh}
    _L1_gnn_all = _L1_gnn_setup()
    _L1_gnn_in = {k: v for k, v in _L1_gnn_all.items() if k in ('W_self', 'W_neigh')}
    del _L1_gnn_all

    def _L2_gnn_setup():
        import jax, jax.numpy as jnp
        import numpy as np
        N, DIM = (8192, 128)

        def _gru_cell(x, h, W_ih, W_hh, b_ih, b_hh):
            gi = x @ W_ih.T + b_ih
            gh = h @ W_hh.T + b_hh
            i_r, i_z, i_n = jnp.split(gi, 3, axis=-1)
            h_r, h_z, h_n = jnp.split(gh, 3, axis=-1)
            r = jax.nn.sigmoid(i_r + h_r)
            z = jax.nn.sigmoid(i_z + h_z)
            n = jnp.tanh(i_n + r * h_n)
            return (1.0 - z) * n + z * h
        key = jax.random.key(seed)
        ks = jax.random.split(key, 8)
        states = jax.random.normal(ks[0], (N, DIM), dtype=jnp.float32)
        adj = jax.random.uniform(ks[1], (N, N), dtype=jnp.float32)
        s = 1.0 / np.sqrt(DIM)
        W_msg = jax.random.uniform(ks[2], (DIM, DIM), minval=-s, maxval=s, dtype=jnp.float32)
        b_msg = jax.random.uniform(ks[3], (DIM,), minval=-s, maxval=s, dtype=jnp.float32)
        W_ih = jax.random.uniform(ks[4], (3 * DIM, DIM), minval=-s, maxval=s, dtype=jnp.float32)
        W_hh = jax.random.uniform(ks[5], (3 * DIM, DIM), minval=-s, maxval=s, dtype=jnp.float32)
        b_ih = jax.random.uniform(ks[6], (3 * DIM,), minval=-s, maxval=s, dtype=jnp.float32)
        b_hh = jax.random.uniform(ks[7], (3 * DIM,), minval=-s, maxval=s, dtype=jnp.float32)
        return {'states': states, 'adj': adj, 'W_msg': W_msg, 'b_msg': b_msg, 'W_ih': W_ih, 'W_hh': W_hh, 'b_ih': b_ih, 'b_hh': b_hh}
    _L2_gnn_all = _L2_gnn_setup()
    _L2_gnn_in = {k: v for k, v in _L2_gnn_all.items() if k in ('W_msg', 'b_msg', 'W_ih', 'W_hh', 'b_ih', 'b_hh')}
    del _L2_gnn_all

    def _L3_gnn_setup():
        import jax, jax.numpy as jnp
        import numpy as np
        EPS = 1e-07
        MAX_TANH = 1.0 - 1e-06

        def _norm(v):
            return jnp.maximum(jnp.linalg.norm(v, axis=-1, keepdims=True), EPS)

        def log_map_zero(y):
            n = _norm(y)
            return jnp.arctanh(jnp.clip(n, 0.0, MAX_TANH)) * y / n

        def exp_map_zero(v):
            n = _norm(v)
            return jnp.tanh(n) * v / n

        def h_add(x, y):
            xy = jnp.sum(x * y, axis=-1, keepdims=True)
            x2 = jnp.sum(x * x, axis=-1, keepdims=True)
            y2 = jnp.sum(y * y, axis=-1, keepdims=True)
            num = (1.0 + 2.0 * xy + y2) * x + (1.0 - x2) * y
            den = 1.0 + 2.0 * xy + x2 * y2
            return num / jnp.maximum(den, EPS)

        def h_mul(x, W):
            return exp_map_zero(log_map_zero(x) @ W)
        key = jax.random.key(seed)
        k1, k2, k3, k4 = jax.random.split(key, 4)
        N, F_IN, F_OUT = (4096, 128, 128)
        x = 0.05 * jax.random.normal(k1, (N, F_IN), dtype=jnp.float32)
        a = (jax.random.uniform(k2, (N, N)) < 0.01).astype(jnp.float32)
        adj = a / jnp.maximum(a.sum(axis=1, keepdims=True), 1.0)
        lim_e = np.sqrt(6.0 / (F_IN + F_IN)) * np.sqrt(2.0)
        lim_l = np.sqrt(6.0 / (2 * F_IN + F_OUT)) * np.sqrt(2.0)
        embed = jax.random.uniform(k3, (F_IN, F_IN), minval=-lim_e, maxval=lim_e, dtype=jnp.float32)
        layer = jax.random.uniform(k4, (2 * F_IN, F_OUT), minval=-lim_l, maxval=lim_l, dtype=jnp.float32)
        embed_bias = jnp.zeros((F_IN,), dtype=jnp.float32)
        layer_bias = jnp.zeros((F_OUT,), dtype=jnp.float32)
        return {'x': x, 'adj': adj, 'embed': embed, 'layer': layer, 'embed_bias': embed_bias, 'layer_bias': layer_bias}
    _L3_gnn_all = _L3_gnn_setup()
    _L3_gnn_in = {k: v for k, v in _L3_gnn_all.items() if k in ('embed', 'layer', 'embed_bias', 'layer_bias')}
    del _L3_gnn_all
    return {'x': x, 'adj': adj, 'L0_gnn_W': _L0_gnn_in['W'], 'L0_gnn_a': _L0_gnn_in['a'], 'L1_gnn_W_self': _L1_gnn_in['W_self'], 'L1_gnn_W_neigh': _L1_gnn_in['W_neigh'], 'L2_gnn_W_msg': _L2_gnn_in['W_msg'], 'L2_gnn_b_msg': _L2_gnn_in['b_msg'], 'L2_gnn_W_ih': _L2_gnn_in['W_ih'], 'L2_gnn_W_hh': _L2_gnn_in['W_hh'], 'L2_gnn_b_ih': _L2_gnn_in['b_ih'], 'L2_gnn_b_hh': _L2_gnn_in['b_hh'], 'L3_gnn_embed': _L3_gnn_in['embed'], 'L3_gnn_layer': _L3_gnn_in['layer'], 'L3_gnn_embed_bias': _L3_gnn_in['embed_bias'], 'L3_gnn_layer_bias': _L3_gnn_in['layer_bias']}

def reference(x, adj, L0_gnn_W, L0_gnn_a, L1_gnn_W_self, L1_gnn_W_neigh, L2_gnn_W_msg, L2_gnn_b_msg, L2_gnn_W_ih, L2_gnn_W_hh, L2_gnn_b_ih, L2_gnn_b_hh, L3_gnn_embed, L3_gnn_layer, L3_gnn_embed_bias, L3_gnn_layer_bias):
    import jax
    import jax.numpy as jnp

    def _L0_gnn_ref(x, adj, W, a):
        import jax, jax.numpy as jnp
        import numpy as np
        N, IN_DIM, OUT_DIM, HEADS = (2048, 128, 32, 4)
        EDGE_PROB = 0.015
        n = x.shape[0]
        xp = (x @ W).reshape(n, HEADS, OUT_DIM)
        a_j, a_i = (a[:OUT_DIM], a[OUT_DIM:])
        s_j = jnp.einsum('nhd,d->nh', xp, a_j)
        s_i = jnp.einsum('nhd,d->nh', xp, a_i)
        scale = jnp.float32(1.0 / np.sqrt(OUT_DIM))
        e = (s_i[:, None, :] + s_j[None, :, :]) * scale
        e = e + ((1.0 - adj) * jnp.float32(-1000000000.0))[:, :, None]
        att = jax.nn.softmax(e, axis=1)
        out = jnp.einsum('ijh,jhd->ihd', att, xp)
        return out.reshape(n, HEADS * OUT_DIM)

    def _L1_gnn_ref(h, adj, W_self, W_neigh):
        import jax, jax.numpy as jnp
        import numpy as np
        deg = jnp.clip(jnp.sum(adj, axis=1, keepdims=True), 1.0)
        h_neigh = adj @ h / deg
        return h @ W_self + h_neigh @ W_neigh

    def _L2_gnn_ref(states, adj, W_msg, b_msg, W_ih, W_hh, b_ih, b_hh):
        import jax, jax.numpy as jnp
        import numpy as np
        N, DIM = (8192, 128)

        def _gru_cell(x, h, W_ih, W_hh, b_ih, b_hh):
            gi = x @ W_ih.T + b_ih
            gh = h @ W_hh.T + b_hh
            i_r, i_z, i_n = jnp.split(gi, 3, axis=-1)
            h_r, h_z, h_n = jnp.split(gh, 3, axis=-1)
            r = jax.nn.sigmoid(i_r + h_r)
            z = jax.nn.sigmoid(i_z + h_z)
            n = jnp.tanh(i_n + r * h_n)
            return (1.0 - z) * n + z * h
        agg = adj @ states
        msg = jax.nn.relu(agg @ W_msg.T + b_msg)
        return _gru_cell(msg, states, W_ih, W_hh, b_ih, b_hh)

    def _L3_gnn_ref(x, adj, embed, layer, embed_bias, layer_bias):
        import jax, jax.numpy as jnp
        import numpy as np
        EPS = 1e-07
        MAX_TANH = 1.0 - 1e-06

        def _norm(v):
            return jnp.maximum(jnp.linalg.norm(v, axis=-1, keepdims=True), EPS)

        def log_map_zero(y):
            n = _norm(y)
            return jnp.arctanh(jnp.clip(n, 0.0, MAX_TANH)) * y / n

        def exp_map_zero(v):
            n = _norm(v)
            return jnp.tanh(n) * v / n

        def h_add(x, y):
            xy = jnp.sum(x * y, axis=-1, keepdims=True)
            x2 = jnp.sum(x * x, axis=-1, keepdims=True)
            y2 = jnp.sum(y * y, axis=-1, keepdims=True)
            num = (1.0 + 2.0 * xy + y2) * x + (1.0 - x2) * y
            den = 1.0 + 2.0 * xy + x2 * y2
            return num / jnp.maximum(den, EPS)

        def h_mul(x, W):
            return exp_map_zero(log_map_zero(x) @ W)
        h = h_mul(x, embed)
        h = h_add(h, embed_bias[None, :])
        neigh = exp_map_zero(adj @ log_map_zero(h))
        out = h_mul(jnp.concatenate((x, neigh), axis=1), layer)
        out = h_add(out, layer_bias[None, :])
        return out
    h = jnp.maximum(_layernorm(x, axis=-1), 0.0)
    x = x + _L0_gnn_ref(h, adj, L0_gnn_W, L0_gnn_a)
    h = jnp.maximum(_layernorm(x, axis=-1), 0.0)
    x = x + _L1_gnn_ref(h, adj, L1_gnn_W_self, L1_gnn_W_neigh)
    h = jnp.maximum(_layernorm(x, axis=-1), 0.0)
    x = x + _L2_gnn_ref(h, adj, L2_gnn_W_msg, L2_gnn_b_msg, L2_gnn_W_ih, L2_gnn_W_hh, L2_gnn_b_ih, L2_gnn_b_hh)
    h = jnp.maximum(_layernorm(x, axis=-1), 0.0)
    x = x + _L3_gnn_ref(h, adj, L3_gnn_embed, L3_gnn_layer, L3_gnn_embed_bias, L3_gnn_layer_bias)
    return x

_drawn_inputs = setup_inputs


def setup_inputs(seed=0):
    import zlib

    import numpy as np

    out = dict(_drawn_inputs(seed))
    spreads = {'L3_gnn_embed_bias': (0.0, 0.8), 'L3_gnn_layer_bias': (0.0, 0.8)}
    factors = {'L0_gnn_a': 3.8,
     'L2_gnn_b_msg': 8.0,
     'L2_gnn_b_ih': 6.973,
     'L2_gnn_b_hh': 8.0,
     'L3_gnn_embed': 8.0}
    for name, (base, spread) in spreads.items():
        noise = np.random.default_rng([zlib.crc32(name.encode()), seed]).standard_normal(out[name].shape)
        drawn = base * np.exp(spread * noise) if base else spread * noise
        out[name] = jnp.asarray(drawn.astype(out[name].dtype))
    for name, factor in factors.items():
        out[name] = (out[name] * factor).astype(out[name].dtype)
    return out
```

```python
import concourse.bass as bass
from concourse import mybir
from contextlib import ExitStack


P = 128
N = 4096
D = 128
NT = N // P
TG = 4
NG = NT // TG
GW = TG * P
HEADS = 4
HD = D // HEADS
SPLIT = 1024.0
EPS_LN = 1e-5
EPS_BALL = 1e-7
MAX_TANH = 1.0 - 1e-6
SERIES_BELOW = 0.25

PIECE_T = NT // 2
PIECE = PIECE_T * P
NPIECE = 2 * NT
NBUF = 3
PIECES_STATS, PIECES_PROJ, PIECES_SPLIT, PIECES_MAIN = 1, 1, 1, 5

HI = D + HEADS + 1
LO = D + HEADS
OPW = HI + LO

C_NEIGH = 0
C_MSG = C_NEIGH + D
C_IH = C_MSG + D
C_HH = C_IH + 3 * D
C_EMB = C_HH + 3 * D
C_LAY = C_EMB + D
C_B3E = C_LAY + 2 * D
C_B3L = C_B3E + D
C_BMSG = C_B3L + D
C_BIH = C_BMSG + 1
C_BHH = C_BIH + 3
C_ALL = C_BHH + 3 + 1


def build_graph_stack(nc, x_rows, adj_pieces, proj, consts0, consts1, out_rows):
    fp32, fp16, u8, u32 = mybir.dt.float32, mybir.dt.float16, mybir.dt.uint8, mybir.dt.uint32
    fp8 = mybir.dt.float8e4
    ALU = mybir.AluOpType
    ACT = mybir.ActivationFunctionType
    AX = mybir.AxisListType
    import math
    SCALE = 1.0 / math.sqrt(HD)

    with ExitStack() as ctx:
        def sb(name, shape, dt):
            return ctx.enter_context(nc.sbuf_tensor(name, shape, dt))

        def sem(name):
            return ctx.enter_context(nc.semaphore(name))

        adj = sb("adj", [P, NT, NT, P], u8)
        x = sb("x", [P, NT, D], fp32)
        hs_a = sb("hs_a", [P, NT, 2, D], fp16)
        region_op = sb("region_op", [P, NT * OPW], fp16)
        region_st = sb("region_st", [P, NBUF * PIECE], fp32)
        c0 = sb("c0", [P, 2 * D], fp32)
        rowbuf = sb("rowbuf", [P, TG * HI], fp32)
        hT = sb("hT", [P, GW], fp32)
        w = sb("w", [P, NT, HEADS], fp32)
        nnz = sb("nnz", [P, NPIECE], fp32)
        deg = sb("deg", [P, NT], fp32)
        mv = sb("mv", [P, TG, 2], fp32)
        mean = sb("mean", [P, NT], fp32)
        rs = sb("rs", [P, NT], fp32)
        small = sb("small", [P, 80], fp32)

        ident, wself = c0[:, 0:D], c0[:, D:2 * D]
        xp = hs_a[:].rearrange("p t a d -> p (t a d)").bitcast(fp32).rearrange("p (t d) -> p t d", d=D)
        op0 = region_op[:].rearrange("p (t c) -> p t c", c=OPW)
        hs_b = region_op[:, 0:NT * 2 * D].rearrange("p (t a d) -> p t a d", a=2, d=D)
        early = region_op[:, 0:NT * OPW].bitcast(fp32)
        pw = early[:, 0:2 * D + HEADS]
        pwa = early[:, 2 * D + HEADS:3 * D + 2 * HEADS]
        E0 = 3 * D + 2 * HEADS
        xn_early = early[:, E0:E0 + 2 * GW].rearrange("p (b t d) -> p b t d", b=2, t=TG)
        hT_early = early[:, E0 + 2 * GW:E0 + 4 * GW].rearrange("p (b n) -> p b n", b=2)
        stage = region_st[:].rearrange("p (b n) -> p b n", b=NBUF)
        numden = rowbuf[:].rearrange("p (t c) -> p t c", c=HI)
        xn = rowbuf[:, 0:GW].rearrange("p (t d) -> p t d", d=D)
        c1 = region_st[:, 0:C_ALL]

        def work(i):
            return region_st[:, C_ALL + i * GW:C_ALL + (i + 1) * GW]

        aT, msgT, rT, zT, tT, uT, row_a, row_b = [work(i) for i in range(8)]
        scr = region_st[:, C_ALL + 8 * GW:C_ALL + 8 * GW + 4 * 64]

        def col4(i):
            return scr[:, 4 * i:4 * i + 4]

        def tiles(v):
            return v.rearrange("p (t d) -> p t d", d=D)

        (NRM, CL, A1, B1, Q, LNQ, PP, SER, MASK, AT, KAP, SSH, SSE, DOT, NE_H, NE_E, NE_Z, N2, TH, ALF, XY, X2, TT,
         NUM, DEN, CA, CB, SSZ, SSA, BETA, SSC, COEF) = range(32)
        y2e, y2l, brz = scr[:, 130:131], scr[:, 131:132], scr[:, 132:134]
        STEPS_2, STEPS_3 = 87, 55

        ve = small[:, 0:4]
        mhalf, phalf = small[:, 4:8], small[:, 8:12]
        ext, extall = small[:, 12:20], small[:, 20:28]
        shift = small[:, 28:32]
        rden = small[:, 32:48]
        ones_col = small[:, 48:49]
        st = small[:, 52:76].rearrange("p (t s) -> p t s", s=6)

        agg = ctx.enter_context(nc.psum_tensor("agg", [P, 2, GW], fp32))
        bank = [agg[:, 0, :], agg[:, 1, :]] + [ctx.enter_context(nc.psum_tensor(f"bank{i}", [P, GW], fp32))[:] for i in range(2, 8)]

        S = {n: sem(n) for n in (
            "x_in", "proj_in", "c0_in", "c1_in", "landed", "conv_done", "nnz_done",
            "consts_set", "dve_step", "act_step", "pool_step",
            "ve_ready", "rs_ready", "st_free", "wa_full", "wa_done", "xn0_ready", "tr0_full", "hT0_ready", "xp_full", "xp_read",
            "ext_ready", "extall_ready", "shift_ready", "w_ready", "whi_ready", "wlo_ready", "y_ready", "hi0_ready", "op0_ready",
            "acc_full", "acc_read", "x_ready",
            "xnew_ready", "hi_ready", "hs_ready",
            "pre_xn", "pre_tr", "pre_hT",
            "agg_full", "aT_ready", "l1_self", "l1_neigh",
            "msg_full", "msg_ready", "gates_full", "rz_ready", "t_ready", "n_ready", "u_ready", "uT_full",
            "x3_tr", "h3T_ready", "emb_full", "l1_x", "l2_x",
            "ss_ready", "nrm_ready", "hrow_ready", "ln_in", "ln_out", "th_in", "th_out", "z_ready", "zs_ready",
            "coef_ready", "sq_ready", "norms_full", "p1_full", "p2_full", "p1_read", "v_ready", "x4_ready", "out_done")}
        landing = [sem(f"landing{b}") for b in range(NBUF)]

        block = ctx.enter_context(nc.Block())

        def tile_of(g, t):
            return bass.ds(g * TG + t, 1)

        def group_of(g):
            return bass.ds(g * TG, TG)

        class Steps:

            def __init__(self, eng, s):
                self.eng, self.s, self.base, self.g, self.per, self.k = eng, s, 0, 0, 0, 0

            def loop(self, g, per):
                self.g, self.per, self.k = g, per, 0

            def end(self, trips):
                assert self.k == self.per, (self.k, self.per)
                self.base += trips * self.per
                self.g, self.per, self.k = 0, 0, 0

            def step(self, ins):
                ins.then_inc(self.s, 1)
                self.k += 1
                if not self.per:
                    self.base, self.k = self.base + 1, 0

            def settle(self):
                self.eng.wait_ge(self.s, self.base + self.g * self.per + self.k)

            def link(self, ins):
                self.step(ins)
                self.settle()

        @block.sync
        def _(sp):
            sp.dma_start(x[:], x_rows).then_inc(S["x_in"], 16)
            sp.dma_start(pw, proj).then_inc(S["proj_in"], 16)
            sp.dma_start(c0[:], consts0).then_inc(S["c0_in"], 16)
            for n in range(NBUF):
                sp.dma_start(stage[:, n, :], adj_pieces[n]).then_inc(landing[n], 16)
            sp.wait_ge(landing[0], 16)
            sp.sem_inc(S["landed"], 1)

            def relay_and_refill(r, n_of, b):
                nxt = (b + 1) % NBUF
                sp.wait_ge(landing[nxt], 16 * r + (32 if nxt == 0 else 16))
                sp.sem_inc(S["landed"], 1)
                sp.wait_ge(S["conv_done"], n_of + 1)
                sp.wait_ge(S["nnz_done"], n_of + 1)
                sp.dma_start(stage[:, b, :], adj_pieces[bass.ds(n_of + NBUF, 1)].rearrange("a p n -> p (a n)")
                             if not isinstance(n_of, int) else adj_pieces[n_of + NBUF]).then_inc(landing[b], 16)

            rounds = (NPIECE - NBUF) // NBUF
            with sp.Fori(0, rounds) as r:
                for b in range(NBUF):
                    relay_and_refill(r, r * NBUF + b, b)
            for n in range(rounds * NBUF, NPIECE - NBUF):
                relay_and_refill(n // NBUF, n, n % NBUF)
            for n in range(NPIECE - NBUF + 1, NPIECE):
                sp.wait_ge(landing[n % NBUF], 16 * (n // NBUF + 1))
                sp.sem_inc(S["landed"], 1)
            sp.wait_ge(S["conv_done"], NPIECE)
            sp.wait_ge(S["nnz_done"], NPIECE)
            sp.dma_start(c1, consts1).then_inc(S["c1_in"], 16)
            with sp.Fori(0, NG) as g:
                sp.wait_ge(S["x4_ready"], g + 1)
                sp.dma_start(out_rows[:, group_of(g), :], x[:, group_of(g), :]).then_inc(S["out_done"], 16)
            sp.wait_ge(S["out_done"], 16 * NG)

        @block.vector
        def _(dve):
            v = nc.vector
            me = Steps(dve, S["dve_step"])

            def copy(dst, src):
                return v.tensor_scalar(dst, src, 1.0, None, ALU.mult)

            def convert(n):
                dve.wait_ge(S["landed"], n + 1)
                adj_flat = adj[:].rearrange("p i j n -> p (i j n)")
                src = region_st[:, bass.ds((n % NBUF) * PIECE, PIECE)]
                v.tensor_scalar(adj_flat[:, bass.ds(n * PIECE, PIECE)], src, 1.0, 56.0,
                                ALU.is_equal, ALU.mult).then_inc(S["conv_done"], 1)

            def anchor():
                v.memset(small[:, 50:51], 0.0)

            def statistics(g):
                anchor()
                for t in range(TG):
                    me.step(v.bn_stats(st[:, t, :], x[:, tile_of(g, t), :].rearrange("p a d -> p (a d)")))
                me.settle()
                anchor()
                for t in range(TG):
                    me.step(v.bn_aggr(mv[:, t, :], st[:, t, :]))
                me.settle()
                me.step(copy(mean[:, group_of(g)].rearrange("p (t a) -> p t a", a=1), mv[:, :, 0:1]))
                v.tensor_scalar(ve.rearrange("p (t a) -> p t a", a=1), mv[:, :, 1:2], EPS_LN,
                                1.0 / SPLIT ** 2, ALU.add, ALU.mult).then_inc(S["ve_ready"], 1)

            def normalised(g, dst):
                for t in range(TG):
                    last = v.tensor_scalar(dst(t), x[:, tile_of(g, t), :].rearrange("p a d -> p (a d)"),
                                           mean[:, tile_of(g, t)],
                                           rs[:, tile_of(g, t)], ALU.subtract, ALU.mult)
                    if t < TG - 1:
                        me.step(last)
                return last

            v.memset(mhalf, -0.5)
            v.memset(ones_col, 1.0)
            me.link(v.memset(phalf, 0.5))
            v.memset(small[:, 49:50], 0.0).then_inc(S["consts_set"], 1)
            dve.wait_ge(S["proj_in"], 16)
            me.step(copy(pwa[:, 0:D], pw[:, 0:D]))
            dve.wait_ge(S["wa_full"], 1)
            copy(pwa[:, D:D + HEADS], bank[4][:, 0:HEADS]).then_inc(S["wa_done"], 1)
            dve.wait_ge(S["x_in"], 16)

            with dve.Fori(0, NG) as g:
                me.loop(g, 2 * TG + 1)
                statistics(g)
                convert(g)
                dve.wait_ge(S["rs_ready"], g + 1)
            me.end(NG)

            def early_rows(g):
                normalised(g, lambda t: xn_early[:, bass.ds(g % 2, 1), t, :].rearrange("p a d -> p (a d)")
                           if not isinstance(g, int) else xn_early[:, g % 2, t, :]).then_inc(S["xn0_ready"], 1)

            def projections(g):
                dve.wait_ge(S["xp_full"], g + 1)
                for half in range(2):
                    b = bank[5 + half][:, 0:2 * (D + HEADS)].rearrange("p (t c) -> p t c", c=D + HEADS)
                    me.step(copy(xp[:, bass.ds(g * TG + 2 * half, 2), :], b[:, :, 0:D]))
                    last = copy(w[:, bass.ds(g * TG + 2 * half, 2), :], b[:, :, D:D + HEADS])
                    if half == 0:
                        me.step(last)
                last.then_inc(S["xp_read"], 1)

            per_rows = TG - 1
            me.loop(0, per_rows)
            early_rows(0)
            me.end(1)
            with dve.Fori(1, NG) as g:
                me.loop(g - 1, per_rows + 3)
                early_rows(g)
                convert(g + NG * PIECES_STATS - 1)
                projections(g - 1)
            me.end(NG - 1)
            convert(NG * (PIECES_STATS + PIECES_PROJ) - 1)
            me.loop(0, 3)
            projections(NG - 1)
            me.end(1)
            dve.wait_ge(S["xp_read"], NG)
            me.step(v.tensor_reduce(ext[:, 0:4], w[:].rearrange("p t h -> p h t"), AX.X, ALU.max))
            me.link(v.tensor_reduce(ext[:, 4:8], w[:].rearrange("p t h -> p h t"), AX.X, ALU.min))
            v.tensor_scalar(ext[:, 4:8], ext[:, 4:8], -1.0, None, ALU.mult).then_inc(S["ext_ready"], 1)
            dve.wait_ge(S["extall_ready"], 1)
            v.tensor_scalar(shift, extall[:, 0:4], -SCALE, math.log(SPLIT), ALU.mult, ALU.add).then_inc(S["shift_ready"], 1)

            n0 = NG * (PIECES_STATS + PIECES_PROJ)
            dve.wait_ge(S["w_ready"], HEADS)
            me.step(v.memset(op0[:, :, D + HEADS:HI], 1.0))
            dve.wait_ge(S["whi_ready"], 1)
            v.tensor_tensor(op0[:, :, HI + D:OPW], w[:], op0[:, :, D:D + HEADS], ALU.subtract).then_inc(S["wlo_ready"], 1)
            with dve.Fori(0, NG) as g:
                y = xp[:, group_of(g), :]
                yh = y.rearrange("p t (h d) -> p (t h) d", d=HD)
                wb = w[:, group_of(g), :].rearrange("p t h -> p (t h)")
                wb = wb.rearrange("p (c a) -> p c a", a=1).to_broadcast([P, TG * HEADS, HD])
                v.tensor_tensor(yh, yh, wb, ALU.mult).then_inc(S["y_ready"], 1)
                convert(g + n0)
                dve.wait_ge(S["y_ready"], g + 1)
                dve.wait_ge(S["hi0_ready"], g + 1)
                v.tensor_tensor(op0[:, group_of(g), HI:HI + D], y, op0[:, group_of(g), 0:D],
                                ALU.subtract).then_inc(S["op0_ready"], 1)

            n1 = n0 + NG * PIECES_SPLIT

            def take(g, t):
                dve.wait_ge(S["acc_full"], g * TG + t + 1)
                b = bank[t]
                me.link(copy(numden[:, t, :], b[:, 0:HI]))
                v.tensor_tensor(numden[:, t, 0:LO], numden[:, t, 0:LO], b[:, HI:OPW], ALU.add).then_inc(S["acc_read"], 1)

            def operand(g, count, xnew, hs):
                dve.wait_ge(S["rs_ready"], g + NG + count + 1)
                normalised(g, lambda t: xnew[:, t, :]).then_inc(S["xnew_ready"], 1)
                dve.wait_ge(S["hi_ready"], g + count + 1)
                dve.wait_ge(S["xnew_ready"], g + count + 1)
                v.scalar_tensor_tensor(hs[:, group_of(g), 1, :], xnew, 0.0, hs[:, group_of(g), 0, :],
                                       ALU.max, ALU.subtract).then_inc(S["hs_ready"], 1)
                dve.wait_ge(S["hs_ready"], g + count + 1)

            with dve.Fori(0, NG) as g:
                me.loop(g, TG + 4 + 2 * TG + 1 + TG - 1)
                n = g * PIECES_MAIN + n1
                convert(n)
                convert(n + 1)
                take(g, 0)
                take(g, 1)
                convert(n + 2)
                take(g, 2)
                convert(n + 3)
                convert(n + 4)
                take(g, 3)
                dve.wait_ge(S["acc_read"], g * TG + TG)
                me.step(copy(deg[:, group_of(g)].rearrange("p (t a) -> p t a", a=1), numden[:, :, D + HEADS:HI]))
                me.link(v.reciprocal(rden.rearrange("p (t h) -> p t h", h=HEADS), numden[:, :, D:D + HEADS]))
                num = numden[:, :, 0:D].rearrange("p t (h d) -> p t h d", d=HD)
                rb = rden.rearrange("p (t h a) -> p t h a", h=HEADS, a=1).to_broadcast([P, TG, HEADS, HD])
                me.link(v.tensor_tensor(num, num, rb, ALU.mult))
                me.link(v.tensor_tensor(x[:, group_of(g), :], x[:, group_of(g), :], numden[:, :, 0:D], ALU.add))
                statistics(g)
                operand(g, 0, xn, hs_a)
            me.end(NG)

            me.link(v.tensor_scalar(deg[:], deg[:], 1.0, None, ALU.max))
            me.link(v.reciprocal(deg[:], deg[:]))

            def pre_rows(g):
                normalised(g, lambda t: xn[:, t, :]).then_inc(S["pre_xn"], 1)

            dve.wait_ge(S["c1_in"], 16)
            with dve.Fori(0, NG) as g:
                me.loop(g, (TG - 1) + TG + 1 + 2 * TG + 1 + (TG - 1))
                pre_rows(g)
                dve.wait_ge(S["l1_self"], g + 1)
                dve.wait_ge(S["l1_neigh"], g + 1)
                for t in range(TG):
                    xt = x[:, tile_of(g, t), :].rearrange("p a d -> p (a d)")
                    me.step(v.scalar_tensor_tensor(xt, bank[3][:, t * D:(t + 1) * D], deg[:, tile_of(g, t)], xt,
                                                   ALU.mult, ALU.add))
                me.settle()
                me.link(v.tensor_tensor(x[:, group_of(g), :], x[:, group_of(g), :], tiles(bank[4]), ALU.add))
                statistics(g)
                operand(g, NG, tiles(row_a), hs_b)
            me.end(NG)

            C = col4

            def artanh_over(nrm, dst, ln_count):
                me.link(v.tensor_scalar(C(CL), nrm, MAX_TANH, None, ALU.min))
                me.step(v.tensor_scalar(C(A1), C(CL), 1.0, None, ALU.add))
                me.step(v.tensor_scalar(C(B1), C(CL), -1.0, 1.0, ALU.mult, ALU.add))
                me.link(v.tensor_tensor(C(PP), C(CL), C(CL), ALU.mult))
                me.link(v.reciprocal(C(B1), C(B1)))
                v.tensor_tensor(C(Q), C(A1), C(B1), ALU.mult).then_inc(S["ln_in"], 1)
                me.link(v.tensor_scalar(C(SER), C(PP), 1.0 / 11, None, ALU.mult))
                for k in (9, 7, 5, 3):
                    me.link(v.scalar_tensor_tensor(C(SER), C(SER), 1.0 / k, C(PP), ALU.add, ALU.mult))
                me.step(v.scalar_tensor_tensor(C(SER), C(SER), 1.0, C(CL), ALU.add, ALU.mult))
                me.step(v.tensor_scalar(C(MASK), C(CL), SERIES_BELOW, None, ALU.is_lt))
                me.step(v.reciprocal(C(KAP), nrm))
                dve.wait_ge(S["ln_out"], ln_count)
                me.link(v.tensor_scalar(C(AT), C(LNQ), 0.5, None, ALU.mult))
                me.link(v.tensor_tensor(C(SER), C(SER), C(AT), ALU.subtract))
                me.link(v.tensor_tensor(C(SER), C(SER), C(MASK), ALU.mult))
                me.link(v.tensor_tensor(C(AT), C(AT), C(SER), ALU.add))
                me.link(v.tensor_tensor(dst, C(AT), C(KAP), ALU.mult))

            def exp_and_add(e_tiles, dst_tiles, kappa, nrm_count, th_count, bias, y2, done):
                for t in range(TG):
                    me.step(v.tensor_tensor_reduce(out=row_b[:, t * D:(t + 1) * D], in0=e_tiles(t), in1=bias, scale=1.0,
                                                   scalar=0.0, op0=ALU.mult, op1=ALU.add, accum_out=C(DOT)[:, t:t + 1]))
                dve.wait_ge(S["nrm_ready"], nrm_count)
                me.settle()
                me.link(v.tensor_tensor(C(N2), C(NE_E), kappa, ALU.mult))
                v.tensor_scalar(C(N2), C(N2), EPS_BALL, None, ALU.max).then_inc(S["th_in"], 1)
                dve.wait_ge(S["th_in"], th_count)
                me.link(v.reciprocal(C(ALF), C(N2)))
                me.link(v.tensor_tensor(C(ALF), C(ALF), kappa, ALU.mult))
                dve.wait_ge(S["th_out"], th_count)
                me.link(v.tensor_tensor(C(ALF), C(ALF), C(TH), ALU.mult))
                me.step(v.tensor_tensor(C(XY), C(ALF), C(DOT), ALU.mult))
                me.link(v.tensor_tensor(C(X2), C(ALF), C(ALF), ALU.mult))
                me.step(v.tensor_scalar(C(TT), C(XY), 2.0, 1.0, ALU.mult, ALU.add))
                me.link(v.tensor_tensor(C(X2), C(X2), C(SSE), ALU.mult))
                me.step(v.scalar_tensor_tensor(C(NUM), C(TT), y2, C(ALF), ALU.add, ALU.mult))
                me.step(v.scalar_tensor_tensor(C(DEN), C(X2), y2, C(TT), ALU.mult, ALU.add))
                me.link(v.tensor_scalar(C(CB), C(X2), -1.0, 1.0, ALU.mult, ALU.add))
                me.link(v.tensor_scalar(C(DEN), C(DEN), EPS_BALL, None, ALU.max))
                me.link(v.reciprocal(C(DEN), C(DEN)))
                me.step(v.tensor_tensor(C(CA), C(NUM), C(DEN), ALU.mult))
                me.link(v.tensor_tensor(C(CB), C(CB), C(DEN), ALU.mult))
                for t in range(TG):
                    me.step(v.tensor_scalar(row_b[:, t * D:(t + 1) * D], bias, C(CB)[:, t:t + 1], None, ALU.mult))
                me.settle()
                for t in range(TG):
                    last = v.scalar_tensor_tensor(dst_tiles(t), e_tiles(t), C(CA)[:, t:t + 1], row_b[:, t * D:(t + 1) * D],
                                                  ALU.mult, ALU.add)
                    if t < TG - 1:
                        me.step(last)
                last.then_inc(done, 1)

            b3e, b3l = c1[:, C_B3E:C_B3E + D], c1[:, C_B3L:C_B3L + D]
            for b, y2 in ((b3e, y2e), (b3l, y2l)):
                me.link(v.tensor_tensor_reduce(out=row_b[:, 0:D], in0=b, in1=b, scale=1.0, scalar=0.0, op0=ALU.mult,
                                               op1=ALU.add, accum_out=y2))
            v.tensor_tensor(brz, c1[:, C_BIH:C_BIH + 2], c1[:, C_BHH:C_BHH + 2], ALU.add).then_inc(S["consts_set"], 1)

            with dve.Fori(0, NG) as g:
                me.loop(g, STEPS_2)
                pre_rows(g)
                dve.wait_ge(S["gates_full"], g + 1)
                dve.wait_ge(S["rz_ready"], g + 1)
                me.link(v.scalar_tensor_tensor(tT, bank[7], c1[:, C_BHH + 2:C_BHH + 3], rT, ALU.add, ALU.mult))
                v.tensor_tensor(tT, tT, bank[6], ALU.add).then_inc(S["t_ready"], 1)
                dve.wait_ge(S["n_ready"], g + 1)
                me.link(v.tensor_tensor(uT, hT[:], tT, ALU.subtract))
                me.link(v.tensor_tensor(uT, uT, zT, ALU.mult))
                v.tensor_tensor(uT, uT, tT, ALU.add).then_inc(S["u_ready"], 1)
                dve.wait_ge(S["uT_full"], g + 1)
                me.link(v.tensor_tensor(x[:, group_of(g), :], x[:, group_of(g), :], tiles(bank[2]), ALU.add))
                statistics(g)
                dve.wait_ge(S["rs_ready"], g + 3 * NG + 1)
                normalised(g, lambda t: tiles(row_a)[:, t, :]).then_inc(S["xnew_ready"], 1)
                dve.wait_ge(S["hrow_ready"], g + 1)
                for t in range(TG):
                    r = row_b[:, t * D:(t + 1) * D]
                    me.step(v.tensor_tensor_reduce(out=zT[:, t * D:(t + 1) * D], in0=r, in1=r, scale=1.0, scalar=0.0,
                                                   op0=ALU.mult, op1=ALU.add, accum_out=C(SSH)[:, t:t + 1]))
                me.settle()
                copy(w[:, group_of(g), 0:1], C(SSH).rearrange("p (t a) -> p t a", a=1)).then_inc(S["ss_ready"], 1)
                dve.wait_ge(S["nrm_ready"], g * 3 + 1)
                me.link(v.tensor_scalar(C(NRM), C(NE_H), EPS_BALL, None, ALU.max))
                artanh_over(C(NRM), C(SSC), g * 2 + 1)
                dve.wait_ge(S["emb_full"], g + 1)
                exp_and_add(lambda t: bank[3][:, t * D:(t + 1) * D], lambda t: row_a[:, t * D:(t + 1) * D],
                            C(SSC), g * 3 + 2, g + 1, b3e, y2e, S["z_ready"])
                dve.wait_ge(S["nrm_ready"], g * 3 + 3)
                me.link(v.tensor_scalar(C(NRM), C(NE_Z), EPS_BALL, None, ALU.max))
                artanh_over(C(NRM), C(BETA), g * 2 + 2)
                v.tensor_scalar(C(COEF), C(BETA), SPLIT, None, ALU.mult).then_inc(S["coef_ready"], 1)
                dve.wait_ge(S["hi_ready"], g + 2 * NG + 1)
                v.tensor_tensor(hs_a[:, group_of(g), 1, :], tiles(row_a), hs_a[:, group_of(g), 0, :],
                                ALU.subtract).then_inc(S["hs_ready"], 1)
                dve.wait_ge(S["hs_ready"], g + 2 * NG + 1)
            me.end(NG)

            with dve.Fori(0, NG) as g:
                me.loop(g, STEPS_3)
                pre_rows(g)
                dve.wait_ge(S["norms_full"], g + 1)
                copy(C(SSA), bank[5][:, 0:TG]).then_inc(S["ss_ready"], 1)
                dve.wait_ge(S["nrm_ready"], g * 3 + 3 * NG + 1)
                v.tensor_scalar(C(N2), C(NE_H), EPS_BALL, None, ALU.max).then_inc(S["th_in"], 1)
                dve.wait_ge(S["th_in"], g * 2 + NG + 1)
                me.step(v.reciprocal(C(BETA), C(N2)))
                dve.wait_ge(S["th_out"], g * 2 + NG + 1)
                me.settle()
                me.link(v.tensor_tensor(C(BETA), C(BETA), C(TH), ALU.mult))
                me.link(v.tensor_tensor(C(SSC), C(BETA), C(BETA), ALU.mult))
                me.link(v.tensor_tensor(C(SSC), C(SSC), C(SSA), ALU.mult))
                v.tensor_tensor(C(SSC).rearrange("p (t a) -> p t a", a=1), C(SSC).rearrange("p (t a) -> p t a", a=1),
                                w[:, group_of(g), 0:1], ALU.add).then_inc(S["ss_ready"], 1)
                dve.wait_ge(S["p1_read"], g + 1)
                dve.wait_ge(S["p2_full"], g + 1)
                for t in range(TG):
                    r = row_a[:, t * D:(t + 1) * D]
                    last = v.scalar_tensor_tensor(r, bank[3][:, t * D:(t + 1) * D], C(BETA)[:, t:t + 1], r,
                                                  ALU.mult, ALU.add)
                    if t < TG - 1:
                        me.step(last)
                last.then_inc(S["v_ready"], 1)
                dve.wait_ge(S["nrm_ready"], g * 3 + 3 * NG + 2)
                me.link(v.tensor_scalar(C(NRM), C(NE_Z), EPS_BALL, None, ALU.max))
                artanh_over(C(NRM), C(SSC), g + 2 * NG + 1)
                dve.wait_ge(S["v_ready"], g + 1)
                exp_and_add(lambda t: row_a[:, t * D:(t + 1) * D], lambda t: zT[:, t * D:(t + 1) * D],
                            C(SSC), g * 3 + 3 * NG + 3, g * 2 + NG + 2, b3l, y2l, S["z_ready"])
                dve.wait_ge(S["z_ready"], g + NG + 1)
                v.tensor_tensor(x[:, group_of(g), :], x[:, group_of(g), :], tiles(zT), ALU.add).then_inc(S["x4_ready"], 1)
            me.end(NG)

        @block.gpsimd
        def _(pool):
            q = nc.gpsimd

            def power(dst, src, half):
                return q.tensor_tensor(dst, src, half, ALU.pow)

            pool.wait_ge(S["consts_set"], 1)

            def inverse_deviation(g, count):
                pool.wait_ge(S["ve_ready"], g + count + 1)
                power(rs[:, group_of(g)], ve, mhalf).then_inc(S["rs_ready"], 1)

            with pool.Fori(0, NG) as g:
                inverse_deviation(g, 0)
            pool.wait_ge(S["ext_ready"], 1)
            q.partition_all_reduce(extall, ext, P, bass.bass_isa.ReduceOp.max).then_inc(S["extall_ready"], 1)
            with pool.Fori(0, NG) as g:
                inverse_deviation(g, NG)
            with pool.Fori(0, NG) as g:
                inverse_deviation(g, 2 * NG)
            with pool.Fori(0, NG) as g:
                inverse_deviation(g, 3 * NG)
                pool.wait_ge(S["ss_ready"], g + 1)
                power(col4(NE_H), col4(SSH), phalf).then_inc(S["nrm_ready"], 1)
                pool.wait_ge(S["sq_ready"], g * 2 + 1)
                power(col4(NE_E), col4(SSE), phalf).then_inc(S["nrm_ready"], 1)
                pool.wait_ge(S["sq_ready"], g * 2 + 2)
                power(col4(NE_Z), col4(SSZ), phalf).then_inc(S["nrm_ready"], 1)
            with pool.Fori(0, NG) as g:
                pool.wait_ge(S["ss_ready"], g * 2 + NG + 1)
                power(col4(NE_H), col4(SSA), phalf).then_inc(S["nrm_ready"], 1)
                pool.wait_ge(S["ss_ready"], g * 2 + NG + 2)
                power(col4(NE_Z), col4(SSC), phalf).then_inc(S["nrm_ready"], 1)
                pool.wait_ge(S["sq_ready"], g + 2 * NG + 1)
                power(col4(NE_E), col4(SSE), phalf).then_inc(S["nrm_ready"], 1)

        @block.scalar
        def _(act):
            a = nc.scalar

            def count(n):
                act.wait_ge(S["conv_done"], n + 1)
                buf = region_st[:, bass.ds((n % NBUF) * PIECE, PIECE)]
                a.activation(buf, buf.bitcast(u32), ACT.Sign, accum_out=nnz[:, bass.ds(n, 1)]).then_inc(S["nnz_done"], 1)

            with act.Fori(0, NG) as g:
                count(g)
            with act.Fori(0, NG) as g:
                count(g + NG)
                act.wait_ge(S["tr0_full"], g + 1)
                a.activation(hT_early[:, bass.ds(g % 2, 1), :].rearrange("p a n -> p (a n)"), bank[4], ACT.Relu,
                             scale=1.0 / SPLIT).then_inc(S["hT0_ready"], 1)
            act.wait_ge(S["shift_ready"], 1)
            for h in range(HEADS):
                wh = w[:, :, h:h + 1].rearrange("p t a -> p (t a)")
                a.activation(wh, wh, ACT.Exp, bias=shift[:, h:h + 1], scale=SCALE).then_inc(S["w_ready"], 1)
            act.wait_ge(S["w_ready"], HEADS)
            a.copy(op0[:, :, D:D + HEADS], w[:]).then_inc(S["whi_ready"], 1)
            n0 = NG * (PIECES_STATS + PIECES_PROJ)
            with act.Fori(0, NG) as g:
                act.wait_ge(S["y_ready"], g + 1)
                a.copy(op0[:, group_of(g), 0:D], xp[:, group_of(g), :]).then_inc(S["hi0_ready"], 1)
                count(g + n0)

            def high_part(g, cnt, src, hs, func):
                act.wait_ge(S["xnew_ready"], g + cnt + 1)
                a.activation(hs[:, group_of(g), 0, :], src, func).then_inc(S["hi_ready"], 1)

            n1 = n0 + NG * PIECES_SPLIT
            with act.Fori(0, NG) as g:
                for i in range(PIECES_MAIN):
                    count(g * PIECES_MAIN + (n1 + i))
                high_part(g, 0, xn, hs_a, ACT.Relu)

            def own_rows_T(g, cnt):
                act.wait_ge(S["pre_tr"], g + cnt + 1)
                a.activation(hT[:], bank[2], ACT.Relu, scale=1.0 / SPLIT).then_inc(S["pre_hT"], 1)

            def aggregated(g, cnt, square):
                act.wait_ge(S["agg_full"], g + cnt + 1)
                src = agg[:, bass.ds(g % 2, 1), :].rearrange("p a n -> p (a n)")
                if square:
                    a.activation(msgT, src, ACT.Square, scale=1.0 / SPLIT)
                a.activation(aT, src, ACT.Copy, scale=1.0 / SPLIT).then_inc(S["aT_ready"], 1)

            def square_sums(src, sums):
                for t in range(TG):
                    last = a.activation(junk_rows[:, t * D:(t + 1) * D], src[:, t * D:(t + 1) * D], ACT.Square,
                                        accum_out=sums[:, t:t + 1])
                last.then_inc(S["sq_ready"], 1)

            with act.Fori(0, NG) as g:
                own_rows_T(g, 0)
                aggregated(g, 0, False)
                high_part(g, NG, tiles(row_a), hs_b, ACT.Relu)
            junk_rows = msgT
            act.wait_ge(S["consts_set"], 2)
            with act.Fori(0, NG) as g:
                own_rows_T(g, NG)
                aggregated(g, NG, False)
                act.wait_ge(S["msg_full"], g + 1)
                a.activation(msgT, bank[3], ACT.Relu, bias=c1[:, C_BMSG:C_BMSG + 1]).then_inc(S["msg_ready"], 1)
                act.wait_ge(S["gates_full"], g + 1)
                a.activation(rT, bank[4], ACT.Sigmoid, bias=brz[:, 0:1])
                a.activation(zT, bank[5], ACT.Sigmoid, bias=brz[:, 1:2]).then_inc(S["rz_ready"], 1)
                act.wait_ge(S["t_ready"], g + 1)
                a.activation(tT, tT, ACT.Tanh, bias=c1[:, C_BIH + 2:C_BIH + 3]).then_inc(S["n_ready"], 1)
                act.wait_ge(S["x3_tr"], g + 1)
                a.activation(hT[:], bank[2], ACT.Relu, scale=1.0 / SPLIT).then_inc(S["h3T_ready"], 1)
                act.wait_ge(S["xnew_ready"], g + 2 * NG + 1)
                a.activation(row_b, row_a, ACT.Relu, scale=1.0 / SPLIT).then_inc(S["hrow_ready"], 1)
                act.wait_ge(S["emb_full"], g + 1)
                square_sums(bank[3], col4(SSE))
                act.wait_ge(S["ln_in"], g * 2 + 1)
                a.activation(col4(LNQ), col4(Q), ACT.Ln).then_inc(S["ln_out"], 1)
                act.wait_ge(S["th_in"], g + 1)
                a.activation(col4(TH), col4(N2), ACT.Tanh).then_inc(S["th_out"], 1)
                act.wait_ge(S["z_ready"], g + 1)
                square_sums(row_a, col4(SSZ))
                act.wait_ge(S["ln_in"], g * 2 + 2)
                a.activation(col4(LNQ), col4(Q), ACT.Ln).then_inc(S["ln_out"], 1)
                act.wait_ge(S["coef_ready"], g + 1)
                act.wait_ge(S["sq_ready"], g * 2 + 2)
                for t in range(TG):
                    r = row_a[:, t * D:(t + 1) * D]
                    last = a.activation(r, r, ACT.Copy, scale=col4(COEF)[:, t:t + 1])
                last.then_inc(S["zs_ready"], 1)
                act.wait_ge(S["zs_ready"], g + 1)
                a.activation(hs_a[:, group_of(g), 0, :], tiles(row_a), ACT.Copy).then_inc(S["hi_ready"], 1)
            with act.Fori(0, NG) as g:
                own_rows_T(g, 2 * NG)
                aggregated(g, 2 * NG, True)
                act.wait_ge(S["p1_full"], g + 1)
                a.activation(row_a, bank[4], ACT.Copy).then_inc(S["p1_read"], 1)
                act.wait_ge(S["th_in"], g * 2 + NG + 1)
                a.activation(col4(TH), col4(N2), ACT.Tanh).then_inc(S["th_out"], 1)
                act.wait_ge(S["v_ready"], g + 1)
                act.wait_ge(S["norms_full"], g + 1)
                square_sums(row_a, col4(SSE))
                act.wait_ge(S["ln_in"], g + 2 * NG + 1)
                a.activation(col4(LNQ), col4(Q), ACT.Ln).then_inc(S["ln_out"], 1)
                act.wait_ge(S["th_in"], g * 2 + NG + 2)
                a.activation(col4(TH), col4(N2), ACT.Tanh).then_inc(S["th_out"], 1)

        @block.tensor
        def _(pe):
            mm = nc.tensor.matmul
            adj8 = adj[:].bitcast(fp8)

            def transposes(src, dst):
                for t in range(TG):
                    last = nc.tensor.transpose(dst[:, t * D:(t + 1) * D], src(t), ident)
                return last

            def per_tile(srcT, weights, dst):
                for t in range(TG):
                    last = mm(dst[:, t * D:(t + 1) * D], srcT[:, t * D:(t + 1) * D], weights, start=True, stop=True)
                return last

            pe.wait_ge(S["proj_in"], 16)
            mm(bank[4][:, 0:HEADS], pw[:, D:2 * D], pw[:, 2 * D:2 * D + HEADS], start=True, stop=True).then_inc(S["wa_full"], 1)
            pe.wait_ge(S["wa_done"], 1)
            pe.wait_ge(S["c0_in"], 16)
            for g in range(NG):
                pe.wait_ge(S["xn0_ready"], g + 1)
                transposes(lambda t: xn_early[:, g % 2, t, :], bank[4]).then_inc(S["tr0_full"], 1)
                pe.wait_ge(S["hT0_ready"], g + 1)
                if g:
                    pe.wait_ge(S["xp_read"], g)
                for t in range(TG):
                    half, s = t // 2, (t % 2) * (D + HEADS)
                    last = mm(bank[5 + half][:, s:s + D + HEADS], hT_early[:, g % 2, t * D:(t + 1) * D], pwa,
                              start=True, stop=True)
                last.then_inc(S["xp_full"], 1)

            pe.wait_ge(S["wlo_ready"], 1)
            for it in range(NT):
                pe.wait_ge(S["conv_done"], 2 * (it + 1))
                if it >= TG:
                    pe.wait_ge(S["acc_read"], it - TG + 1)
                for jt in range(NT):
                    if it == 0 and jt % TG == 0:
                        pe.wait_ge(S["op0_ready"], jt // TG + 1)
                    last = mm(bank[it % TG][:, 0:OPW], adj8[:, it, jt, :], op0[:, jt, :],
                              start=(jt == 0), stop=(jt == NT - 1))
                last.then_inc(S["acc_full"], 1)

            def own_transposes(s):
                pe.wait_ge(S["pre_xn"], s + 1)
                transposes(lambda t: xn[:, t, :], bank[2]).then_inc(S["pre_tr"], 1)

            def own_self(s):
                pe.wait_ge(S["pre_hT"], s + 1)
                if s == 0:
                    pe.wait_ge(S["acc_read"], NT)
                per_tile(hT, wself, bank[4]).then_inc(S["l1_self"], 1)

            def neighbours(s):
                pe.wait_ge(S["aT_ready"], s + 1)
                per_tile(aT, c1[:, C_NEIGH:C_NEIGH + D], bank[3]).then_inc(S["l1_neigh"], 1)

            def message(s):
                pe.wait_ge(S["aT_ready"], s + 1)
                mm(bank[3], c1[:, C_MSG:C_MSG + D], aT, start=True, stop=True).then_inc(S["msg_full"], 1)

            def gates(s):
                pe.wait_ge(S["pre_hT"], s + 1)
                pe.wait_ge(S["msg_ready"], s - NG + 1)
                for i, b in ((0, 4), (1, 5)):
                    mm(bank[b], c1[:, C_HH + i * D:C_HH + (i + 1) * D], hT[:], start=True, stop=False)
                    mm(bank[b], c1[:, C_IH + i * D:C_IH + (i + 1) * D], msgT, start=False, stop=True)
                mm(bank[7], c1[:, C_HH + 2 * D:C_HH + 3 * D], hT[:], start=True, stop=True)
                mm(bank[6], c1[:, C_IH + 2 * D:C_IH + 3 * D], msgT, start=True, stop=True).then_inc(S["gates_full"], 1)

            def update_back(s):
                pe.wait_ge(S["u_ready"], s - NG + 1)
                transposes(lambda t: uT[:, t * D:(t + 1) * D], bank[2]).then_inc(S["uT_full"], 1)

            def new_transposes(s):
                pe.wait_ge(S["xnew_ready"], s + NG + 1)
                transposes(lambda t: row_a[:, t * D:(t + 1) * D], bank[2]).then_inc(S["x3_tr"], 1)

            def embed(s):
                pe.wait_ge(S["h3T_ready"], s - NG + 1)
                per_tile(hT, c1[:, C_EMB:C_EMB + D], bank[3]).then_inc(S["emb_full"], 1)

            def own_top(s):
                pe.wait_ge(S["pre_hT"], s + 1)
                per_tile(hT, c1[:, C_LAY:C_LAY + D], bank[4]).then_inc(S["p1_full"], 1)

            def norms(s):
                pe.wait_ge(S["aT_ready"], s + 1)
                for t in range(TG):
                    last = mm(bank[5][:, t:t + 1], msgT[:, t * D:(t + 1) * D], ones_col, start=True, stop=True)
                last.then_inc(S["norms_full"], 1)

            def bottom(s):
                per_tile(aT, c1[:, C_LAY + D:C_LAY + 2 * D], bank[3]).then_inc(S["p2_full"], 1)

            own = {1: {40: own_transposes, 46: own_self}, 2: {56: own_transposes}, 3: {50: own_transposes, 55: own_top}}
            after = {1: {6: neighbours}, 2: {6: message, 11: gates, 28: update_back, 40: new_transposes, 46: embed},
                     3: {6: norms, 9: bottom}}

            pe.wait_ge(S["acc_read"], NT)
            pe.wait_ge(S["c1_in"], 16)
            for s in range(3 * NG):
                layer, c = s // NG + 1, s % NG
                hs = hs_b if layer == 2 else hs_a
                if s >= 2:
                    pe.wait_ge(S["aT_ready"], s - 1)
                dst = agg[:, s % 2, :].rearrange("p (a b) -> p a b", a=TG)
                for k in range(2 * NT):
                    jt, part = k // 2, k % 2
                    if k and s and k in after[(s - 1) // NG + 1]:
                        after[(s - 1) // NG + 1][k](s - 1)
                    if k in own[layer]:
                        own[layer][k](s)
                    if c == 0 and jt % TG == 0 and part == 0:
                        pe.wait_ge(S["hs_ready"], (layer - 1) * NG + jt // TG + 1)
                    last = mm(dst, hs[:, jt, part, :], adj8[:, c * TG:(c + 1) * TG, jt, :],
                              start=(k == 0), stop=(k == 2 * NT - 1))
                last.then_inc(S["agg_full"], 1)
            for k in after[3]:
                after[3][k](3 * NG - 1)


def kernel(**inputs):
    import numpy as _np
    import concourse.bacc as _bacc
    from concourse import mybir as _mybir
    from concourse.bass_utils import run_bass_kernel_spmd as _run

    g = {k: _np.asarray(v) for k, v in inputs.items()}
    f = _np.float32
    rows = lambda b: _np.broadcast_to(b[None, :], (P, D))
    blocks = _np.zeros((D, HEADS), f)
    for h in range(HEADS):
        blocks[h * HD:(h + 1) * HD, h] = g["L0_gnn_a"][:HD]
    arrays = {
        "x_rows": g["x"].reshape(NT, P, D).transpose(1, 0, 2),
        "adj_pieces": g["adj"].reshape(NT, P, 2, PIECE_T, P).transpose(0, 2, 4, 3, 1).reshape(NPIECE, P, PIECE),
        "proj": _np.concatenate([g["L0_gnn_W"], g["L0_gnn_W"].T, blocks], axis=1),
        "consts0": _np.concatenate([_np.eye(P, dtype=f), g["L1_gnn_W_self"]], axis=1),
        "consts1": _np.concatenate([
            g["L1_gnn_W_neigh"], g["L2_gnn_W_msg"].T, g["L2_gnn_W_ih"].T, g["L2_gnn_W_hh"].T, g["L3_gnn_embed"],
            g["L3_gnn_layer"][:D], g["L3_gnn_layer"][D:], rows(g["L3_gnn_embed_bias"]), rows(g["L3_gnn_layer_bias"]),
            g["L2_gnn_b_msg"][:, None], g["L2_gnn_b_ih"].reshape(3, D).T, g["L2_gnn_b_hh"].reshape(3, D).T,
            _np.zeros((P, 1), f)], axis=1),
    }
    arrays = {k: _np.ascontiguousarray(a) for k, a in arrays.items()}
    nc = _bacc.Bacc("TRN2", target_bir_lowering=False, num_devices=1)
    args = [nc.dram_tensor(k, a.shape, _mybir.dt.from_np(a.dtype), kind="ExternalInput").ap() for k, a in arrays.items()]
    out = nc.dram_tensor("out_rows", (P, NT, D), _mybir.dt.float32, kind="ExternalOutput").ap()
    build_graph_stack(nc, *args, out)
    r = _run(nc, [arrays], core_ids=[0])
    return r.results[0]["out_rows"].transpose(1, 0, 2).reshape(N, D)
```

```python
import concourse.bass as bass
from concourse import mybir
from contextlib import ExitStack


P = 128
N = 4096
D = 128
NT = N // P
TG = 4
NG = NT // TG
GW = TG * P
HEADS = 4
HD = D // HEADS
SPLIT = 1024.0
EPS_LN = 1e-5
EPS_BALL = 1e-7
MAX_TANH = 1.0 - 1e-6
SERIES_BELOW = 0.25
WIDE_SPREAD = 8.0

PIECE_T = NT // 2
PIECE = PIECE_T * P
NPIECE = 2 * NT
NBUF = 3
DVE_PART = PIECE // 2
ONE_FP8 = float(0x38)
PIECES_STATS, PIECES_PROJ, PIECES_SPLIT, PIECES_MAIN = 1, 1, 1, 5

HI = D + HEADS + 1
LO = D + HEADS
OPW = HI + LO

CHUNKS = N // GW
TURNS_START, TURNS_ROWS, TURNS_MASK, TURNS_LOGITS, TURNS_OUT, TURNS_OPERAND = 3, 11, 3, 3, 4, 7
TURNS_HEAD = 4 + TURNS_LOGITS * CHUNKS + 5 + TURNS_OUT * CHUNKS + 1
TURNS_TILE = TURNS_MASK * CHUNKS + HEADS * TURNS_HEAD
TURN_ROWS = TURNS_START
TURN_ATTEND = TURN_ROWS + TURNS_ROWS * NT
TURN_OPERAND = TURN_ATTEND + TURNS_TILE * NT
TURN_END = TURN_OPERAND + TURNS_OPERAND * NT
MASKED = 1e9

M_SELF, M_NEIGH, M_MSG, M_HR, M_HZ, M_HN, M_EMB, M_TOP, M_BOT = range(9)
NM = 9
M_IH = NM
N_RAW = (NM + 3) * D
R_EMB, R_LAY = 0, D
R_COL = 2 * D
N_ROWS = R_COL + 8
W_TOP = 4096.0


def build_graph_stack(nc, x_rows, adj_pieces, proj, consts0, matrices, vectors, p1_rows, out_rows):
    fp32, fp16, u8, u32 = mybir.dt.float32, mybir.dt.float16, mybir.dt.uint8, mybir.dt.uint32
    fp8 = mybir.dt.float8e4
    ALU = mybir.AluOpType
    ACT = mybir.ActivationFunctionType
    AX = mybir.AxisListType
    import math
    SCALE = 1.0 / math.sqrt(HD)

    with ExitStack() as ctx:
        def sb(name, shape, dt):
            return ctx.enter_context(nc.sbuf_tensor(name, shape, dt))

        def sem(name):
            return ctx.enter_context(nc.semaphore(name))

        adj = sb("adj", [P, NT, NT, P], u8)
        x = sb("x", [P, NT, D], fp32)
        hs_a = sb("hs_a", [P, NT, 2, D], fp16)
        region_op = sb("region_op", [P, NT * OPW], fp16)
        region_st = sb("region_st", [P, NBUF * PIECE], fp32)
        ident = sb("ident", [P, D], fp32)
        ident16 = sb("ident16", [P, D], fp16)
        rowbuf = sb("rowbuf", [P, TG * HI], fp32)
        hT = sb("hT", [P, GW], fp32)
        w = sb("w", [P, NT, HEADS], fp32)
        deg = sb("deg", [P, NT], fp32)
        mv = sb("mv", [P, TG, 2], fp32)
        mean = sb("mean", [P, NT], fp32)
        ssh = sb("ssh", [P, NT], fp32)
        rs = sb("rs", [P, NT], fp32)
        small = sb("small", [P, 80 + D + 24], fp32)

        xp = hs_a[:].rearrange("p t a d -> p (t a d)").bitcast(fp32).rearrange("p (t d) -> p t d", d=D)
        op0 = region_op[:].rearrange("p (t c) -> p t c", c=OPW)
        hs_b = region_op[:, 0:NT * 2 * D].rearrange("p (t a d) -> p t a d", a=2, d=D)
        early = region_op[:, 0:NT * OPW].bitcast(fp32)
        pw = early[:, 0:2 * D + 2 * HEADS]
        pwa = early[:, 2 * D + 2 * HEADS:3 * D + 3 * HEADS]
        E0 = 3 * D + 3 * HEADS
        xn_early = early[:, E0:E0 + 2 * GW].rearrange("p (b t d) -> p b t d", b=2, t=TG)
        hT_early = early[:, E0 + 2 * GW:E0 + 4 * GW].rearrange("p (b n) -> p b n", b=2)
        stage = region_st[:].rearrange("p (b n) -> p b n", b=NBUF)
        numden = rowbuf[:].rearrange("p (t c) -> p t c", c=HI)
        xn = rowbuf[:, 0:GW].rearrange("p (t d) -> p t d", d=D)
        at = [0]

        def take_words(n):
            at[0] += n
            return region_st[:, at[0] - n:at[0]]

        w_ih = take_words(3 * D)
        vec = take_words(N_ROWS)
        w16 = take_words(NM * D).bitcast(fp16).rearrange("p (a m d) -> p a m d", a=2, m=NM)
        scr = take_words(240)
        work0 = at[0]

        def work():
            return take_words(GW)

        aT16, msgT, rT, zT, dT, row16, h3T16, z_rows = [work() for _ in range(8)]
        raw0 = ((NPIECE - 1) % NBUF + 1) * PIECE
        raw = region_st[:, raw0:raw0 + N_RAW].rearrange("p (m d) -> p m d", d=D)
        magnitude = region_st[:, raw0 + N_RAW:raw0 + N_RAW + NM * D].rearrange("p (m d) -> p m d", d=D)
        aT16 = aT16.bitcast(fp16).rearrange("p (a n) -> p a n", a=2)
        hT16 = hT[:].bitcast(fp16).rearrange("p (a n) -> p a n", a=2)
        h3T16 = h3T16.bitcast(fp16).rearrange("p (a n) -> p a n", a=2)
        row16 = row16.bitcast(fp16).rearrange("p (a t d) -> p a t d", a=2, t=TG)
        p1_sb = rowbuf[:, 0:GW]
        p1_in = region_st[:, work0 + 2 * GW:work0 + 4 * GW]
        junk = w[:].rearrange("p t h -> p (t h)")
        junk8 = junk.bitcast(u8)
        b3e, b3l = vec[:, R_EMB:R_EMB + D], vec[:, R_LAY:R_LAY + D]
        b_msg = vec[:, R_COL:R_COL + 1]
        b_ih, b_hh = vec[:, R_COL + 1:R_COL + 4], vec[:, R_COL + 4:R_COL + 7]

        def col4(i):
            return scr[:, 4 * i:4 * i + 4]

        def tiles(v):
            return v.rearrange("p (t d) -> p t d", d=D)

        def tile(v, t):
            return v[:, t * D:(t + 1) * D]

        (NRM, CL, LNP, LNM, PP, SER, MASK, AT, KAP) = range(0, 18, 2)
        (NE_Z, NE_H, SSH, SSE, DOT, NE_E, N2, TH, ALF, XY, X2, TT, NUM, DEN, CA, CB, SSZ, SSA, BETA, SSC,
         COEF) = range(18, 39)
        Z_ONLY, H_ONLY, BOTH = (0, 1), (1, 2), (0, 2)

        def pair(i, part):
            return scr[:, 4 * (i + part[0]):4 * (i + part[1])]

        dve_junk = small[:, 80:208].bitcast(u8)
        STEPS_2, STEPS_3 = 59, 49
        y2e, y2l, brz, b_hn = scr[:, 158:159], scr[:, 159:160], scr[:, 160:162], scr[:, 162:163]
        top, w_scale, w_unscale = scr[:, 163:172], scr[:, 172:181], scr[:, 181:190]
        w_unsplit = scr[:, 190:199]
        topall, ih_scale = scr[:, 199:208], scr[:, 208:210]

        mhalf, phalf = small[:, 4:8], small[:, 8:12]
        ext, extall = small[:, 211:220], small[:, 220:229]
        shift = small[:, 28:32]
        rden = small[:, 32:48]
        ones_col = small[:, 48:49]
        odd, wide = small[:, 208:209], small[:, 209:210]
        flag = small[0:1, 210:211].bitcast(mybir.dt.int32)
        st = small[:, 52:76].rearrange("p (t s) -> p t s", s=6)

        logits = early[:, 0:N]
        outs = early[:, N:N + HD]
        hT_all = region_st[:, 0:N]
        gen = region_st[:, N:]
        gw, wa = gen[:, 0:2 * D + 2 * HEADS], gen[:, 264:272]
        gmv, gst, grs = gen[:, 272:274], gen[:, 274:280], gen[:, 280:281]
        s_dst, gmax, gden = gen[:, 281:282], gen[:, 282:283], gen[:, 283:284]
        missing = gen[:, 288:288 + N // 4].bitcast(u8)
        pT = rowbuf[:, 0:GW]
        a16, gxn, wa_wide = hT[:, 0:GW // 2].bitcast(fp16), hT[:, GW // 2:GW // 2 + D], hT[:, GW // 2 + D:GW]

        acc = ctx.enter_context(nc.psum_tensor("acc", [P, 8, GW], fp32))
        agg = acc[:, 0:2, :]
        bank = [acc[:, i, :] for i in range(8)]
        tr16 = bank[2].bitcast(fp16).rearrange("p (a n) -> p a n", a=2)

        S = {n: sem(n) for n in (
            "x_in", "proj_in", "c0_in", "c1_in", "landed", "conv_v", "conv_s",
            "consts_set", "dve_step", "act_step", "pool_step",
            "ve_ready", "rs_ready", "st_free", "wa_full", "wa_done", "xn0_ready", "tr0_full", "hT0_ready", "xp_full", "xp_read",
            "ext_ready", "extall_ready", "shift_ready", "w_ready", "whi_ready", "wlo_ready", "y_ready", "hi0_ready", "op0_ready",
            "acc_full", "acc_read", "xnew_ready", "hi_ready", "hs_ready",
            "top_ready", "topall_ready", "w16_ready", "odd_ready", "odd_sum", "flag_ready", "turn", "gen_in",
            "pre_tr", "pre_hT", "agg_full", "aThi_ready", "aT_ready", "l1_self", "l1_neigh",
            "msg_full", "msg_ready", "gates_full", "rz_ready", "t_ready", "n_ready", "u_ready", "uT_full",
            "relu_ready", "row16hi_ready", "row16_ready", "ssh_ready", "x3_ready", "h3_tr", "h3T_ready", "emb_full", "top_full", "p1_ready", "p1_out", "p1_in",
            "nrmh_ready", "nrme_ready", "nrmz_ready", "sqe_ready", "sqz_ready", "ln_in", "ln_out", "th_in", "th_out",
            "z_ready", "coef_ready", "zs_ready", "bhi_ready", "norms_full", "ssa_ready", "ssc_ready", "p2_full", "v_ready",
            "x4_ready", "out_done")}
        landing = [sem(f"landing{b}") for b in range(NBUF)]

        block = ctx.enter_context(nc.Block())

        def tile_of(g, t):
            return bass.ds(g * TG + t, 1)

        def group_of(g):
            return bass.ds(g * TG, TG)

        class Steps:

            def __init__(self, eng, s):
                self.eng, self.s, self.base, self.g, self.per, self.k = eng, s, 0, 0, 0, 0

            def loop(self, g, per):
                self.g, self.per, self.k = g, per, 0

            def end(self, trips):
                assert self.k == self.per, (self.k, self.per)
                self.base += trips * self.per
                self.g, self.per, self.k = 0, 0, 0

            def step(self, ins):
                ins.then_inc(self.s, 1)
                self.k += 1
                if not self.per:
                    self.base, self.k = self.base + 1, 0

            def settle(self):
                self.eng.wait_ge(self.s, self.base + self.g * self.per + self.k)

            def link(self, ins):
                self.step(ins)
                self.settle()

        @block.sync
        def _(sp):
            sp.dma_start(x[:], x_rows).then_inc(S["x_in"], 16)
            sp.dma_start(pw, proj).then_inc(S["proj_in"], 16)
            sp.dma_start(ident[:], consts0).then_inc(S["c0_in"], 16)
            for n in range(NBUF):
                sp.dma_start(stage[:, n, :], adj_pieces[n]).then_inc(landing[n], 16)
            sp.wait_ge(landing[0], 16)
            sp.sem_inc(S["landed"], 1)

            def relay_and_refill(r, n_of, b):
                nxt = (b + 1) % NBUF
                sp.wait_ge(landing[nxt], 16 * r + (32 if nxt == 0 else 16))
                sp.sem_inc(S["landed"], 1)
                sp.wait_ge(S["conv_v"], n_of + 1)
                sp.wait_ge(S["conv_s"], n_of + 1)
                sp.dma_start(stage[:, b, :], adj_pieces[bass.ds(n_of + NBUF, 1)].rearrange("a p n -> p (a n)")
                             if not isinstance(n_of, int) else adj_pieces[n_of + NBUF]).then_inc(landing[b], 16)

            rounds = (NPIECE - NBUF) // NBUF
            with sp.Fori(0, rounds) as r:
                for b in range(NBUF):
                    relay_and_refill(r, r * NBUF + b, b)
            for n in range(rounds * NBUF, NPIECE - NBUF):
                relay_and_refill(n // NBUF, n, n % NBUF)
            for n in range(NPIECE - NBUF + 1, NPIECE):
                sp.wait_ge(landing[n % NBUF], 16 * (n // NBUF + 1))
                sp.sem_inc(S["landed"], 1)
            sp.wait_ge(S["conv_v"], NPIECE - 1)
            sp.wait_ge(S["conv_s"], NPIECE - 1)
            sp.dma_start(raw.rearrange("p m d -> p (m d)"), matrices).then_inc(S["c1_in"], 16)
            sp.wait_ge(S["conv_v"], NPIECE)
            sp.wait_ge(S["conv_s"], NPIECE)
            sp.dma_start(vec, vectors).then_inc(S["c1_in"], 16)
            sp.wait_ge(S["flag_ready"], 1)
            general = sp.value_load(flag, min_val=0, max_val=1)
            with sp.If(general > 0):
                sp.wait_ge(S["c1_in"], 32)
                sp.dma_start(x[:], x_rows).then_inc(S["gen_in"], 16)
                sp.dma_start(gw, proj).then_inc(S["gen_in"], 16)
                sp.wait_ge(S["gen_in"], 32)
                sp.sem_inc(S["turn"], 1)
                sp.wait_ge(S["turn"], TURN_END)
                sp.dma_start(raw.rearrange("p m d -> p (m d)"), matrices).then_inc(S["gen_in"], 16)
                sp.dma_start(vec, vectors).then_inc(S["gen_in"], 16)
                sp.wait_ge(S["gen_in"], 64)
                sp.sem_inc(S["turn"], 1)
            sp.sem_inc(S["p1_out"], 16)
            with sp.Fori(0, NG) as g:
                sp.wait_ge(S["p1_ready"], g + 1)
                sp.dma_start(p1_rows[:, group_of(g), :], tiles(p1_sb)).then_inc(S["p1_out"], 16)
            sp.wait_ge(S["p1_out"], 16 * NG + 16)
            sp.wait_ge(S["uT_full"], NG)

            def fetch_p1(g):
                buf = p1_in[:, bass.ds(g % 2 * GW, GW)] if not isinstance(g, int) else p1_in[:, g % 2 * GW:(g % 2 + 1) * GW]
                sp.dma_start(tiles(buf), p1_rows[:, group_of(g), :]).then_inc(S["p1_in"], 16)

            def store(g):
                sp.wait_ge(S["x4_ready"], g + 1)
                sp.dma_start(out_rows[:, group_of(g), :], x[:, group_of(g), :]).then_inc(S["out_done"], 16)

            fetch_p1(0)
            sp.wait_ge(S["p1_in"], 16)
            fetch_p1(1)
            with sp.Fori(0, NG - 2) as g:
                store(g)
                sp.wait_ge(S["p1_in"], g * 16 + 32)
                fetch_p1(g + 2)
            store(NG - 2)
            store(NG - 1)
            sp.wait_ge(S["out_done"], 16 * NG)

        @block.vector
        def _(dve):
            v = nc.vector
            me = Steps(dve, S["dve_step"])

            def copy(dst, src):
                return v.tensor_scalar(dst, src, 1.0, None, ALU.mult)

            def convert(n):
                dve.wait_ge(S["landed"], n + 1)
                adj_flat = adj[:].rearrange("p i j n -> p (i j n)")
                src = region_st[:, bass.ds((n % NBUF) * PIECE, DVE_PART)]
                v.tensor_scalar(adj_flat[:, bass.ds(n * PIECE, DVE_PART)], src, ONE_FP8, None, ALU.mult).then_inc(S["conv_v"], 1)

            def anchor():
                v.memset(small[:, 50:51], 0.0)

            def statistics(g):
                anchor()
                for t in range(TG):
                    me.step(v.bn_stats(st[:, t, :], x[:, tile_of(g, t), :].rearrange("p a d -> p (a d)")))
                me.settle()
                anchor()
                for t in range(TG):
                    me.step(v.bn_aggr(mv[:, t, :], st[:, t, :]))
                me.settle()
                me.step(copy(mean[:, group_of(g)].rearrange("p (t a) -> p t a", a=1), mv[:, :, 0:1]))
                v.tensor_scalar(rs[:, group_of(g)].rearrange("p (t a) -> p t a", a=1), mv[:, :, 1:2], EPS_LN,
                                1.0 / SPLIT ** 2, ALU.add, ALU.mult).then_inc(S["ve_ready"], 1)

            def normalised(g, dst, steps=True):
                for t in range(TG):
                    last = v.tensor_scalar(dst(t), x[:, tile_of(g, t), :].rearrange("p a d -> p (a d)"),
                                           mean[:, tile_of(g, t)],
                                           rs[:, tile_of(g, t)], ALU.subtract, ALU.mult)
                    if steps and t < TG - 1:
                        me.step(last)
                return last

            dve.wait_ge(S["c0_in"], 16)
            copy(ident16[:], ident[:])
            v.memset(mhalf, -0.5)
            v.memset(ones_col, 1.0)
            me.link(v.memset(phalf, 0.5))
            v.memset(small[:, 49:50], 0.0).then_inc(S["consts_set"], 1)
            dve.wait_ge(S["proj_in"], 16)
            me.step(copy(pwa[:, 0:D], pw[:, 0:D]))
            me.step(v.tensor_tensor_reduce(out=junk, in0=pw[:, D:2 * D], in1=pw[:, D:2 * D], scale=1.0, scalar=0.0,
                                           op0=ALU.mult, op1=ALU.add, accum_out=ext[:, 8:9]))
            dve.wait_ge(S["wa_full"], 1)
            copy(pwa[:, D:D + HEADS], bank[4][:, 0:HEADS]).then_inc(S["wa_done"], 1)
            dve.wait_ge(S["x_in"], 16)

            with dve.Fori(0, NG) as g:
                me.loop(g, 2 * TG + 1)
                statistics(g)
                convert(g)
            me.end(NG)

            dve.wait_ge(S["rs_ready"], NG)

            def early_rows(g):
                normalised(g, lambda t: xn_early[:, bass.ds(g % 2, 1), t, :].rearrange("p a d -> p (a d)")
                           if not isinstance(g, int) else xn_early[:, g % 2, t, :], steps=False).then_inc(S["xn0_ready"], 1)

            early_rows(0)
            with dve.Fori(1, NG) as g:
                convert(g + NG * PIECES_STATS - 1)
                dve.wait_ge(S["tr0_full"], g)
                early_rows(g)
            convert(NG * (PIECES_STATS + PIECES_PROJ) - 1)
            dve.wait_ge(S["xp_read"], NG)
            me.step(v.tensor_reduce(ext[:, 0:4], w[:].rearrange("p t h -> p h t"), AX.X, ALU.max))
            me.link(v.tensor_reduce(ext[:, 4:8], w[:].rearrange("p t h -> p h t"), AX.X, ALU.min))
            v.tensor_scalar(ext[:, 4:8], ext[:, 4:8], -1.0, None, ALU.mult).then_inc(S["ext_ready"], 1)
            dve.wait_ge(S["extall_ready"], 1)
            me.link(v.tensor_tensor(rden[:, 0:4], extall[:, 0:4], extall[:, 4:8], ALU.add))
            me.link(v.tensor_reduce(wide, rden[:, 0:4], AX.X, ALU.max))
            me.link(v.tensor_scalar(wide, wide, WIDE_SPREAD / SCALE, None, ALU.is_gt))
            me.link(v.tensor_scalar(rden[:, 4:5], extall[:, 8:9], (60000.0 / SPLIT) ** 2 / D, None, ALU.is_gt))
            me.step(v.tensor_tensor(wide, wide, rden[:, 4:5], ALU.max))
            v.tensor_scalar(shift, extall[:, 0:4], -SCALE, math.log(SPLIT), ALU.mult, ALU.add).then_inc(S["shift_ready"], 1)

            n0 = NG * (PIECES_STATS + PIECES_PROJ)
            dve.wait_ge(S["w_ready"], HEADS)
            me.step(v.memset(op0[:, :, D + HEADS:HI], 1.0))
            dve.wait_ge(S["whi_ready"], 1)
            v.tensor_tensor(op0[:, :, HI + D:OPW], w[:], op0[:, :, D:D + HEADS], ALU.subtract).then_inc(S["wlo_ready"], 1)
            with dve.Fori(0, NG) as g:
                y = xp[:, group_of(g), :]
                yh = y.rearrange("p t (h d) -> p (t h) d", d=HD)
                wb = w[:, group_of(g), :].rearrange("p t h -> p (t h)")
                wb = wb.rearrange("p (c a) -> p c a", a=1).to_broadcast([P, TG * HEADS, HD])
                v.tensor_tensor(yh, yh, wb, ALU.mult).then_inc(S["y_ready"], 1)
                convert(g + n0)
                dve.wait_ge(S["y_ready"], g + 1)
                dve.wait_ge(S["hi0_ready"], g + 1)
                v.tensor_tensor(op0[:, group_of(g), HI:HI + D], y, op0[:, group_of(g), 0:D],
                                ALU.subtract).then_inc(S["op0_ready"], 1)

            n1 = n0 + NG * PIECES_SPLIT

            def attend(g, n):
                last = isinstance(g, int)
                for i in range(PIECES_MAIN if last else 3):
                    convert(n + i)
                dve.wait_ge(S["acc_full"], (g + 1) * TG)
                sums = acc[:, bass.ds(g % 2 * TG, TG), :] if not last else acc[:, g % 2 * TG:(g % 2 + 1) * TG, :]
                me.step(v.tensor_scalar(deg[:, group_of(g)].rearrange("p (t a) -> p t a", a=1), sums[:, :, D + HEADS:HI],
                                        1.0, None, ALU.mult))
                me.link(v.tensor_scalar(rden.rearrange("p (t h) -> p t h", h=HEADS), sums[:, :, D:D + HEADS],
                                        1e-12, None, ALU.max))
                me.link(v.reciprocal(rden, rden))
                num = sums[:, :, 0:D].rearrange("p t (h d) -> p t h d", d=HD)
                rb = rden.rearrange("p (t h a) -> p t h a", h=HEADS, a=1).to_broadcast([P, TG, HEADS, HD])
                v.tensor_tensor(xn.rearrange("p t (h d) -> p t h d", d=HD), num, rb, ALU.mult).then_inc(S["acc_read"], 1)
                if not last:
                    convert(n + 3)
                dve.wait_ge(S["acc_read"], g + 1)
                me.link(v.tensor_tensor(x[:, group_of(g), :], x[:, group_of(g), :], xn, ALU.add))
                statistics(g)
                if not last:
                    convert(n + 4)
                operand(g, 0, xn, hs_a)

            def operand(g, count, xnew, hs):
                dve.wait_ge(S["rs_ready"], g + NG + count + 1)
                normalised(g, lambda t: xnew[:, t, :]).then_inc(S["xnew_ready"], 1)
                dve.wait_ge(S["hi_ready"], g + count + 1)
                dve.wait_ge(S["xnew_ready"], g + count + 1)
                v.scalar_tensor_tensor(hs[:, group_of(g), 1, :], xnew, 0.0, hs[:, group_of(g), 0, :],
                                       ALU.max, ALU.subtract).then_inc(S["hs_ready"], 1)
                dve.wait_ge(S["hs_ready"], g + count + 1)

            with dve.Fori(0, NG - 1) as g:
                me.loop(g, 4 + 2 * TG + 1 + TG - 1)
                attend(g, g * PIECES_MAIN + n1)
            me.end(NG - 1)
            attend(NG - 1, (NG - 1) * PIECES_MAIN + n1)

            def general_attention():
                turn = S["turn"]

                def row_of(v3, i):
                    return v3[:, bass.ds(i, 1), :].rearrange("p a d -> p (a d)")

                def tile_statistics(i, at, scale):
                    dve.wait_ge(turn, at)
                    anchor()
                    v.bn_stats(gst, row_of(x, i)).then_inc(turn, 1)
                    dve.wait_ge(turn, at + 1)
                    anchor()
                    v.bn_aggr(gmv, gst).then_inc(turn, 1)
                    dve.wait_ge(turn, at + 2)
                    v.tensor_scalar(grs, gmv[:, 1:2], EPS_LN, scale, ALU.add, ALU.mult).then_inc(turn, 1)
                    dve.wait_ge(turn, at + 4)
                    v.tensor_scalar(gxn, row_of(x, i), gmv[:, 0:1], grs, ALU.subtract, ALU.mult).then_inc(turn, 1)

                dve.wait_ge(turn, 2)
                copy(wa, bank[0][:, 0:2 * HEADS]).then_inc(turn, 1)
                with dve.Fori(0, NT) as i:
                    at = i * TURNS_ROWS + TURN_ROWS
                    tile_statistics(i, at, 1.0)
                    dve.wait_ge(turn, at + 5)
                    v.tensor_scalar(gxn, gxn, 0.0, None, ALU.max).then_inc(turn, 1)
                    dve.wait_ge(turn, at + 7)
                    copy(tile(pT, 0), bank[0][:, 0:D]).then_inc(turn, 1)
                    dve.wait_ge(turn, at + 8)
                    copy(hT_all[:, bass.ds(i * D, D)], tile(pT, 0)).then_inc(turn, 1)
                    dve.wait_ge(turn, at + 10)
                    copy(row_of(xp, i), bank[1][:, 0:D]).then_inc(turn, 1)
                with dve.Fori(0, NT) as i:
                    at = i * TURNS_TILE + TURN_ATTEND
                    for c in range(CHUNKS):
                        k = at + c * TURNS_MASK
                        dve.wait_ge(turn, k)
                        src = adj[:, bass.ds(i, 1), c * TG:(c + 1) * TG, :].rearrange("p a j n -> p (a j n)")
                        v.tensor_scalar(a16, src, 1.0 / ONE_FP8, None, ALU.mult).then_inc(turn, 1)
                        dve.wait_ge(turn, k + 2)
                        v.tensor_scalar(missing[:, c * GW:(c + 1) * GW], bank[0], -1.0, 1.0, ALU.mult,
                                        ALU.add).then_inc(turn, 1)
                    for h in range(HEADS):
                        k = at + (CHUNKS * TURNS_MASK + h * TURNS_HEAD)
                        dve.wait_ge(turn, k)
                        copy(wa_wide, wa[:, h:h + 1].to_broadcast([P, D])).then_inc(turn, 1)
                        dve.wait_ge(turn, k + 1)
                        copy(tile(pT, 0), hT_all[:, bass.ds(i * D, D)]).then_inc(turn, 1)
                        dve.wait_ge(turn, k + 3)
                        copy(s_dst, bank[1][:, 0:1]).then_inc(turn, 1)
                        for c in range(CHUNKS):
                            kc = k + (4 + c * TURNS_LOGITS)
                            lc = logits[:, c * GW:(c + 1) * GW]
                            dve.wait_ge(turn, kc + 1)
                            v.tensor_scalar(lc, bank[2], s_dst, SCALE, ALU.add, ALU.mult).then_inc(turn, 1)
                            dve.wait_ge(turn, kc + 2)
                            v.scalar_tensor_tensor(lc, missing[:, c * GW:(c + 1) * GW], -MASKED, lc, ALU.mult,
                                                   ALU.add).then_inc(turn, 1)
                        k = k + (4 + CHUNKS * TURNS_LOGITS)
                        dve.wait_ge(turn, k)
                        v.tensor_reduce(gmax, logits, AX.X, ALU.max).then_inc(turn, 1)
                        dve.wait_ge(turn, k + 1)
                        v.tensor_scalar(gmax, gmax, -1.0, None, ALU.mult).then_inc(turn, 1)
                        dve.wait_ge(turn, k + 3)
                        v.reciprocal(gden, gden).then_inc(turn, 1)
                        dve.wait_ge(turn, k + 4)
                        v.memset(outs, 0.0).then_inc(turn, 1)
                        for c in range(CHUNKS):
                            kc = k + (5 + c * TURNS_OUT)
                            dve.wait_ge(turn, kc + 1)
                            copy(pT, bank[3]).then_inc(turn, 1)
                            dve.wait_ge(turn, kc + 3)
                            v.tensor_tensor(outs, outs, bank[4][:, 0:HD], ALU.add).then_inc(turn, 1)
                        dve.wait_ge(turn, k + (5 + CHUNKS * TURNS_OUT))
                        xh = x[:, bass.ds(i, 1), h * HD:(h + 1) * HD].rearrange("p a d -> p (a d)")
                        v.scalar_tensor_tensor(xh, outs, gden, xh, ALU.mult, ALU.add).then_inc(turn, 1)
                with dve.Fori(0, NT) as i:
                    at = i * TURNS_OPERAND + TURN_OPERAND
                    tile_statistics(i, at, 1.0 / SPLIT ** 2)
                    hi = hs_a[:, bass.ds(i, 1), 0, :].rearrange("p a d -> p (a d)")
                    lo = hs_a[:, bass.ds(i, 1), 1, :].rearrange("p a d -> p (a d)")
                    dve.wait_ge(turn, at + 5)
                    v.tensor_scalar(hi, gxn, 0.0, None, ALU.max).then_inc(turn, 1)
                    dve.wait_ge(turn, at + 6)
                    v.scalar_tensor_tensor(lo, gxn, 0.0, hi, ALU.max, ALU.subtract).then_inc(turn, 1)
                dve.wait_ge(turn, TURN_END + 1)

            me.link(v.tensor_reduce(odd, deg[:], AX.X, ALU.min))
            me.link(v.tensor_scalar(odd, odd, 0.5, None, ALU.is_lt))
            v.tensor_tensor(odd, odd, wide, ALU.max).then_inc(S["odd_ready"], 1)
            dve.wait_ge(S["odd_sum"], 1)
            v.tensor_scalar(flag, bank[0][0:1, 0:1], 0.5, None, ALU.is_gt).then_inc(S["flag_ready"], 1)
            dve.wait_ge(S["flag_ready"], 1)
            general = dve.value_load(flag, min_val=0, max_val=1)
            with dve.If(general > 0):
                general_attention()

            dve.wait_ge(S["c1_in"], 32)
            me.link(v.tensor_scalar(magnitude.bitcast(u32), raw[:, 0:NM, :].bitcast(u32), 0x7FFFFFFF, None, ALU.bitwise_and))
            v.tensor_reduce(top, magnitude, AX.X, ALU.max).then_inc(S["top_ready"], 1)
            me.step(v.tensor_scalar(deg[:], deg[:], 1.0, None, ALU.max))
            dve.wait_ge(S["topall_ready"], 1)
            me.link(v.tensor_scalar(topall, topall, 1e-30, 1.0 / W_TOP, ALU.max, ALU.mult))
            me.link(v.reciprocal(w_scale, topall))
            for m in range(NM):
                me.step(v.tensor_scalar(raw[:, m, :], raw[:, m, :], w_scale[:, m:m + 1], None, ALU.mult))
            me.settle()
            me.link(copy(w16[:, 0, :, :], raw[:, 0:NM, :]))
            me.step(v.tensor_tensor(w16[:, 1, :, :], raw[:, 0:NM, :], w16[:, 0, :, :], ALU.subtract))
            me.step(v.tensor_scalar(w_unsplit, topall, 1.0 / SPLIT, None, ALU.mult))
            me.step(copy(w_unscale, topall))
            me.step(v.tensor_scalar(ih_scale, w_scale[:, M_HR:M_HZ + 1], SPLIT, None, ALU.mult))
            me.step(v.tensor_scalar(b_hn, w_scale[:, M_HN:M_HN + 1], SPLIT, None, ALU.mult))
            me.link(v.reciprocal(deg[:], deg[:]))
            me.step(v.tensor_scalar(deg[:], deg[:], w_unscale[:, M_NEIGH:M_NEIGH + 1], None, ALU.mult))
            me.step(v.tensor_tensor(b_hn, b_hn, b_hh[:, 2:3], ALU.mult))
            me.step(v.tensor_tensor(brz, b_ih[:, 0:2], b_hh[:, 0:2], ALU.add))
            for i in range(2):
                me.step(v.tensor_scalar(tile(w_ih, i), raw[:, M_IH + i, :], ih_scale[:, i:i + 1], None, ALU.mult))
            me.step(copy(tile(w_ih, 2), raw[:, M_IH + 2, :]))
            for b, y2 in ((b3e, y2e), (b3l, y2l)):
                me.link(v.tensor_tensor_reduce(out=junk, in0=b, in1=b, scale=1.0, scalar=0.0, op0=ALU.mult,
                                               op1=ALU.add, accum_out=y2))
            v.memset(small[:, 51:52], 0.0).then_inc(S["w16_ready"], 1)

            def low_aggregate(g, count):
                dve.wait_ge(S["aThi_ready"], g + count + 1)
                src = agg[:, bass.ds((g + count) % 2, 1), :].rearrange("p a n -> p (a n)")
                v.scalar_tensor_tensor(aT16[:, 1, :], src, 1.0 / SPLIT, aT16[:, 0, :], ALU.mult,
                                       ALU.subtract).then_inc(S["aT_ready"], 1)

            with dve.Fori(0, NG) as g:
                me.loop(g, TG + 1 + 2 * TG + 1 + (TG - 1))
                low_aggregate(g, 0)
                dve.wait_ge(S["l1_self"], g + 1)
                dve.wait_ge(S["l1_neigh"], g + 1)
                for t in range(TG):
                    xt = x[:, tile_of(g, t), :].rearrange("p a d -> p (a d)")
                    me.step(v.scalar_tensor_tensor(xt, tile(bank[3], t), deg[:, tile_of(g, t)], xt, ALU.mult, ALU.add))
                me.settle()
                me.link(v.scalar_tensor_tensor(x[:, group_of(g), :], tiles(bank[4]), w_unsplit[:, M_SELF:M_SELF + 1],
                                               x[:, group_of(g), :], ALU.mult, ALU.add))
                statistics(g)
                operand(g, NG, tiles(dT), hs_b)
            me.end(NG)

            C = col4

            def artanh_start(part):
                nrm, (clipped, floored) = pair(NE_Z, part), (pair(CL, part), pair(NRM, part))
                me.step(v.tensor_scalar(floored, nrm, EPS_BALL, None, ALU.max))
                v.tensor_scalar(clipped, nrm, EPS_BALL, MAX_TANH, ALU.max, ALU.min).then_inc(S["ln_in"], 1)

            def artanh_series(part, count):
                clipped, square, series = pair(CL, part), pair(PP, part), pair(SER, part)
                dve.wait_ge(S["ln_in"], count)
                me.link(v.tensor_tensor(square, clipped, clipped, ALU.mult))
                me.step(v.reciprocal(pair(KAP, part), pair(NRM, part)))
                me.link(v.tensor_scalar(series, square, 1.0 / 11, None, ALU.mult))
                for k in (9, 7, 5, 3):
                    me.link(v.scalar_tensor_tensor(series, series, 1.0 / k, square, ALU.add, ALU.mult))
                me.step(v.scalar_tensor_tensor(series, series, 1.0, clipped, ALU.add, ALU.mult))
                me.step(v.tensor_scalar(pair(MASK, part), clipped, SERIES_BELOW, None, ALU.is_lt))

            def artanh_finish(part, count):
                series, at = pair(SER, part), pair(AT, part)
                dve.wait_ge(S["ln_out"], count)
                me.link(v.tensor_tensor(at, pair(LNP, part), pair(LNM, part), ALU.subtract))
                me.link(v.scalar_tensor_tensor(series, at, -0.5, series, ALU.mult, ALU.add))
                me.link(v.tensor_tensor(series, series, pair(MASK, part), ALU.mult))
                me.link(v.scalar_tensor_tensor(at, at, 0.5, series, ALU.mult, ALU.add))
                me.link(v.tensor_tensor(pair(KAP, part), at, pair(KAP, part), ALU.mult))

            def dots(e_tiles, bias, scale):
                for t in range(TG):
                    me.step(v.tensor_tensor_reduce(out=tile(dve_junk, t), in0=e_tiles(t), in1=bias, scale=scale,
                                                   scalar=0.0, op0=ALU.mult, op1=ALU.add, accum_out=C(DOT)[:, t:t + 1]))

            def exp_argument(kappa):
                me.link(v.tensor_tensor(C(N2), C(NE_E), kappa, ALU.mult))
                v.tensor_scalar(C(N2), C(N2), EPS_BALL, None, ALU.max).then_inc(S["th_in"], 1)

            def sum_coefficients(kappa, th_count, y2):
                dve.wait_ge(S["th_in"], th_count)
                me.link(v.reciprocal(C(ALF), C(N2)))
                me.link(v.tensor_tensor(C(ALF), C(ALF), kappa, ALU.mult))
                dve.wait_ge(S["th_out"], th_count)
                me.link(v.tensor_tensor(C(ALF), C(ALF), C(TH), ALU.mult))
                me.step(v.tensor_tensor(C(XY), C(ALF), C(DOT), ALU.mult))
                me.link(v.tensor_tensor(C(X2), C(ALF), C(ALF), ALU.mult))
                me.step(v.tensor_scalar(C(TT), C(XY), 2.0, 1.0, ALU.mult, ALU.add))
                me.link(v.tensor_tensor(C(X2), C(X2), C(SSE), ALU.mult))
                me.step(v.scalar_tensor_tensor(C(NUM), C(TT), y2, C(ALF), ALU.add, ALU.mult))
                me.step(v.scalar_tensor_tensor(C(DEN), C(X2), y2, C(TT), ALU.mult, ALU.add))
                me.link(v.tensor_scalar(C(CB), C(X2), -1.0, 1.0, ALU.mult, ALU.add))
                me.link(v.tensor_scalar(C(DEN), C(DEN), EPS_BALL, None, ALU.max))
                me.link(v.reciprocal(C(DEN), C(DEN)))
                me.step(v.tensor_tensor(C(CA), C(NUM), C(DEN), ALU.mult))
                me.link(v.tensor_tensor(C(CB), C(CB), C(DEN), ALU.mult))

            def ball_rows(e_tiles, bias):
                for t in range(TG):
                    me.step(v.tensor_scalar(tile(z_rows, t), e_tiles(t), C(CA)[:, t:t + 1], None, ALU.mult))
                me.settle()
                for t in range(TG):
                    last = v.scalar_tensor_tensor(tile(z_rows, t), bias, C(CB)[:, t:t + 1], tile(z_rows, t), ALU.mult, ALU.add)
                    if t < TG - 1:
                        me.step(last)
                last.then_inc(S["z_ready"], 1)

            def layer2(a, b, c):
                A, B, E = a is not None, b is not None, c is not None
                if A:
                    low_aggregate(a, NG)
                if B:
                    dve.wait_ge(S["rs_ready"], b + 3 * NG + 1)
                    normalised(b, lambda t: tile(dT, t)).then_inc(S["xnew_ready"], 1)
                if E:
                    ball_rows(lambda t: tile(bank[3], t), b3e)
                if B:
                    dve.wait_ge(S["row16hi_ready"], b + 1)
                    v.scalar_tensor_tensor(row16[:, 1, :, :], tiles(dT), 0.0, row16[:, 0, :, :], ALU.max,
                                           ALU.subtract).then_inc(S["row16_ready"], 1)
                part = BOTH if B and E else H_ONLY if B else Z_ONLY
                count = b + 1 if B else NG + 1
                if E:
                    dve.wait_ge(S["nrmz_ready"], c + 1)
                if B:
                    dve.wait_ge(S["nrmh_ready"], b + 1)
                if B or E:
                    artanh_start(part)
                if B:
                    me.step(copy(ssh[:, group_of(b)], C(SSH)))
                if B or E:
                    artanh_series(part, count)
                if A:
                    me.step(v.tensor_tensor(dT, hT16[:, 0, :], hT16[:, 1, :], ALU.add))
                    dve.wait_ge(S["gates_full"], a + 1)
                    dve.wait_ge(S["rz_ready"], a + 1)
                    me.link(v.scalar_tensor_tensor(rT, bank[7], b_hn, rT, ALU.add, ALU.mult))
                    v.scalar_tensor_tensor(rT, rT, w_unsplit[:, M_HN:M_HN + 1], bank[6], ALU.mult,
                                           ALU.add).then_inc(S["t_ready"], 1)
                    dve.wait_ge(S["n_ready"], a + 1)
                    me.link(v.scalar_tensor_tensor(dT, dT, 1.0 / SPLIT, rT, ALU.mult, ALU.subtract))
                    me.link(v.tensor_tensor(zT, zT, dT, ALU.mult))
                    v.tensor_tensor(zT, zT, rT, ALU.add).then_inc(S["u_ready"], 1)
                if B or E:
                    artanh_finish(part, count)
                if E:
                    v.tensor_scalar(C(COEF), pair(KAP, Z_ONLY), SPLIT, None, ALU.mult).then_inc(S["coef_ready"], 1)
                if B:
                    dve.wait_ge(S["sqe_ready"], b + 1)
                    dots(lambda t: tile(bank[3], t), b3e, w_unsplit[:, M_EMB:M_EMB + 1])
                    dve.wait_ge(S["nrme_ready"], b + 1)
                    exp_argument(pair(KAP, H_ONLY))
                if A:
                    dve.wait_ge(S["uT_full"], a + 1)
                    v.tensor_tensor(x[:, group_of(a), :], x[:, group_of(a), :], tiles(bank[7]), ALU.add).then_inc(S["x3_ready"], 1)
                    dve.wait_ge(S["x3_ready"], a + 1)
                    statistics(a)
                if E:
                    dve.wait_ge(S["bhi_ready"], c + 1)
                    v.tensor_tensor(hs_a[:, group_of(c), 1, :], tiles(z_rows), hs_a[:, group_of(c), 0, :],
                                    ALU.subtract).then_inc(S["hs_ready"], 1)
                if B:
                    sum_coefficients(pair(KAP, H_ONLY), b + 1, y2e)
                    me.link(v.tensor_scalar(C(CA), C(CA), w_unsplit[:, M_EMB:M_EMB + 1], None, ALU.mult))
                if E:
                    dve.wait_ge(S["hs_ready"], c + 2 * NG + 1)

            layer2(0, None, None)
            layer2(1, 0, None)
            with dve.Fori(2, NG) as g:
                me.loop(g - 2, STEPS_2)
                layer2(g, g - 1, g - 2)
            me.end(NG - 2)
            layer2(None, NG - 1, NG - 2)
            layer2(None, None, NG - 1)

            with dve.Fori(0, NG) as g:
                me.loop(g, STEPS_3)
                low_aggregate(g, 2 * NG)
                dve.wait_ge(S["norms_full"], g + 1)
                copy(C(SSA), bank[5][:, 0:TG]).then_inc(S["ssa_ready"], 1)
                dve.wait_ge(S["nrmh_ready"], g + NG + 1)
                v.tensor_scalar(C(N2), C(NE_H), EPS_BALL, None, ALU.max).then_inc(S["th_in"], 1)
                dve.wait_ge(S["th_in"], g * 2 + NG + 1)
                me.link(v.reciprocal(C(BETA), C(N2)))
                dve.wait_ge(S["th_out"], g * 2 + NG + 1)
                me.link(v.tensor_tensor(C(BETA), C(BETA), C(TH), ALU.mult))
                me.step(v.tensor_scalar(C(COEF), C(BETA), w_unscale[:, M_BOT:M_BOT + 1], None, ALU.mult))
                me.link(v.tensor_tensor(C(SSC), C(BETA), C(BETA), ALU.mult))
                me.link(v.tensor_tensor(C(SSC), C(SSC), C(SSA), ALU.mult))
                v.tensor_tensor(C(SSC), C(SSC), ssh[:, group_of(g)], ALU.add).then_inc(S["ssc_ready"], 1)
                dve.wait_ge(S["p1_in"], g * 16 + 16)
                dve.wait_ge(S["p2_full"], g + 1)

                def vrow(t):
                    return tile(dT, t)

                for t in range(TG):
                    last = v.scalar_tensor_tensor(vrow(t), tile(bank[3], t), C(COEF)[:, t:t + 1],
                                                  p1_in[:, bass.ds(g % 2 * GW + t * D, D)], ALU.mult, ALU.add)
                    if t < TG - 1:
                        me.step(last)
                last.then_inc(S["v_ready"], 1)
                dve.wait_ge(S["nrmz_ready"], g + NG + 1)
                artanh_start(Z_ONLY)
                artanh_series(Z_ONLY, g + NG + 2)
                artanh_finish(Z_ONLY, g + NG + 2)
                dve.wait_ge(S["v_ready"], g + 1)
                dots(vrow, b3l, 1.0)
                dve.wait_ge(S["nrme_ready"], g + NG + 1)
                exp_argument(pair(KAP, Z_ONLY))
                sum_coefficients(pair(KAP, Z_ONLY), g * 2 + NG + 2, y2l)
                ball_rows(vrow, b3l)
                dve.wait_ge(S["z_ready"], g + NG + 1)
                v.tensor_tensor(x[:, group_of(g), :], x[:, group_of(g), :], tiles(z_rows), ALU.add).then_inc(S["x4_ready"], 1)
                dve.wait_ge(S["x4_ready"], g + 1)
            me.end(NG)

        @block.gpsimd
        def _(pool):
            q = nc.gpsimd

            def power(dst, src, half):
                return q.tensor_tensor(dst, src, half, ALU.pow)

            pool.wait_ge(S["consts_set"], 1)

            def inverse_deviation(g, count):
                pool.wait_ge(S["ve_ready"], g + count + 1)
                power(rs[:, group_of(g)], rs[:, group_of(g)], mhalf).then_inc(S["rs_ready"], 1)

            with pool.Fori(0, NG) as g:
                inverse_deviation(g, 0)
            pool.wait_ge(S["ext_ready"], 1)
            q.partition_all_reduce(extall, ext, P, bass.bass_isa.ReduceOp.max).then_inc(S["extall_ready"], 1)
            with pool.Fori(0, NG) as g:
                inverse_deviation(g, NG)
            pool.wait_ge(S["flag_ready"], 1)
            general = pool.value_load(flag, min_val=0, max_val=1)
            with pool.If(general > 0):
                for first, per in ((TURN_ROWS, TURNS_ROWS), (TURN_OPERAND, TURNS_OPERAND)):
                    with pool.Fori(0, NT) as i:
                        pool.wait_ge(S["turn"], i * per + (first + 3))
                        power(grs, grs, mhalf[:, 0:1]).then_inc(S["turn"], 1)
                pool.wait_ge(S["turn"], TURN_END + 1)
            pool.wait_ge(S["top_ready"], 1)
            q.partition_all_reduce(topall, top, P, bass.bass_isa.ReduceOp.max).then_inc(S["topall_ready"], 1)
            with pool.Fori(0, NG) as g:
                inverse_deviation(g, 2 * NG)

            def norm_h(g):
                pool.wait_ge(S["ssh_ready"], g + 1)
                power(col4(NE_H), col4(SSH), phalf).then_inc(S["nrmh_ready"], 1)

            def norm_e(g, count):
                pool.wait_ge(S["sqe_ready"], g + count + 1)
                power(col4(NE_E), col4(SSE), phalf).then_inc(S["nrme_ready"], 1)

            def norm_z(g):
                pool.wait_ge(S["sqz_ready"], g + 1)
                power(col4(NE_Z), col4(SSZ), phalf).then_inc(S["nrmz_ready"], 1)

            inverse_deviation(0, 3 * NG)
            with pool.Fori(1, NG) as g:
                norm_h(g - 1)
                norm_e(g - 1, 0)
                inverse_deviation(g, 3 * NG)
                norm_z(g - 1)
            norm_h(NG - 1)
            norm_e(NG - 1, 0)
            norm_z(NG - 1)
            with pool.Fori(0, NG) as g:
                pool.wait_ge(S["ssa_ready"], g + 1)
                power(col4(NE_H), col4(SSA), phalf).then_inc(S["nrmh_ready"], 1)
                pool.wait_ge(S["ssc_ready"], g + 1)
                power(col4(NE_Z), col4(SSC), phalf).then_inc(S["nrmz_ready"], 1)
                norm_e(g, NG)

        @block.scalar
        def _(act):
            a = nc.scalar

            def convert(n):
                act.wait_ge(S["landed"], n + 1)
                adj_flat = adj[:].rearrange("p i j n -> p (i j n)")
                a.activation(adj_flat[:, bass.ds(n * PIECE + DVE_PART, PIECE - DVE_PART)],
                             region_st[:, bass.ds((n % NBUF) * PIECE + DVE_PART, PIECE - DVE_PART)], ACT.Copy,
                             scale=ONE_FP8).then_inc(S["conv_s"], 1)

            def relu_rows_T(g):
                act.wait_ge(S["tr0_full"], g + 1)
                dst = hT_early[:, bass.ds(g % 2, 1), :].rearrange("p a n -> p (a n)") if not isinstance(g, int) else hT_early[:, g % 2, :]
                a.activation(dst, bank[4], ACT.Relu, scale=1.0 / SPLIT).then_inc(S["hT0_ready"], 1)

            def projections(g):
                act.wait_ge(S["xp_full"], g + 1)
                for half in range(2):
                    b = bank[5 + half][:, 0:2 * (D + HEADS)].rearrange("p (t c) -> p t c", c=D + HEADS)
                    a.activation(xp[:, bass.ds(g * TG + 2 * half, 2), :], b[:, :, 0:D], ACT.Copy)
                    last = a.activation(w[:, bass.ds(g * TG + 2 * half, 2), :], b[:, :, D:D + HEADS], ACT.Copy)
                last.then_inc(S["xp_read"], 1)

            with act.Fori(0, NG) as g:
                convert(g)
            relu_rows_T(0)
            with act.Fori(1, NG) as g:
                convert(g + NG * PIECES_STATS - 1)
                relu_rows_T(g)
                projections(g - 1)
            projections(NG - 1)
            convert(NG * (PIECES_STATS + PIECES_PROJ) - 1)
            act.wait_ge(S["shift_ready"], 1)
            for h in range(HEADS):
                wh = w[:, :, h:h + 1].rearrange("p t a -> p (t a)")
                a.activation(wh, wh, ACT.Exp, bias=shift[:, h:h + 1], scale=SCALE).then_inc(S["w_ready"], 1)
            act.wait_ge(S["w_ready"], HEADS)
            a.copy(op0[:, :, D:D + HEADS], w[:]).then_inc(S["whi_ready"], 1)
            n0 = NG * (PIECES_STATS + PIECES_PROJ)
            with act.Fori(0, NG) as g:
                act.wait_ge(S["y_ready"], g + 1)
                a.copy(op0[:, group_of(g), 0:D], xp[:, group_of(g), :]).then_inc(S["hi0_ready"], 1)
                convert(g + n0)

            def high_part(g, cnt, src, hs, func):
                act.wait_ge(S["xnew_ready"], g + cnt + 1)
                a.activation(hs[:, group_of(g), 0, :], src, func).then_inc(S["hi_ready"], 1)

            n1 = n0 + NG * PIECES_SPLIT
            with act.Fori(0, NG) as g:
                for i in range(PIECES_MAIN):
                    convert(g * PIECES_MAIN + (n1 + i))
                high_part(g, 0, xn, hs_a, ACT.Relu)

            def own_rows_T(g, cnt):
                act.wait_ge(S["pre_tr"], g + cnt + 1)
                a.activation(hT16, tr16, ACT.Copy).then_inc(S["pre_hT"], 1)

            def high_aggregate(g, cnt, square):
                act.wait_ge(S["agg_full"], g + cnt + 1)
                src = agg[:, bass.ds((g + cnt) % 2, 1), :].rearrange("p a n -> p (a n)")
                if square:
                    a.activation(msgT, src, ACT.Square, scale=1.0 / SPLIT)
                a.activation(aT16[:, 0, :], src, ACT.Copy, scale=1.0 / SPLIT).then_inc(S["aThi_ready"], 1)

            def square_sums(src, sums, scale=1.0):
                for t in range(TG):
                    last = a.activation(tile(junk8, t), src(t), ACT.Square, scale=scale, accum_out=sums[:, t:t + 1])
                return last

            def logarithms(part, n):
                act.wait_ge(S["ln_in"], n)
                a.activation(pair(LNP, part), pair(CL, part), ACT.Ln, bias=1.0)
                a.activation(pair(LNM, part), pair(CL, part), ACT.Ln, bias=1.0, scale=-1.0).then_inc(S["ln_out"], 1)

            def tanh_of(n):
                act.wait_ge(S["th_in"], n)
                a.activation(col4(TH), col4(N2), ACT.Tanh).then_inc(S["th_out"], 1)

            act.wait_ge(S["flag_ready"], 1)
            general = act.value_load(flag, min_val=0, max_val=1)
            with act.If(general > 0):
                with act.Fori(0, NT) as i:
                    for h in range(HEADS):
                        k = CHUNKS * TURNS_MASK + h * TURNS_HEAD + 4 + CHUNKS * TURNS_LOGITS + 2
                        act.wait_ge(S["turn"], i * TURNS_TILE + (TURN_ATTEND + k))
                        a.activation(logits, logits, ACT.Exp, bias=gmax, accum_out=gden).then_inc(S["turn"], 1)
                act.wait_ge(S["turn"], TURN_END + 1)

            with act.Fori(0, NG) as g:
                own_rows_T(g, 0)
                high_aggregate(g, 0, False)
                high_part(g, NG, tiles(dT), hs_b, ACT.Relu)

            def layer2(s, b, c):
                A, B, E = s is not None, b is not None, c is not None
                if A:
                    if not (isinstance(s, int) and s == 0):
                        act.wait_ge(S["u_ready"], s)
                    own_rows_T(s, NG)
                    high_aggregate(s, NG, False)
                if B:
                    act.wait_ge(S["xnew_ready"], b + 2 * NG + 1)
                    a.activation(row16[:, 0, :, :], tiles(dT), ACT.Relu).then_inc(S["row16hi_ready"], 1)
                if A:
                    act.wait_ge(S["msg_full"], s + 1)
                    a.activation(msgT, bank[6], ACT.Relu, bias=b_msg, scale=w_unscale[:, M_MSG:M_MSG + 1]).then_inc(S["msg_ready"], 1)
                if E:
                    act.wait_ge(S["z_ready"], c + 1)
                    square_sums(lambda t: tile(z_rows, t), col4(SSZ)).then_inc(S["sqz_ready"], 1)
                if B:
                    act.wait_ge(S["row16_ready"], b + 1)
                    a.activation(dT, dT, ACT.Relu).then_inc(S["relu_ready"], 1)
                    act.wait_ge(S["relu_ready"], b + 1)
                    square_sums(lambda t: tile(dT, t), col4(SSH), 1.0 / SPLIT).then_inc(S["ssh_ready"], 1)
                if A:
                    act.wait_ge(S["gates_full"], s + 1)
                    a.activation(rT, bank[4], ACT.Sigmoid, bias=brz[:, 0:1], scale=w_unsplit[:, M_HR:M_HR + 1])
                    a.activation(zT, bank[5], ACT.Sigmoid, bias=brz[:, 1:2], scale=w_unsplit[:, M_HZ:M_HZ + 1]).then_inc(S["rz_ready"], 1)
                if B:
                    act.wait_ge(S["h3_tr"], b + 1)
                    a.activation(h3T16, tr16, ACT.Copy).then_inc(S["h3T_ready"], 1)
                if A:
                    act.wait_ge(S["t_ready"], s + 1)
                    a.activation(rT, rT, ACT.Tanh, bias=b_ih[:, 2:3]).then_inc(S["n_ready"], 1)
                if B or E:
                    logarithms(BOTH if B and E else H_ONLY if B else Z_ONLY, b + 1 if B else NG + 1)
                if B:
                    act.wait_ge(S["emb_full"], b + 1)
                    square_sums(lambda t: tile(bank[3], t), col4(SSE), w_unsplit[:, M_EMB:M_EMB + 1]).then_inc(S["sqe_ready"], 1)
                    act.wait_ge(S["top_full"], b + 1)
                    act.wait_ge(S["p1_out"], b * 16 + 16)
                    a.activation(p1_sb, bank[4], ACT.Copy, scale=w_unsplit[:, M_TOP:M_TOP + 1]).then_inc(S["p1_ready"], 1)
                    tanh_of(b + 1)
                if E:
                    act.wait_ge(S["coef_ready"], c + 1)
                    act.wait_ge(S["sqz_ready"], c + 1)
                    for t in range(TG):
                        r = tile(z_rows, t)
                        last = a.activation(r, r, ACT.Copy, scale=col4(COEF)[:, t:t + 1])
                    last.then_inc(S["zs_ready"], 1)
                    act.wait_ge(S["zs_ready"], c + 1)
                    a.activation(hs_a[:, group_of(c), 0, :], tiles(z_rows), ACT.Copy).then_inc(S["bhi_ready"], 1)

            act.wait_ge(S["w16_ready"], 1)
            layer2(0, None, None)
            layer2(1, 0, None)
            with act.Fori(2, NG) as g:
                layer2(g, g - 1, g - 2)
            layer2(None, NG - 1, NG - 2)
            layer2(None, None, NG - 1)

            with act.Fori(0, NG) as g:
                high_aggregate(g, 2 * NG, True)
                tanh_of(g * 2 + NG + 1)
                act.wait_ge(S["v_ready"], g + 1)
                square_sums(lambda t: tile(dT, t), col4(SSE)).then_inc(S["sqe_ready"], 1)
                logarithms(Z_ONLY, g + NG + 2)
                tanh_of(g * 2 + NG + 2)

        @block.tensor
        def _(pe):
            mm = nc.tensor.matmul
            adj8 = adj[:].bitcast(fp8)

            def transposes(src, dst):
                for t in range(TG):
                    last = nc.tensor.transpose(dst[:, t * D:(t + 1) * D], src(t), ident[:])
                return last

            def per_tile(srcT, weights, dst):
                for t in range(TG):
                    last = mm(dst[:, t * D:(t + 1) * D], srcT[:, t * D:(t + 1) * D], weights, start=True, stop=True)
                return last

            pe.wait_ge(S["proj_in"], 16)
            mm(bank[4][:, 0:HEADS], pw[:, D:2 * D], pw[:, 2 * D:2 * D + HEADS], start=True, stop=True).then_inc(S["wa_full"], 1)
            pe.wait_ge(S["wa_done"], 1)
            pe.wait_ge(S["c0_in"], 16)
            for g in range(NG):
                pe.wait_ge(S["xn0_ready"], g + 1)
                transposes(lambda t: xn_early[:, g % 2, t, :], bank[4]).then_inc(S["tr0_full"], 1)
                pe.wait_ge(S["hT0_ready"], g + 1)
                if g:
                    pe.wait_ge(S["xp_read"], g)
                for t in range(TG):
                    half, s = t // 2, (t % 2) * (D + HEADS)
                    last = mm(bank[5 + half][:, s:s + D + HEADS], hT_early[:, g % 2, t * D:(t + 1) * D], pwa,
                              start=True, stop=True)
                last.then_inc(S["xp_full"], 1)

            pe.wait_ge(S["wlo_ready"], 1)
            for it in range(NT):
                pe.wait_ge(S["conv_v"], 2 * (it + 1))
                pe.wait_ge(S["conv_s"], 2 * (it + 1))
                if it >= 2 * TG and it % TG == 0:
                    pe.wait_ge(S["acc_read"], it // TG - 1)
                for jt in range(NT):
                    if it == 0 and jt % TG == 0:
                        pe.wait_ge(S["op0_ready"], jt // TG + 1)
                    mm(bank[it % (2 * TG)][:, 0:HI], adj8[:, it, jt, :], op0[:, jt, 0:HI], start=(jt == 0), stop=False)
                    last = mm(bank[it % (2 * TG)][:, 0:LO], adj8[:, it, jt, :], op0[:, jt, HI:OPW], start=False,
                              stop=(jt == NT - 1))
                last.then_inc(S["acc_full"], 1)

            def split_transposes(src):
                for part in range(2):
                    for t in range(TG):
                        last = nc.tensor.transpose(tr16[:, part, t * D:(t + 1) * D], src(part, t), ident16[:])
                return last

            def rows_times(srcT, m, dst):
                for t in range(TG):
                    for part, other in ((0, 0), (0, 1), (1, 0)):
                        last = mm(tile(dst, t), srcT[:, part, t * D:(t + 1) * D], w16[:, other, m, :],
                                  start=(part + other == 0), stop=(part == 1))
                return last

            def matrix_times(m, srcT, dst, stop=True):
                for other, part in ((0, 0), (0, 1), (1, 0)):
                    last = mm(dst, w16[:, other, m, :], srcT[:, part, :], start=(part + other == 0), stop=(stop and other == 1))
                return last

            def own_transposes(s):
                c = s % NG
                if s == 0:
                    pe.wait_ge(S["w16_ready"], 1)
                hs = hs_a if s < NG else hs_b
                split_transposes(lambda part, t: hs[:, c * TG + t, part, :]).then_inc(S["pre_tr"], 1)

            def own_self(s):
                pe.wait_ge(S["pre_hT"], s + 1)
                if s:
                    pe.wait_ge(S["xnew_ready"], s + NG)
                else:
                    pe.wait_ge(S["w16_ready"], 1)
                rows_times(hT16, M_SELF, bank[4]).then_inc(S["l1_self"], 1)

            def neighbours(s):
                pe.wait_ge(S["aT_ready"], s + 1)
                rows_times(aT16, M_NEIGH, bank[3]).then_inc(S["l1_neigh"], 1)

            def hidden_gates(s):
                pe.wait_ge(S["pre_hT"], s + 1)
                if s > NG:
                    pe.wait_ge(S["rz_ready"], s - NG)
                    pe.wait_ge(S["x3_ready"], s - NG)
                    if s > NG + 1:
                        pe.wait_ge(S["p1_ready"], s - NG - 1)
                else:
                    pe.wait_ge(S["hs_ready"], 2 * NG)
                matrix_times(M_HR, hT16, bank[4], stop=False)
                matrix_times(M_HZ, hT16, bank[5], stop=False)
                matrix_times(M_HN, hT16, bank[7])

            def message(s):
                pe.wait_ge(S["aT_ready"], s + 1)
                if s > NG:
                    pe.wait_ge(S["t_ready"], s - NG)
                matrix_times(M_MSG, aT16, bank[6]).then_inc(S["msg_full"], 1)

            def message_gates(s):
                pe.wait_ge(S["msg_ready"], s - NG + 1)
                mm(bank[4], tile(w_ih, 0), msgT, start=False, stop=True)
                mm(bank[5], tile(w_ih, 1), msgT, start=False, stop=True)
                mm(bank[6], tile(w_ih, 2), msgT, start=True, stop=True).then_inc(S["gates_full"], 1)

            def update_back(s):
                pe.wait_ge(S["u_ready"], s - NG + 1)
                for t in range(TG):
                    last = nc.tensor.transpose(tile(bank[7], t), tile(zT, t), ident[:])
                last.then_inc(S["uT_full"], 1)

            def new_transposes(s):
                pe.wait_ge(S["row16_ready"], s - NG + 1)
                split_transposes(lambda part, t: row16[:, part, t, :]).then_inc(S["h3_tr"], 1)

            def embed(s):
                pe.wait_ge(S["h3T_ready"], s - NG + 1)
                if s > NG:
                    pe.wait_ge(S["z_ready"], s - NG)
                rows_times(h3T16, M_EMB, bank[3]).then_inc(S["emb_full"], 1)

            def own_part(s):
                if s > NG:
                    pe.wait_ge(S["p1_ready"], s - NG)
                if s + 1 < 2 * NG:
                    pe.wait_ge(S["rz_ready"], s - NG + 2)
                rows_times(h3T16, M_TOP, bank[4]).then_inc(S["top_full"], 1)

            def norms(s):
                pe.wait_ge(S["aT_ready"], s + 1)
                for t in range(TG):
                    last = mm(bank[5][:, t:t + 1], tile(msgT, t), ones_col, start=True, stop=True)
                last.then_inc(S["norms_full"], 1)

            def bottom(s):
                if s == 2 * NG:
                    pe.wait_ge(S["z_ready"], NG)
                rows_times(aT16, M_BOT, bank[3]).then_inc(S["p2_full"], 1)

            own = {1: {44: own_transposes, 56: own_self}, 2: {62: own_transposes}, 3: {}}
            after = {1: {8: neighbours},
                     2: {1: hidden_gates, 6: message, 11: message_gates},
                     3: {6: norms, 9: bottom}}
            late = {15: new_transposes, 26: embed, 32: own_part}
            back = {44: update_back}
            final = {36: update_back, 45: new_transposes, 46: embed, 47: own_part}

            pe.wait_ge(S["acc_read"], NG)
            pe.wait_ge(S["odd_ready"], 1)
            mm(bank[0][0:1, 0:1], odd, ones_col, start=True, stop=True).then_inc(S["odd_sum"], 1)
            pe.wait_ge(S["flag_ready"], 1)
            general = pe.value_load(flag, min_val=0, max_val=1)
            with pe.If(general > 0):
                turn = S["turn"]
                pe.wait_ge(turn, 1)
                mm(bank[0][:, 0:2 * HEADS], gw[:, D:2 * D], gw[:, 2 * D:2 * D + 2 * HEADS], start=True, stop=True).then_inc(turn, 1)
                with pe.Fori(0, NT) as i:
                    at = i * TURNS_ROWS + TURN_ROWS
                    pe.wait_ge(turn, at + 6)
                    nc.tensor.transpose(bank[0][:, 0:D], gxn, ident[:]).then_inc(turn, 1)
                    pe.wait_ge(turn, at + 9)
                    mm(bank[1][:, 0:D], tile(pT, 0), gw[:, 0:D], start=True, stop=True).then_inc(turn, 1)
                with pe.Fori(0, NT) as i:
                    at = i * TURNS_TILE + TURN_ATTEND
                    for c in range(CHUNKS):
                        pe.wait_ge(turn, at + (c * TURNS_MASK + 1))
                        for t in range(TG):
                            last = mm(tile(bank[0], t), a16[:, t * P:(t + 1) * P], ident16[:], start=True, stop=True)
                        last.then_inc(turn, 1)
                    for h in range(HEADS):
                        k = CHUNKS * TURNS_MASK + h * TURNS_HEAD
                        pe.wait_ge(turn, at + (k + 2))
                        mm(bank[1][:, 0:1], tile(pT, 0), wa[:, HEADS + h:HEADS + h + 1],
                           start=True, stop=True).then_inc(turn, 1)
                        for c in range(CHUNKS):
                            pe.wait_ge(turn, at + (k + 4 + c * TURNS_LOGITS))
                            mm(bank[2], wa_wide, hT_all[:, c * GW:(c + 1) * GW], start=True, stop=True).then_inc(turn, 1)
                        k += 4 + CHUNKS * TURNS_LOGITS + 5
                        for c in range(CHUNKS):
                            pe.wait_ge(turn, at + (k + c * TURNS_OUT))
                            transposes(lambda t: logits[:, (c * TG + t) * P:(c * TG + t + 1) * P], bank[3]).then_inc(turn, 1)
                            pe.wait_ge(turn, at + (k + c * TURNS_OUT + 2))
                            for t in range(TG):
                                last = mm(bank[4][:, 0:HD], tile(pT, t), xp[:, c * TG + t, h * HD:(h + 1) * HD],
                                          start=(t == 0), stop=(t == TG - 1))
                            last.then_inc(turn, 1)
                pe.wait_ge(turn, TURN_END + 1)
            for s in range(3 * NG):
                layer, c = s // NG + 1, s % NG
                hs = hs_b if layer == 2 else hs_a
                if s >= 2:
                    pe.wait_ge(S["aT_ready"], s - 1)
                dst = agg[:, s % 2, :].rearrange("p (a b) -> p a b", a=TG)
                for k in range(2 * NT):
                    jt, part = k // 2, k % 2
                    if k and s and k in after[(s - 1) // NG + 1]:
                        after[(s - 1) // NG + 1][k](s - 1)
                    if k in late and NG <= s - 2 < 2 * NG - 1:
                        late[k](s - 2)
                    if k in back and NG <= s - 1 < 2 * NG - 1:
                        back[k](s - 1)
                    if k in final and s == 2 * NG:
                        final[k](s - 1)
                    if k in own[layer]:
                        own[layer][k](s)
                    if c == 0 and jt % TG == 0 and part == 0:
                        pe.wait_ge(S["hs_ready"], (layer - 1) * NG + jt // TG + 1)
                    last = mm(dst, hs[:, jt, part, :], adj8[:, c * TG:(c + 1) * TG, jt, :],
                              start=(k == 0), stop=(k == 2 * NT - 1))
                last.then_inc(S["agg_full"], 1)
            for k in after[3]:
                after[3][k](3 * NG - 1)


def kernel(**inputs):
    import numpy as _np
    import concourse.bacc as _bacc
    from concourse import mybir as _mybir
    from concourse.bass_utils import run_bass_kernel_spmd as _run

    g = {k: _np.asarray(v) for k, v in inputs.items()}
    f = _np.float32
    rows = lambda b: _np.broadcast_to(b[None, :], (P, D))
    blocks = _np.zeros((D, 2 * HEADS), f)
    for h in range(HEADS):
        blocks[h * HD:(h + 1) * HD, h] = g["L0_gnn_a"][:HD]
        blocks[h * HD:(h + 1) * HD, HEADS + h] = g["L0_gnn_a"][HD:]
    arrays = {
        "x_rows": g["x"].reshape(NT, P, D).transpose(1, 0, 2),
        "adj_pieces": g["adj"].reshape(NT, P, 2, PIECE_T, P).transpose(0, 2, 4, 3, 1).reshape(NPIECE, P, PIECE),
        "proj": _np.concatenate([g["L0_gnn_W"], g["L0_gnn_W"].T, blocks], axis=1),
        "consts0": _np.eye(P, dtype=f),
        "matrices": _np.concatenate([
            g["L1_gnn_W_self"], g["L1_gnn_W_neigh"], g["L2_gnn_W_msg"].T, g["L2_gnn_W_hh"].T, g["L3_gnn_embed"],
            g["L3_gnn_layer"][:D], g["L3_gnn_layer"][D:], g["L2_gnn_W_ih"].T], axis=1),
        "vectors": _np.concatenate([
            rows(g["L3_gnn_embed_bias"]), rows(g["L3_gnn_layer_bias"]), g["L2_gnn_b_msg"][:, None],
            g["L2_gnn_b_ih"].reshape(3, D).T, g["L2_gnn_b_hh"].reshape(3, D).T, _np.zeros((P, 1), f)], axis=1),
    }
    arrays = {k: _np.ascontiguousarray(a) for k, a in arrays.items()}
    nc = _bacc.Bacc("TRN2", target_bir_lowering=False, num_devices=1)
    args = [nc.dram_tensor(k, a.shape, _mybir.dt.from_np(a.dtype), kind="ExternalInput").ap() for k, a in arrays.items()]
    p1 = nc.dram_tensor("p1_rows", (P, NT, D), _mybir.dt.float32, kind="Internal").ap()
    out = nc.dram_tensor("out_rows", (P, NT, D), _mybir.dt.float32, kind="ExternalOutput").ap()
    build_graph_stack(nc, *args, p1, out)
    r = _run(nc, [arrays], core_ids=[0])
    return r.results[0]["out_rows"].transpose(1, 0, 2).reshape(N, D)
```

```python
import concourse.bass as bass
from concourse import mybir
from contextlib import ExitStack


P = 128
N = 4096
D = 128
NT = N // P
TG = 4
NG = NT // TG
GW = TG * P
HEADS = 4
HD = D // HEADS
SPLIT = 1024.0
EPS_LN = 1e-5
EPS_BALL = 1e-7
MAX_TANH = 1.0 - 1e-6
SERIES_BELOW = 0.25
WIDE_SPREAD = 8.0

PIECE_T = NT // 2
PIECE = PIECE_T * P
NPIECE = 2 * NT
NBUF = 3
DVE_PART = PIECE // 2
ONE_FP8 = float(0x38)
PIECES_STATS, PIECES_PROJ, PIECES_SPLIT, PIECES_MAIN = 1, 1, 1, 5
PIECES_WEIGHTS = 2
FIRST_SPLIT = NG * (PIECES_STATS + PIECES_PROJ) + PIECES_WEIGHTS
FIRST_MAIN = FIRST_SPLIT + NG * PIECES_SPLIT

HI = D + HEADS + 1
LO = D + HEADS
OPW = HI + LO

CHUNKS = N // GW
TURNS_START, TURNS_ROWS, TURNS_MASK, TURNS_LOGITS, TURNS_OUT, TURNS_OPERAND = 3, 11, 3, 3, 4, 7
TURNS_HEAD = 4 + TURNS_LOGITS * CHUNKS + 5 + TURNS_OUT * CHUNKS + 1
TURNS_TILE = TURNS_MASK * CHUNKS + HEADS * TURNS_HEAD
TURN_ROWS = TURNS_START
TURN_ATTEND = TURN_ROWS + TURNS_ROWS * NT
TURN_OPERAND = TURN_ATTEND + TURNS_TILE * NT
TURN_END = TURN_OPERAND + TURNS_OPERAND * NT
MASKED = 1e9

M_SELF, M_NEIGH, M_MSG, M_HR, M_HZ, M_HN, M_EMB, M_TOP, M_BOT = range(9)
NM = 9
M_IH = NM
N_RAW = (NM + 3) * D
R_EMB, R_LAY = 0, D
R_COL = 2 * D
N_ROWS = R_COL + 8
W_TOP = 4096.0


def build_graph_stack(nc, x_rows, adj_pieces, proj, consts0, matrices, vectors, p1_rows, out_rows):
    fp32, fp16, u8, u32 = mybir.dt.float32, mybir.dt.float16, mybir.dt.uint8, mybir.dt.uint32
    fp8 = mybir.dt.float8e4
    ALU = mybir.AluOpType
    ACT = mybir.ActivationFunctionType
    AX = mybir.AxisListType
    import math
    SCALE = 1.0 / math.sqrt(HD)

    with ExitStack() as ctx:
        def sb(name, shape, dt):
            return ctx.enter_context(nc.sbuf_tensor(name, shape, dt))

        def sem(name):
            return ctx.enter_context(nc.semaphore(name))

        adj = sb("adj", [P, NT, NT, P], u8)
        x = sb("x", [P, NT, D], fp32)
        hs_a = sb("hs_a", [P, NT, 2, D], fp16)
        region_op = sb("region_op", [P, NT * OPW], fp16)
        region_st = sb("region_st", [P, NBUF * PIECE], fp32)
        ident = sb("ident", [P, D], fp32)
        ident16 = sb("ident16", [P, D], fp16)
        rowbuf = sb("rowbuf", [P, TG * HI], fp32)
        hT = sb("hT", [P, GW], fp32)
        w = sb("w", [P, NT, HEADS], fp32)
        deg = sb("deg", [P, NT], fp32)
        mv = sb("mv", [P, TG, 2], fp32)
        mean = sb("mean", [P, NT], fp32)
        ssh = sb("ssh", [P, NT], fp32)
        rs = sb("rs", [P, NT], fp32)
        small = sb("small", [P, 80 + D + 44], fp32)

        xp = hs_a[:].rearrange("p t a d -> p (t a d)").bitcast(fp32).rearrange("p (t d) -> p t d", d=D)
        op0 = region_op[:].rearrange("p (t c) -> p t c", c=OPW)
        hs_b = region_op[:, 0:NT * 2 * D].rearrange("p (t a d) -> p t a d", a=2, d=D)
        early = region_op[:, 0:NT * OPW].bitcast(fp32)
        pw = early[:, 0:2 * D + 2 * HEADS]
        pwa = early[:, 2 * D + 2 * HEADS:3 * D + 3 * HEADS]
        E0 = 3 * D + 3 * HEADS
        xn_early = early[:, E0:E0 + 2 * GW].rearrange("p (b t d) -> p b t d", b=2, t=TG)
        hT_early = early[:, E0 + 2 * GW:E0 + 4 * GW].rearrange("p (b n) -> p b n", b=2)
        stage = region_st[:].rearrange("p (b n) -> p b n", b=NBUF)
        numden = rowbuf[:].rearrange("p (t c) -> p t c", c=HI)
        xn = rowbuf[:, 0:GW].rearrange("p (t d) -> p t d", d=D)
        at = [0]

        def take_words(n):
            at[0] += n
            return region_st[:, at[0] - n:at[0]]

        w_ih = take_words(3 * D)
        vec = take_words(N_ROWS)
        w16 = take_words(NM * D).bitcast(fp16).rearrange("p (a m d) -> p a m d", a=2, m=NM)
        scr = take_words(240)
        work0 = at[0]

        def work():
            return take_words(GW)

        aT16, msgT, rT, zT, dT, row16, h3T16, z_rows = [work() for _ in range(8)]
        raw0 = ((NPIECE - 1) % NBUF + 1) * PIECE
        raw = region_st[:, raw0:raw0 + N_RAW].rearrange("p (m d) -> p m d", d=D)
        magnitude = region_st[:, raw0 + N_RAW:raw0 + N_RAW + NM * D].rearrange("p (m d) -> p m d", d=D)
        aT16 = aT16.bitcast(fp16).rearrange("p (a n) -> p a n", a=2)
        hT16 = hT[:].bitcast(fp16).rearrange("p (a n) -> p a n", a=2)
        h3T16 = h3T16.bitcast(fp16).rearrange("p (a n) -> p a n", a=2)
        row16 = row16.bitcast(fp16).rearrange("p (a t d) -> p a t d", a=2, t=TG)
        p1_sb = rowbuf[:, 0:GW]
        p1_in = region_st[:, work0 + 2 * GW:work0 + 4 * GW]
        junk = w[:].rearrange("p t h -> p (t h)")
        junk8 = junk.bitcast(u8)
        b3e, b3l = vec[:, R_EMB:R_EMB + D], vec[:, R_LAY:R_LAY + D]
        b_msg = vec[:, R_COL:R_COL + 1]
        b_ih, b_hh = vec[:, R_COL + 1:R_COL + 4], vec[:, R_COL + 4:R_COL + 7]

        def col4(i):
            return scr[:, 4 * i:4 * i + 4]

        def tiles(v):
            return v.rearrange("p (t d) -> p t d", d=D)

        def tile(v, t):
            return v[:, t * D:(t + 1) * D]

        (NRM, CL, LNP, LNM, PP, SER, MASK, AT, KAP) = range(0, 18, 2)
        (NE_Z, NE_H, SSH, SSE, DOT, NE_E, N2, TH, ALF, XY, X2, TT, NUM, DEN, CA, CB, SSZ, SSA, BETA, SSC,
         COEF) = range(18, 39)
        N2A, THA = 53, 54
        Z_ONLY, H_ONLY, BOTH = (0, 1), (1, 2), (0, 2)

        def pair(i, part):
            return scr[:, 4 * (i + part[0]):4 * (i + part[1])]

        dve_junk = small[:, 80:208].bitcast(u8)
        STEPS_2, STEPS_3 = 59, 49
        y2e, y2l, brz, b_hn = scr[:, 158:159], scr[:, 159:160], scr[:, 160:162], scr[:, 162:163]
        w_scale, w_unscale = scr[:, 172:181], scr[:, 181:190]
        w_unsplit = scr[:, 190:199]
        ih_scale = scr[:, 208:210]

        mhalf, phalf = small[:, 4:8], small[:, 8:12]
        top, topall = small[:, 232:241], small[:, 241:250]
        ext, extall = small[:, 211:220], small[:, 220:229]
        shift = small[:, 28:32]
        rden = small[:, 32:48]
        ones_col = small[:, 48:49]
        odd, wide = small[:, 208:209], small[:, 209:210]
        flag = small[0:1, 210:211].bitcast(mybir.dt.int32)
        st = small[:, 52:76].rearrange("p (t s) -> p t s", s=6)

        logits = early[:, 0:N]
        outs = early[:, N:N + HD]
        hT_all = region_st[:, 0:N]
        gen = region_st[:, N:]
        gw, wa = gen[:, 0:2 * D + 2 * HEADS], gen[:, 264:272]
        gmv, gst, grs = gen[:, 272:274], gen[:, 274:280], gen[:, 280:281]
        s_dst, gmax, gden = gen[:, 281:282], gen[:, 282:283], gen[:, 283:284]
        missing = gen[:, 288:288 + N // 4].bitcast(u8)
        pT = rowbuf[:, 0:GW]
        a16, gxn, wa_wide = hT[:, 0:GW // 2].bitcast(fp16), hT[:, GW // 2:GW // 2 + D], hT[:, GW // 2 + D:GW]

        acc = ctx.enter_context(nc.psum_tensor("acc", [P, 8, GW], fp32))
        agg = acc[:, 0:2, :]
        bank = [acc[:, i, :] for i in range(8)]
        tr16 = bank[2].bitcast(fp16).rearrange("p (a n) -> p a n", a=2)

        S = {n: sem(n) for n in (
            "x_in", "proj_in", "c0_in", "c1_in", "c2_in", "landed", "conv_v", "conv_s",
            "consts_set", "dve_step",
            "ve_ready", "rs_ready", "wa_full", "wa_done", "xn0_ready", "tr0_full", "hT0_ready", "xp_full", "xp_read",
            "ext_ready", "extall_ready", "shift_ready", "w_ready", "whi_ready", "wlo_ready", "y_ready", "hi0_ready", "op0_ready",
            "acc_full", "acc_read", "xnew_ready", "hi_ready", "hs_ready",
            "top_ready", "topall_ready", "w16_ready", "odd_ready", "odd_sum", "flag_ready", "turn", "gen_in",
            "pre_tr", "pre_hT", "agg_full", "aThi_ready", "aT_ready", "l1_self", "l1_neigh",
            "msg_full", "msg_ready", "gates_full", "rz_ready", "t_ready", "n_ready", "u_ready", "uT_full",
            "relu_ready", "row16hi_ready", "row16_ready", "ssh_ready", "x3_ready", "h3_tr", "h3T_ready", "emb_full", "top_full", "p1_ready", "p1_out", "p1_in",
            "nrmh_ready", "nrme_ready", "nrmz_ready", "sqe_ready", "sqz_ready", "ln_in", "ln_out", "th_in", "th_out", "tha_in", "tha_out",
            "z_ready", "coef_ready", "zs_ready", "bhi_ready", "norms_full", "ssa_ready", "ssc_ready", "p2_full", "v_ready",
            "x4_ready", "out_done")}
        landing = [sem(f"landing{b}") for b in range(NBUF)]

        block = ctx.enter_context(nc.Block())

        def tile_of(g, t):
            return bass.ds(g * TG + t, 1)

        def group_of(g):
            return bass.ds(g * TG, TG)

        class Steps:

            def __init__(self, eng, s):
                self.eng, self.s, self.base, self.g, self.per, self.k = eng, s, 0, 0, 0, 0

            def loop(self, g, per):
                self.g, self.per, self.k = g, per, 0

            def end(self, trips):
                assert self.k == self.per, (self.k, self.per)
                self.base += trips * self.per
                self.g, self.per, self.k = 0, 0, 0

            def step(self, ins):
                ins.then_inc(self.s, 1)
                self.k += 1
                if not self.per:
                    self.base, self.k = self.base + 1, 0

            def settle(self):
                self.eng.wait_ge(self.s, self.base + self.g * self.per + self.k)

            def link(self, ins):
                self.step(ins)
                self.settle()

        @block.sync
        def _(sp):
            sp.dma_start(x[:], x_rows).then_inc(S["x_in"], 16)
            sp.dma_start(pw, proj).then_inc(S["proj_in"], 16)
            sp.dma_start(ident[:], consts0).then_inc(S["c0_in"], 16)
            for n in range(NBUF):
                sp.dma_start(stage[:, n, :], adj_pieces[n]).then_inc(landing[n], 16)
            sp.wait_ge(landing[0], 16)
            sp.sem_inc(S["landed"], 1)

            def relay_and_refill(r, n_of, b):
                nxt = (b + 1) % NBUF
                sp.wait_ge(landing[nxt], 16 * r + (32 if nxt == 0 else 16))
                sp.sem_inc(S["landed"], 1)
                sp.wait_ge(S["conv_v"], n_of + 1)
                sp.wait_ge(S["conv_s"], n_of + 1)
                sp.dma_start(stage[:, b, :], adj_pieces[bass.ds(n_of + NBUF, 1)].rearrange("a p n -> p (a n)")
                             if not isinstance(n_of, int) else adj_pieces[n_of + NBUF]).then_inc(landing[b], 16)

            rounds = (NPIECE - NBUF) // NBUF
            with sp.Fori(0, rounds) as r:
                for b in range(NBUF):
                    relay_and_refill(r, r * NBUF + b, b)
            for n in range(rounds * NBUF, NPIECE - NBUF):
                relay_and_refill(n // NBUF, n, n % NBUF)
            for n in range(NPIECE - NBUF + 1, NPIECE):
                sp.wait_ge(landing[n % NBUF], 16 * (n // NBUF + 1))
                sp.sem_inc(S["landed"], 1)
            sp.wait_ge(S["conv_v"], NPIECE - 1)
            sp.wait_ge(S["conv_s"], NPIECE - 1)
            sp.dma_start(raw.rearrange("p m d -> p (m d)"), matrices).then_inc(S["c1_in"], 16)
            sp.wait_ge(S["conv_v"], NPIECE)
            sp.wait_ge(S["conv_s"], NPIECE)
            sp.dma_start(vec, vectors).then_inc(S["c2_in"], 16)
            sp.wait_ge(S["flag_ready"], 1)
            general = sp.value_load(flag, min_val=0, max_val=1)
            with sp.If(general > 0):
                sp.wait_ge(S["c1_in"], 16)
                sp.wait_ge(S["c2_in"], 16)
                sp.dma_start(x[:], x_rows).then_inc(S["gen_in"], 16)
                sp.dma_start(gw, proj).then_inc(S["gen_in"], 16)
                sp.wait_ge(S["gen_in"], 32)
                sp.sem_inc(S["turn"], 1)
                sp.wait_ge(S["turn"], TURN_END)
                sp.dma_start(raw.rearrange("p m d -> p (m d)"), matrices).then_inc(S["gen_in"], 16)
                sp.dma_start(vec, vectors).then_inc(S["gen_in"], 16)
                sp.wait_ge(S["gen_in"], 64)
                sp.sem_inc(S["turn"], 1)
            sp.sem_inc(S["p1_out"], 16)
            with sp.Fori(0, NG) as g:
                sp.wait_ge(S["p1_ready"], g + 1)
                sp.dma_start(p1_rows[:, group_of(g), :], tiles(p1_sb)).then_inc(S["p1_out"], 16)
            sp.wait_ge(S["p1_out"], 16 * NG + 16)
            sp.wait_ge(S["uT_full"], NG)

            def fetch_p1(g):
                buf = p1_in[:, bass.ds(g % 2 * GW, GW)] if not isinstance(g, int) else p1_in[:, g % 2 * GW:(g % 2 + 1) * GW]
                sp.dma_start(tiles(buf), p1_rows[:, group_of(g), :]).then_inc(S["p1_in"], 16)

            def store(g):
                sp.wait_ge(S["x4_ready"], g + 1)
                sp.dma_start(out_rows[:, group_of(g), :], x[:, group_of(g), :]).then_inc(S["out_done"], 16)

            fetch_p1(0)
            sp.wait_ge(S["p1_in"], 16)
            fetch_p1(1)
            with sp.Fori(0, NG - 2) as g:
                store(g)
                sp.wait_ge(S["p1_in"], g * 16 + 32)
                fetch_p1(g + 2)
            store(NG - 2)
            store(NG - 1)
            sp.wait_ge(S["out_done"], 16 * NG)

        @block.vector
        def _(dve):
            v = nc.vector
            me = Steps(dve, S["dve_step"])

            def copy(dst, src):
                return v.tensor_scalar(dst, src, 1.0, None, ALU.mult)

            def convert(n):
                dve.wait_ge(S["landed"], n + 1)
                adj_flat = adj[:].rearrange("p i j n -> p (i j n)")
                src = region_st[:, bass.ds((n % NBUF) * PIECE, DVE_PART)]
                v.tensor_scalar(adj_flat[:, bass.ds(n * PIECE, DVE_PART)], src, ONE_FP8, None, ALU.mult).then_inc(S["conv_v"], 1)

            def anchor():
                v.memset(small[:, 50:51], 0.0)

            def statistics(g):
                anchor()
                for t in range(TG):
                    me.step(v.bn_stats(st[:, t, :], x[:, tile_of(g, t), :].rearrange("p a d -> p (a d)")))
                me.settle()
                anchor()
                for t in range(TG):
                    me.step(v.bn_aggr(mv[:, t, :], st[:, t, :]))
                me.settle()
                me.step(copy(mean[:, group_of(g)].rearrange("p (t a) -> p t a", a=1), mv[:, :, 0:1]))
                v.tensor_scalar(rs[:, group_of(g)].rearrange("p (t a) -> p t a", a=1), mv[:, :, 1:2], EPS_LN,
                                1.0 / SPLIT ** 2, ALU.add, ALU.mult).then_inc(S["ve_ready"], 1)

            def normalised(g, dst, steps=True):
                for t in range(TG):
                    last = v.tensor_scalar(dst(t), x[:, tile_of(g, t), :].rearrange("p a d -> p (a d)"),
                                           mean[:, tile_of(g, t)],
                                           rs[:, tile_of(g, t)], ALU.subtract, ALU.mult)
                    if steps and t < TG - 1:
                        me.step(last)
                return last

            dve.wait_ge(S["c0_in"], 16)
            copy(ident16[:], ident[:])
            v.memset(mhalf, -0.5)
            v.memset(ones_col, 1.0)
            me.link(v.memset(phalf, 0.5))
            v.memset(small[:, 49:50], 0.0).then_inc(S["consts_set"], 1)
            dve.wait_ge(S["proj_in"], 16)
            me.step(copy(pwa[:, 0:D], pw[:, 0:D]))
            me.step(v.tensor_tensor_reduce(out=junk, in0=pw[:, D:2 * D], in1=pw[:, D:2 * D], scale=1.0, scalar=0.0,
                                           op0=ALU.mult, op1=ALU.add, accum_out=ext[:, 8:9]))
            dve.wait_ge(S["wa_full"], 1)
            copy(pwa[:, D:D + HEADS], bank[4][:, 0:HEADS]).then_inc(S["wa_done"], 1)
            dve.wait_ge(S["x_in"], 16)

            with dve.Fori(0, NG) as g:
                me.loop(g, 2 * TG + 1)
                statistics(g)
                convert(g)
            me.end(NG)

            dve.wait_ge(S["rs_ready"], NG)

            def early_rows(g):
                normalised(g, lambda t: xn_early[:, bass.ds(g % 2, 1), t, :].rearrange("p a d -> p (a d)")
                           if not isinstance(g, int) else xn_early[:, g % 2, t, :], steps=False).then_inc(S["xn0_ready"], 1)

            early_rows(0)
            with dve.Fori(1, NG) as g:
                convert(g + NG * PIECES_STATS - 1)
                dve.wait_ge(S["tr0_full"], g)
                early_rows(g)
            convert(NG * (PIECES_STATS + PIECES_PROJ) - 1)
            dve.wait_ge(S["xp_read"], NG)
            me.step(v.tensor_reduce(ext[:, 0:4], w[:].rearrange("p t h -> p h t"), AX.X, ALU.max))
            me.link(v.tensor_reduce(ext[:, 4:8], w[:].rearrange("p t h -> p h t"), AX.X, ALU.min))
            v.tensor_scalar(ext[:, 4:8], ext[:, 4:8], -1.0, None, ALU.mult).then_inc(S["ext_ready"], 1)
            convert(FIRST_SPLIT - 2)
            dve.wait_ge(S["extall_ready"], 1)
            me.link(v.tensor_tensor(rden[:, 0:4], extall[:, 0:4], extall[:, 4:8], ALU.add))
            me.link(v.tensor_reduce(wide, rden[:, 0:4], AX.X, ALU.max))
            me.link(v.tensor_scalar(wide, wide, WIDE_SPREAD / SCALE, None, ALU.is_gt))
            me.link(v.tensor_scalar(rden[:, 4:5], extall[:, 8:9], (60000.0 / SPLIT) ** 2 / D, None, ALU.is_gt))
            me.step(v.tensor_tensor(wide, wide, rden[:, 4:5], ALU.max))
            v.tensor_scalar(shift, extall[:, 0:4], -SCALE, math.log(SPLIT), ALU.mult, ALU.add).then_inc(S["shift_ready"], 1)

            convert(FIRST_SPLIT - 1)
            dve.wait_ge(S["w_ready"], HEADS)
            me.step(v.memset(op0[:, :, D + HEADS:HI], 1.0))
            dve.wait_ge(S["whi_ready"], 1)
            v.tensor_tensor(op0[:, :, HI + D:OPW], w[:], op0[:, :, D:D + HEADS], ALU.subtract).then_inc(S["wlo_ready"], 1)
            with dve.Fori(0, NG) as g:
                y = xp[:, group_of(g), :]
                yh = y.rearrange("p t (h d) -> p (t h) d", d=HD)
                wb = w[:, group_of(g), :].rearrange("p t h -> p (t h)")
                wb = wb.rearrange("p (c a) -> p c a", a=1).to_broadcast([P, TG * HEADS, HD])
                v.tensor_tensor(yh, yh, wb, ALU.mult).then_inc(S["y_ready"], 1)
                convert(g + FIRST_SPLIT)
                dve.wait_ge(S["y_ready"], g + 1)
                dve.wait_ge(S["hi0_ready"], g + 1)
                v.tensor_tensor(op0[:, group_of(g), HI:HI + D], y, op0[:, group_of(g), 0:D],
                                ALU.subtract).then_inc(S["op0_ready"], 1)

            def attend(g, n, prev):
                last = isinstance(g, int) and g == NG - 1
                for i in range(NPIECE - n if last else 3):
                    convert(n + i)
                    if i == 1 and prev is not None:
                        low_operand(prev, 0, xn, hs_a)
                if last:
                    dve.wait_ge(S["c1_in"], 16)
                    me.link(v.tensor_scalar(magnitude.bitcast(u32), raw[:, 0:NM, :].bitcast(u32), 0x7FFFFFFF, None, ALU.bitwise_and))
                    v.tensor_reduce(top, magnitude, AX.X, ALU.max).then_inc(S["top_ready"], 1)
                dve.wait_ge(S["acc_full"], (g + 1) * TG)
                sums = acc[:, bass.ds(g % 2 * TG, TG), :] if not isinstance(g, int) else acc[:, g % 2 * TG:(g % 2 + 1) * TG, :]
                me.step(v.tensor_scalar(deg[:, group_of(g)].rearrange("p (t a) -> p t a", a=1), sums[:, :, D + HEADS:HI],
                                        1.0, None, ALU.mult))
                me.link(v.tensor_scalar(rden.rearrange("p (t h) -> p t h", h=HEADS), sums[:, :, D:D + HEADS],
                                        1e-12, None, ALU.max))
                me.link(v.reciprocal(rden, rden))
                num = sums[:, :, 0:D].rearrange("p t (h d) -> p t h d", d=HD)
                rb = rden.rearrange("p (t h a) -> p t h a", h=HEADS, a=1).to_broadcast([P, TG, HEADS, HD])
                v.tensor_tensor(xn.rearrange("p t (h d) -> p t h d", d=HD), num, rb, ALU.mult).then_inc(S["acc_read"], 1)
                if not last:
                    convert(n + 3)
                dve.wait_ge(S["acc_read"], g + 1)
                me.link(v.tensor_tensor(x[:, group_of(g), :], x[:, group_of(g), :], xn, ALU.add))
                statistics(g)
                if not last:
                    convert(n + 4)
                high_operand(g, 0, xn)
                if last:
                    low_operand(g, 0, xn, hs_a)

            def high_operand(g, count, xnew):
                dve.wait_ge(S["rs_ready"], g + NG + count + 1)
                normalised(g, lambda t: xnew[:, t, :]).then_inc(S["xnew_ready"], 1)

            def low_operand(g, count, xnew, hs):
                dve.wait_ge(S["hi_ready"], g + count + 1)
                dve.wait_ge(S["xnew_ready"], g + count + 1)
                v.scalar_tensor_tensor(hs[:, group_of(g), 1, :], xnew, 0.0, hs[:, group_of(g), 0, :],
                                       ALU.max, ALU.subtract).then_inc(S["hs_ready"], 1)
                dve.wait_ge(S["hs_ready"], g + count + 1)

            attend(0, FIRST_MAIN, None)
            with dve.Fori(1, NG - 1) as g:
                me.loop(g - 1, 4 + 2 * TG + 1 + TG - 1)
                attend(g, g * PIECES_MAIN + FIRST_MAIN, g - 1)
            me.end(NG - 2)
            attend(NG - 1, (NG - 1) * PIECES_MAIN + FIRST_MAIN, NG - 2)

            def general_attention():
                turn = S["turn"]

                def row_of(v3, i):
                    return v3[:, bass.ds(i, 1), :].rearrange("p a d -> p (a d)")

                def tile_statistics(i, at, scale):
                    dve.wait_ge(turn, at)
                    anchor()
                    v.bn_stats(gst, row_of(x, i)).then_inc(turn, 1)
                    dve.wait_ge(turn, at + 1)
                    anchor()
                    v.bn_aggr(gmv, gst).then_inc(turn, 1)
                    dve.wait_ge(turn, at + 2)
                    v.tensor_scalar(grs, gmv[:, 1:2], EPS_LN, scale, ALU.add, ALU.mult).then_inc(turn, 1)
                    dve.wait_ge(turn, at + 4)
                    v.tensor_scalar(gxn, row_of(x, i), gmv[:, 0:1], grs, ALU.subtract, ALU.mult).then_inc(turn, 1)

                dve.wait_ge(turn, 2)
                copy(wa, bank[0][:, 0:2 * HEADS]).then_inc(turn, 1)
                with dve.Fori(0, NT) as i:
                    at = i * TURNS_ROWS + TURN_ROWS
                    tile_statistics(i, at, 1.0)
                    dve.wait_ge(turn, at + 5)
                    v.tensor_scalar(gxn, gxn, 0.0, None, ALU.max).then_inc(turn, 1)
                    dve.wait_ge(turn, at + 7)
                    copy(tile(pT, 0), bank[0][:, 0:D]).then_inc(turn, 1)
                    dve.wait_ge(turn, at + 8)
                    copy(hT_all[:, bass.ds(i * D, D)], tile(pT, 0)).then_inc(turn, 1)
                    dve.wait_ge(turn, at + 10)
                    copy(row_of(xp, i), bank[1][:, 0:D]).then_inc(turn, 1)
                with dve.Fori(0, NT) as i:
                    at = i * TURNS_TILE + TURN_ATTEND
                    for c in range(CHUNKS):
                        k = at + c * TURNS_MASK
                        dve.wait_ge(turn, k)
                        src = adj[:, bass.ds(i, 1), c * TG:(c + 1) * TG, :].rearrange("p a j n -> p (a j n)")
                        v.tensor_scalar(a16, src, 1.0 / ONE_FP8, None, ALU.mult).then_inc(turn, 1)
                        dve.wait_ge(turn, k + 2)
                        v.tensor_scalar(missing[:, c * GW:(c + 1) * GW], bank[0], -1.0, 1.0, ALU.mult,
                                        ALU.add).then_inc(turn, 1)
                    for h in range(HEADS):
                        k = at + (CHUNKS * TURNS_MASK + h * TURNS_HEAD)
                        dve.wait_ge(turn, k)
                        copy(wa_wide, wa[:, h:h + 1].to_broadcast([P, D])).then_inc(turn, 1)
                        dve.wait_ge(turn, k + 1)
                        copy(tile(pT, 0), hT_all[:, bass.ds(i * D, D)]).then_inc(turn, 1)
                        dve.wait_ge(turn, k + 3)
                        copy(s_dst, bank[1][:, 0:1]).then_inc(turn, 1)
                        for c in range(CHUNKS):
                            kc = k + (4 + c * TURNS_LOGITS)
                            lc = logits[:, c * GW:(c + 1) * GW]
                            dve.wait_ge(turn, kc + 1)
                            v.tensor_scalar(lc, bank[2], s_dst, SCALE, ALU.add, ALU.mult).then_inc(turn, 1)
                            dve.wait_ge(turn, kc + 2)
                            v.scalar_tensor_tensor(lc, missing[:, c * GW:(c + 1) * GW], -MASKED, lc, ALU.mult,
                                                   ALU.add).then_inc(turn, 1)
                        k = k + (4 + CHUNKS * TURNS_LOGITS)
                        dve.wait_ge(turn, k)
                        v.tensor_reduce(gmax, logits, AX.X, ALU.max).then_inc(turn, 1)
                        dve.wait_ge(turn, k + 1)
                        v.tensor_scalar(gmax, gmax, -1.0, None, ALU.mult).then_inc(turn, 1)
                        dve.wait_ge(turn, k + 3)
                        v.reciprocal(gden, gden).then_inc(turn, 1)
                        dve.wait_ge(turn, k + 4)
                        v.memset(outs, 0.0).then_inc(turn, 1)
                        for c in range(CHUNKS):
                            kc = k + (5 + c * TURNS_OUT)
                            dve.wait_ge(turn, kc + 1)
                            copy(pT, bank[3]).then_inc(turn, 1)
                            dve.wait_ge(turn, kc + 3)
                            v.tensor_tensor(outs, outs, bank[4][:, 0:HD], ALU.add).then_inc(turn, 1)
                        dve.wait_ge(turn, k + (5 + CHUNKS * TURNS_OUT))
                        xh = x[:, bass.ds(i, 1), h * HD:(h + 1) * HD].rearrange("p a d -> p (a d)")
                        v.scalar_tensor_tensor(xh, outs, gden, xh, ALU.mult, ALU.add).then_inc(turn, 1)
                with dve.Fori(0, NT) as i:
                    at = i * TURNS_OPERAND + TURN_OPERAND
                    tile_statistics(i, at, 1.0 / SPLIT ** 2)
                    hi = hs_a[:, bass.ds(i, 1), 0, :].rearrange("p a d -> p (a d)")
                    lo = hs_a[:, bass.ds(i, 1), 1, :].rearrange("p a d -> p (a d)")
                    dve.wait_ge(turn, at + 5)
                    v.tensor_scalar(hi, gxn, 0.0, None, ALU.max).then_inc(turn, 1)
                    dve.wait_ge(turn, at + 6)
                    v.scalar_tensor_tensor(lo, gxn, 0.0, hi, ALU.max, ALU.subtract).then_inc(turn, 1)
                dve.wait_ge(turn, TURN_END + 1)

            me.link(v.tensor_reduce(odd, deg[:], AX.X, ALU.min))
            me.link(v.tensor_scalar(odd, odd, 0.5, None, ALU.is_lt))
            v.tensor_tensor(odd, odd, wide, ALU.max).then_inc(S["odd_ready"], 1)
            dve.wait_ge(S["odd_sum"], 1)
            v.tensor_scalar(flag, bank[4][0:1, 0:1], 0.5, None, ALU.is_gt).then_inc(S["flag_ready"], 1)
            dve.wait_ge(S["flag_ready"], 1)
            general = dve.value_load(flag, min_val=0, max_val=1)
            with dve.If(general > 0):
                general_attention()

            dve.wait_ge(S["c2_in"], 16)
            me.step(v.tensor_scalar(deg[:], deg[:], 1.0, None, ALU.max))
            dve.wait_ge(S["topall_ready"], 1)
            me.link(v.tensor_scalar(topall, topall, 1e-30, 1.0 / W_TOP, ALU.max, ALU.mult))
            me.link(v.reciprocal(w_scale, topall))
            for m in range(NM):
                me.step(v.tensor_scalar(raw[:, m, :], raw[:, m, :], w_scale[:, m:m + 1], None, ALU.mult))
            me.settle()
            me.link(copy(w16[:, 0, :, :], raw[:, 0:NM, :]))
            me.step(v.tensor_tensor(w16[:, 1, :, :], raw[:, 0:NM, :], w16[:, 0, :, :], ALU.subtract))
            me.step(v.tensor_scalar(w_unsplit, topall, 1.0 / SPLIT, None, ALU.mult))
            me.step(copy(w_unscale, topall))
            me.step(v.tensor_scalar(ih_scale, w_scale[:, M_HR:M_HZ + 1], SPLIT, None, ALU.mult))
            me.step(v.tensor_scalar(b_hn, w_scale[:, M_HN:M_HN + 1], SPLIT, None, ALU.mult))
            me.link(v.reciprocal(deg[:], deg[:]))
            me.step(v.tensor_scalar(deg[:], deg[:], w_unscale[:, M_NEIGH:M_NEIGH + 1], None, ALU.mult))
            me.step(v.tensor_tensor(b_hn, b_hn, b_hh[:, 2:3], ALU.mult))
            me.step(v.tensor_tensor(brz, b_ih[:, 0:2], b_hh[:, 0:2], ALU.add))
            for i in range(2):
                me.step(v.tensor_scalar(tile(w_ih, i), raw[:, M_IH + i, :], ih_scale[:, i:i + 1], None, ALU.mult))
            me.step(copy(tile(w_ih, 2), raw[:, M_IH + 2, :]))
            for b, y2 in ((b3e, y2e), (b3l, y2l)):
                me.link(v.tensor_tensor_reduce(out=junk, in0=b, in1=b, scale=1.0, scalar=0.0, op0=ALU.mult,
                                               op1=ALU.add, accum_out=y2))
            v.memset(small[:, 51:52], 0.0).then_inc(S["w16_ready"], 1)

            def low_aggregate(g, count):
                dve.wait_ge(S["aThi_ready"], g + count + 1)
                src = agg[:, bass.ds((g + count) % 2, 1), :].rearrange("p a n -> p (a n)")
                v.scalar_tensor_tensor(aT16[:, 1, :], src, 1.0 / SPLIT, aT16[:, 0, :], ALU.mult,
                                       ALU.subtract).then_inc(S["aT_ready"], 1)

            with dve.Fori(0, NG) as g:
                me.loop(g, TG + 1 + 2 * TG + 1 + (TG - 1))
                low_aggregate(g, 0)
                dve.wait_ge(S["l1_self"], g + 1)
                dve.wait_ge(S["l1_neigh"], g + 1)
                for t in range(TG):
                    xt = x[:, tile_of(g, t), :].rearrange("p a d -> p (a d)")
                    me.step(v.scalar_tensor_tensor(xt, tile(bank[3], t), deg[:, tile_of(g, t)], xt, ALU.mult, ALU.add))
                me.settle()
                me.link(v.scalar_tensor_tensor(x[:, group_of(g), :], tiles(bank[4]), w_unsplit[:, M_SELF:M_SELF + 1],
                                               x[:, group_of(g), :], ALU.mult, ALU.add))
                statistics(g)
                high_operand(g, NG, tiles(dT))
                low_operand(g, NG, tiles(dT), hs_b)
            me.end(NG)

            C = col4

            def artanh_start(part):
                nrm, (clipped, floored) = pair(NE_Z, part), (pair(CL, part), pair(NRM, part))
                me.step(v.tensor_scalar(floored, nrm, EPS_BALL, None, ALU.max))
                v.tensor_scalar(clipped, nrm, EPS_BALL, MAX_TANH, ALU.max, ALU.min).then_inc(S["ln_in"], 1)

            def artanh_series(part, count):
                clipped, square, series = pair(CL, part), pair(PP, part), pair(SER, part)
                dve.wait_ge(S["ln_in"], count)
                me.link(v.tensor_tensor(square, clipped, clipped, ALU.mult))
                me.step(v.reciprocal(pair(KAP, part), pair(NRM, part)))
                me.link(v.tensor_scalar(series, square, 1.0 / 11, None, ALU.mult))
                for k in (9, 7, 5, 3):
                    me.link(v.scalar_tensor_tensor(series, series, 1.0 / k, square, ALU.add, ALU.mult))
                me.step(v.scalar_tensor_tensor(series, series, 1.0, clipped, ALU.add, ALU.mult))
                me.step(v.tensor_scalar(pair(MASK, part), clipped, SERIES_BELOW, None, ALU.is_lt))

            def artanh_finish(part, count):
                series, at = pair(SER, part), pair(AT, part)
                dve.wait_ge(S["ln_out"], count)
                me.link(v.tensor_tensor(at, pair(LNP, part), pair(LNM, part), ALU.subtract))
                me.link(v.scalar_tensor_tensor(series, at, -0.5, series, ALU.mult, ALU.add))
                me.link(v.tensor_tensor(series, series, pair(MASK, part), ALU.mult))
                me.link(v.scalar_tensor_tensor(at, at, 0.5, series, ALU.mult, ALU.add))
                me.link(v.tensor_tensor(pair(KAP, part), at, pair(KAP, part), ALU.mult))

            def dots(e_tiles, bias, scale):
                for t in range(TG):
                    me.step(v.tensor_tensor_reduce(out=tile(dve_junk, t), in0=e_tiles(t), in1=bias, scale=scale,
                                                   scalar=0.0, op0=ALU.mult, op1=ALU.add, accum_out=C(DOT)[:, t:t + 1]))

            def exp_argument(kappa):
                me.link(v.tensor_tensor(C(N2), C(NE_E), kappa, ALU.mult))
                v.tensor_scalar(C(N2), C(N2), EPS_BALL, None, ALU.max).then_inc(S["th_in"], 1)

            def sum_coefficients(kappa, th_count, y2):
                dve.wait_ge(S["th_in"], th_count)
                me.link(v.reciprocal(C(ALF), C(N2)))
                me.link(v.tensor_tensor(C(ALF), C(ALF), kappa, ALU.mult))
                dve.wait_ge(S["th_out"], th_count)
                me.link(v.tensor_tensor(C(ALF), C(ALF), C(TH), ALU.mult))
                me.step(v.tensor_tensor(C(XY), C(ALF), C(DOT), ALU.mult))
                me.link(v.tensor_tensor(C(X2), C(ALF), C(ALF), ALU.mult))
                me.step(v.tensor_scalar(C(TT), C(XY), 2.0, 1.0, ALU.mult, ALU.add))
                me.link(v.tensor_tensor(C(X2), C(X2), C(SSE), ALU.mult))
                me.step(v.scalar_tensor_tensor(C(NUM), C(TT), y2, C(ALF), ALU.add, ALU.mult))
                me.step(v.scalar_tensor_tensor(C(DEN), C(X2), y2, C(TT), ALU.mult, ALU.add))
                me.link(v.tensor_scalar(C(CB), C(X2), -1.0, 1.0, ALU.mult, ALU.add))
                me.link(v.tensor_scalar(C(DEN), C(DEN), EPS_BALL, None, ALU.max))
                me.link(v.reciprocal(C(DEN), C(DEN)))
                me.step(v.tensor_tensor(C(CA), C(NUM), C(DEN), ALU.mult))
                me.link(v.tensor_tensor(C(CB), C(CB), C(DEN), ALU.mult))

            def ball_rows(e_tiles, bias):
                for t in range(TG):
                    me.step(v.tensor_scalar(tile(z_rows, t), e_tiles(t), C(CA)[:, t:t + 1], None, ALU.mult))
                me.settle()
                for t in range(TG):
                    last = v.scalar_tensor_tensor(tile(z_rows, t), bias, C(CB)[:, t:t + 1], tile(z_rows, t), ALU.mult, ALU.add)
                    if t < TG - 1:
                        me.step(last)
                last.then_inc(S["z_ready"], 1)

            def layer2(a, b, c):
                A, B, E = a is not None, b is not None, c is not None
                if A:
                    low_aggregate(a, NG)
                if B:
                    dve.wait_ge(S["rs_ready"], b + 3 * NG + 1)
                    normalised(b, lambda t: tile(dT, t)).then_inc(S["xnew_ready"], 1)
                if E:
                    ball_rows(lambda t: tile(bank[3], t), b3e)
                if B:
                    dve.wait_ge(S["row16hi_ready"], b + 1)
                    v.scalar_tensor_tensor(row16[:, 1, :, :], tiles(dT), 0.0, row16[:, 0, :, :], ALU.max,
                                           ALU.subtract).then_inc(S["row16_ready"], 1)
                part = BOTH if B and E else H_ONLY if B else Z_ONLY
                count = b + 1 if B else NG + 1
                if E:
                    dve.wait_ge(S["nrmz_ready"], c + 1)
                if B:
                    dve.wait_ge(S["nrmh_ready"], b + 1)
                if B or E:
                    artanh_start(part)
                if B:
                    me.step(copy(ssh[:, group_of(b)], C(SSH)))
                if B or E:
                    artanh_series(part, count)
                if A:
                    me.step(v.tensor_tensor(dT, hT16[:, 0, :], hT16[:, 1, :], ALU.add))
                    dve.wait_ge(S["gates_full"], a + 1)
                    dve.wait_ge(S["rz_ready"], a + 1)
                    me.link(v.scalar_tensor_tensor(rT, bank[7], b_hn, rT, ALU.add, ALU.mult))
                    v.scalar_tensor_tensor(rT, rT, w_unsplit[:, M_HN:M_HN + 1], bank[6], ALU.mult,
                                           ALU.add).then_inc(S["t_ready"], 1)
                    dve.wait_ge(S["n_ready"], a + 1)
                    me.link(v.scalar_tensor_tensor(dT, dT, 1.0 / SPLIT, rT, ALU.mult, ALU.subtract))
                    me.link(v.tensor_tensor(zT, zT, dT, ALU.mult))
                    v.tensor_tensor(zT, zT, rT, ALU.add).then_inc(S["u_ready"], 1)
                if B or E:
                    artanh_finish(part, count)
                if E:
                    v.tensor_scalar(C(COEF), pair(KAP, Z_ONLY), SPLIT, None, ALU.mult).then_inc(S["coef_ready"], 1)
                if B:
                    dve.wait_ge(S["sqe_ready"], b + 1)
                    dots(lambda t: tile(bank[3], t), b3e, w_unsplit[:, M_EMB:M_EMB + 1])
                    dve.wait_ge(S["nrme_ready"], b + 1)
                    exp_argument(pair(KAP, H_ONLY))
                if A:
                    dve.wait_ge(S["uT_full"], a + 1)
                    v.tensor_tensor(x[:, group_of(a), :], x[:, group_of(a), :], tiles(bank[7]), ALU.add).then_inc(S["x3_ready"], 1)
                    dve.wait_ge(S["x3_ready"], a + 1)
                    statistics(a)
                if E:
                    dve.wait_ge(S["bhi_ready"], c + 1)
                    v.tensor_tensor(hs_a[:, group_of(c), 1, :], tiles(z_rows), hs_a[:, group_of(c), 0, :],
                                    ALU.subtract).then_inc(S["hs_ready"], 1)
                if B:
                    sum_coefficients(pair(KAP, H_ONLY), b + 1, y2e)
                    me.link(v.tensor_scalar(C(CA), C(CA), w_unsplit[:, M_EMB:M_EMB + 1], None, ALU.mult))
                if E:
                    dve.wait_ge(S["hs_ready"], c + 2 * NG + 1)

            layer2(0, None, None)
            layer2(1, 0, None)
            with dve.Fori(2, NG) as g:
                me.loop(g - 2, STEPS_2)
                layer2(g, g - 1, g - 2)
            me.end(NG - 2)
            layer2(None, NG - 1, NG - 2)
            layer2(None, None, NG - 1)

            def layer3(a, b):
                A, B = a is not None, b is not None

                def vrow(t):
                    return tile(dT, t)

                if A:
                    low_aggregate(a, 2 * NG)
                if B:
                    dve.wait_ge(S["nrmz_ready"], b + NG + 1)
                    artanh_start(Z_ONLY)
                    artanh_series(Z_ONLY, b + NG + 2)
                if A:
                    dve.wait_ge(S["norms_full"], a + 1)
                    copy(C(SSA), bank[5][:, 0:TG]).then_inc(S["ssa_ready"], 1)
                if B:
                    dots(vrow, b3l, 1.0)
                    artanh_finish(Z_ONLY, b + NG + 2)
                    dve.wait_ge(S["nrme_ready"], b + NG + 1)
                    exp_argument(pair(KAP, Z_ONLY))
                if A:
                    dve.wait_ge(S["nrmh_ready"], a + NG + 1)
                    v.tensor_scalar(C(N2A), C(NE_H), EPS_BALL, None, ALU.max).then_inc(S["tha_in"], 1)
                if B:
                    sum_coefficients(pair(KAP, Z_ONLY), b + NG + 1, y2l)
                if A:
                    dve.wait_ge(S["tha_in"], a + 1)
                    me.link(v.reciprocal(C(BETA), C(N2A)))
                    dve.wait_ge(S["tha_out"], a + 1)
                    me.link(v.tensor_tensor(C(BETA), C(BETA), C(THA), ALU.mult))
                    me.step(v.tensor_scalar(C(COEF), C(BETA), w_unscale[:, M_BOT:M_BOT + 1], None, ALU.mult))
                    me.link(v.tensor_tensor(C(SSC), C(BETA), C(BETA), ALU.mult))
                    me.link(v.tensor_tensor(C(SSC), C(SSC), C(SSA), ALU.mult))
                    v.tensor_tensor(C(SSC), C(SSC), ssh[:, group_of(a)], ALU.add).then_inc(S["ssc_ready"], 1)
                if B:
                    ball_rows(vrow, b3l)
                    dve.wait_ge(S["z_ready"], b + NG + 1)
                    v.tensor_tensor(x[:, group_of(b), :], x[:, group_of(b), :], tiles(z_rows), ALU.add).then_inc(S["x4_ready"], 1)
                if A:
                    dve.wait_ge(S["p1_in"], a * 16 + 16)
                    dve.wait_ge(S["p2_full"], a + 1)
                    for t in range(TG):
                        p1_t = p1_in[:, bass.ds(a % 2 * GW + t * D, D)] if not isinstance(a, int) else \
                            p1_in[:, a % 2 * GW + t * D:a % 2 * GW + (t + 1) * D]
                        last = v.scalar_tensor_tensor(vrow(t), tile(bank[3], t), C(COEF)[:, t:t + 1], p1_t, ALU.mult, ALU.add)
                        if t < TG - 1:
                            me.step(last)
                    last.then_inc(S["v_ready"], 1)
                    dve.wait_ge(S["v_ready"], a + 1)
                if B:
                    dve.wait_ge(S["x4_ready"], b + 1)

            layer3(0, None)
            with dve.Fori(1, NG) as g:
                me.loop(g - 1, STEPS_3)
                layer3(g, g - 1)
            me.end(NG - 1)
            layer3(None, NG - 1)

        @block.gpsimd
        def _(pool):
            q = nc.gpsimd

            def power(dst, src, half):
                return q.tensor_tensor(dst, src, half, ALU.pow)

            pool.wait_ge(S["consts_set"], 1)

            def inverse_deviation(g, count):
                pool.wait_ge(S["ve_ready"], g + count + 1)
                power(rs[:, group_of(g)], rs[:, group_of(g)], mhalf).then_inc(S["rs_ready"], 1)

            with pool.Fori(0, NG) as g:
                inverse_deviation(g, 0)
            pool.wait_ge(S["ext_ready"], 1)
            q.partition_all_reduce(extall, ext, P, bass.bass_isa.ReduceOp.max).then_inc(S["extall_ready"], 1)
            with pool.Fori(0, NG - 1) as g:
                inverse_deviation(g, NG)
            pool.wait_ge(S["top_ready"], 1)
            q.partition_all_reduce(topall, top, P, bass.bass_isa.ReduceOp.max).then_inc(S["topall_ready"], 1)
            inverse_deviation(NG - 1, NG)
            pool.wait_ge(S["flag_ready"], 1)
            general = pool.value_load(flag, min_val=0, max_val=1)
            with pool.If(general > 0):
                for first, per in ((TURN_ROWS, TURNS_ROWS), (TURN_OPERAND, TURNS_OPERAND)):
                    with pool.Fori(0, NT) as i:
                        pool.wait_ge(S["turn"], i * per + (first + 3))
                        power(grs, grs, mhalf[:, 0:1]).then_inc(S["turn"], 1)
                pool.wait_ge(S["turn"], TURN_END + 1)
            with pool.Fori(0, NG) as g:
                inverse_deviation(g, 2 * NG)

            def norm_h(g):
                pool.wait_ge(S["ssh_ready"], g + 1)
                power(col4(NE_H), col4(SSH), phalf).then_inc(S["nrmh_ready"], 1)

            def norm_e(g, count):
                pool.wait_ge(S["sqe_ready"], g + count + 1)
                power(col4(NE_E), col4(SSE), phalf).then_inc(S["nrme_ready"], 1)

            def norm_z(g):
                pool.wait_ge(S["sqz_ready"], g + 1)
                power(col4(NE_Z), col4(SSZ), phalf).then_inc(S["nrmz_ready"], 1)

            inverse_deviation(0, 3 * NG)
            with pool.Fori(1, NG) as g:
                norm_h(g - 1)
                norm_e(g - 1, 0)
                inverse_deviation(g, 3 * NG)
                norm_z(g - 1)
            norm_h(NG - 1)
            norm_e(NG - 1, 0)
            norm_z(NG - 1)

            def norms_3(g):
                pool.wait_ge(S["ssa_ready"], g + 1)
                power(col4(NE_H), col4(SSA), phalf).then_inc(S["nrmh_ready"], 1)
                pool.wait_ge(S["ssc_ready"], g + 1)
                power(col4(NE_Z), col4(SSC), phalf).then_inc(S["nrmz_ready"], 1)

            norms_3(0)
            with pool.Fori(1, NG) as g:
                norm_e(g - 1, NG)
                norms_3(g)
            norm_e(NG - 1, NG)

        @block.scalar
        def _(act):
            a = nc.scalar

            def convert(n):
                act.wait_ge(S["landed"], n + 1)
                adj_flat = adj[:].rearrange("p i j n -> p (i j n)")
                a.activation(adj_flat[:, bass.ds(n * PIECE + DVE_PART, PIECE - DVE_PART)],
                             region_st[:, bass.ds((n % NBUF) * PIECE + DVE_PART, PIECE - DVE_PART)], ACT.Copy,
                             scale=ONE_FP8).then_inc(S["conv_s"], 1)

            def relu_rows_T(g):
                act.wait_ge(S["tr0_full"], g + 1)
                dst = hT_early[:, bass.ds(g % 2, 1), :].rearrange("p a n -> p (a n)") if not isinstance(g, int) else hT_early[:, g % 2, :]
                a.activation(dst, bank[4], ACT.Relu, scale=1.0 / SPLIT).then_inc(S["hT0_ready"], 1)

            def projections(g):
                act.wait_ge(S["xp_full"], g + 1)
                for half in range(2):
                    b = bank[5 + half][:, 0:2 * (D + HEADS)].rearrange("p (t c) -> p t c", c=D + HEADS)
                    a.activation(xp[:, bass.ds(g * TG + 2 * half, 2), :], b[:, :, 0:D], ACT.Copy)
                    last = a.activation(w[:, bass.ds(g * TG + 2 * half, 2), :], b[:, :, D:D + HEADS], ACT.Copy)
                last.then_inc(S["xp_read"], 1)

            with act.Fori(0, NG) as g:
                convert(g)
            relu_rows_T(0)
            with act.Fori(1, NG) as g:
                convert(g + NG * PIECES_STATS - 1)
                relu_rows_T(g)
                projections(g - 1)
            projections(NG - 1)
            convert(NG * (PIECES_STATS + PIECES_PROJ) - 1)
            convert(FIRST_SPLIT - 2)
            act.wait_ge(S["shift_ready"], 1)
            for h in range(HEADS):
                wh = w[:, :, h:h + 1].rearrange("p t a -> p (t a)")
                a.activation(wh, wh, ACT.Exp, bias=shift[:, h:h + 1], scale=SCALE).then_inc(S["w_ready"], 1)
            act.wait_ge(S["w_ready"], HEADS)
            a.copy(op0[:, :, D:D + HEADS], w[:]).then_inc(S["whi_ready"], 1)
            convert(FIRST_SPLIT - 1)
            with act.Fori(0, NG) as g:
                act.wait_ge(S["y_ready"], g + 1)
                a.copy(op0[:, group_of(g), 0:D], xp[:, group_of(g), :]).then_inc(S["hi0_ready"], 1)
                convert(g + FIRST_SPLIT)

            def high_part(g, cnt, src, hs, func):
                act.wait_ge(S["xnew_ready"], g + cnt + 1)
                a.activation(hs[:, group_of(g), 0, :], src, func).then_inc(S["hi_ready"], 1)

            convert(FIRST_MAIN)
            with act.Fori(0, NG - 1) as g:
                for i in range(1, PIECES_MAIN):
                    convert(g * PIECES_MAIN + (FIRST_MAIN + i))
                convert(g * PIECES_MAIN + (FIRST_MAIN + PIECES_MAIN))
                high_part(g, 0, xn, hs_a, ACT.Relu)
            for n in range(FIRST_MAIN + (NG - 1) * PIECES_MAIN + 1, NPIECE):
                convert(n)
            high_part(NG - 1, 0, xn, hs_a, ACT.Relu)

            def own_rows_T(g, cnt):
                act.wait_ge(S["pre_tr"], g + cnt + 1)
                a.activation(hT16, tr16, ACT.Copy).then_inc(S["pre_hT"], 1)

            def high_aggregate(g, cnt, square):
                act.wait_ge(S["agg_full"], g + cnt + 1)
                src = agg[:, bass.ds((g + cnt) % 2, 1), :].rearrange("p a n -> p (a n)")
                if square:
                    a.activation(msgT, src, ACT.Square, scale=1.0 / SPLIT)
                a.activation(aT16[:, 0, :], src, ACT.Copy, scale=1.0 / SPLIT).then_inc(S["aThi_ready"], 1)

            def square_sums(src, sums, scale=1.0):
                for t in range(TG):
                    last = a.activation(tile(junk8, t), src(t), ACT.Square, scale=scale, accum_out=sums[:, t:t + 1])
                return last

            def logarithms(part, n):
                act.wait_ge(S["ln_in"], n)
                a.activation(pair(LNP, part), pair(CL, part), ACT.Ln, bias=1.0)
                a.activation(pair(LNM, part), pair(CL, part), ACT.Ln, bias=1.0, scale=-1.0).then_inc(S["ln_out"], 1)

            def tanh_of(n):
                act.wait_ge(S["th_in"], n)
                a.activation(col4(TH), col4(N2), ACT.Tanh).then_inc(S["th_out"], 1)

            act.wait_ge(S["flag_ready"], 1)
            general = act.value_load(flag, min_val=0, max_val=1)
            with act.If(general > 0):
                with act.Fori(0, NT) as i:
                    for h in range(HEADS):
                        k = CHUNKS * TURNS_MASK + h * TURNS_HEAD + 4 + CHUNKS * TURNS_LOGITS + 2
                        act.wait_ge(S["turn"], i * TURNS_TILE + (TURN_ATTEND + k))
                        a.activation(logits, logits, ACT.Exp, bias=gmax, accum_out=gden).then_inc(S["turn"], 1)
                act.wait_ge(S["turn"], TURN_END + 1)

            with act.Fori(0, NG) as g:
                own_rows_T(g, 0)
                high_aggregate(g, 0, False)
                high_part(g, NG, tiles(dT), hs_b, ACT.Relu)

            def layer2(s, b, c):
                A, B, E = s is not None, b is not None, c is not None
                if A:
                    if not (isinstance(s, int) and s == 0):
                        act.wait_ge(S["u_ready"], s)
                    own_rows_T(s, NG)
                    high_aggregate(s, NG, False)
                if B:
                    act.wait_ge(S["xnew_ready"], b + 2 * NG + 1)
                    a.activation(row16[:, 0, :, :], tiles(dT), ACT.Relu).then_inc(S["row16hi_ready"], 1)
                if A:
                    act.wait_ge(S["msg_full"], s + 1)
                    a.activation(msgT, bank[6], ACT.Relu, bias=b_msg, scale=w_unscale[:, M_MSG:M_MSG + 1]).then_inc(S["msg_ready"], 1)
                if E:
                    act.wait_ge(S["z_ready"], c + 1)
                    square_sums(lambda t: tile(z_rows, t), col4(SSZ)).then_inc(S["sqz_ready"], 1)
                if B:
                    act.wait_ge(S["row16_ready"], b + 1)
                    a.activation(dT, dT, ACT.Relu).then_inc(S["relu_ready"], 1)
                    act.wait_ge(S["relu_ready"], b + 1)
                    square_sums(lambda t: tile(dT, t), col4(SSH), 1.0 / SPLIT).then_inc(S["ssh_ready"], 1)
                if A:
                    act.wait_ge(S["gates_full"], s + 1)
                    a.activation(rT, bank[4], ACT.Sigmoid, bias=brz[:, 0:1], scale=w_unsplit[:, M_HR:M_HR + 1])
                    a.activation(zT, bank[5], ACT.Sigmoid, bias=brz[:, 1:2], scale=w_unsplit[:, M_HZ:M_HZ + 1]).then_inc(S["rz_ready"], 1)
                if B:
                    act.wait_ge(S["h3_tr"], b + 1)
                    a.activation(h3T16, tr16, ACT.Copy).then_inc(S["h3T_ready"], 1)
                if A:
                    act.wait_ge(S["t_ready"], s + 1)
                    a.activation(rT, rT, ACT.Tanh, bias=b_ih[:, 2:3]).then_inc(S["n_ready"], 1)
                if B or E:
                    logarithms(BOTH if B and E else H_ONLY if B else Z_ONLY, b + 1 if B else NG + 1)
                if B:
                    act.wait_ge(S["emb_full"], b + 1)
                    square_sums(lambda t: tile(bank[3], t), col4(SSE), w_unsplit[:, M_EMB:M_EMB + 1]).then_inc(S["sqe_ready"], 1)
                    act.wait_ge(S["top_full"], b + 1)
                    act.wait_ge(S["p1_out"], b * 16 + 16)
                    a.activation(p1_sb, bank[4], ACT.Copy, scale=w_unsplit[:, M_TOP:M_TOP + 1]).then_inc(S["p1_ready"], 1)
                    tanh_of(b + 1)
                if E:
                    act.wait_ge(S["coef_ready"], c + 1)
                    act.wait_ge(S["sqz_ready"], c + 1)
                    for t in range(TG):
                        r = tile(z_rows, t)
                        last = a.activation(r, r, ACT.Copy, scale=col4(COEF)[:, t:t + 1])
                    last.then_inc(S["zs_ready"], 1)
                    act.wait_ge(S["zs_ready"], c + 1)
                    a.activation(hs_a[:, group_of(c), 0, :], tiles(z_rows), ACT.Copy).then_inc(S["bhi_ready"], 1)

            act.wait_ge(S["w16_ready"], 1)
            layer2(0, None, None)
            layer2(1, 0, None)
            with act.Fori(2, NG) as g:
                layer2(g, g - 1, g - 2)
            layer2(None, NG - 1, NG - 2)
            layer2(None, None, NG - 1)

            def layer3(c, b):
                A, B = c is not None, b is not None
                if A:
                    if B:
                        act.wait_ge(S["p2_full"], b + 1)
                    high_aggregate(c, 2 * NG, True)
                if B:
                    act.wait_ge(S["v_ready"], b + 1)
                    square_sums(lambda t: tile(dT, t), col4(SSE)).then_inc(S["sqe_ready"], 1)
                    logarithms(Z_ONLY, b + NG + 2)
                    tanh_of(b + NG + 1)
                if A:
                    act.wait_ge(S["tha_in"], c + 1)
                    a.activation(col4(THA), col4(N2A), ACT.Tanh).then_inc(S["tha_out"], 1)

            layer3(0, None)
            with act.Fori(1, NG) as g:
                layer3(g, g - 1)
            layer3(None, NG - 1)

        @block.tensor
        def _(pe):
            mm = nc.tensor.matmul
            adj8 = adj[:].bitcast(fp8)

            def transposes(src, dst):
                for t in range(TG):
                    last = nc.tensor.transpose(dst[:, t * D:(t + 1) * D], src(t), ident[:])
                return last

            def per_tile(srcT, weights, dst):
                for t in range(TG):
                    last = mm(dst[:, t * D:(t + 1) * D], srcT[:, t * D:(t + 1) * D], weights, start=True, stop=True)
                return last

            pe.wait_ge(S["proj_in"], 16)
            mm(bank[4][:, 0:HEADS], pw[:, D:2 * D], pw[:, 2 * D:2 * D + HEADS], start=True, stop=True).then_inc(S["wa_full"], 1)
            pe.wait_ge(S["wa_done"], 1)
            pe.wait_ge(S["c0_in"], 16)
            for g in range(NG):
                pe.wait_ge(S["xn0_ready"], g + 1)
                transposes(lambda t: xn_early[:, g % 2, t, :], bank[4]).then_inc(S["tr0_full"], 1)
                pe.wait_ge(S["hT0_ready"], g + 1)
                if g:
                    pe.wait_ge(S["xp_read"], g)
                for t in range(TG):
                    half, s = t // 2, (t % 2) * (D + HEADS)
                    last = mm(bank[5 + half][:, s:s + D + HEADS], hT_early[:, g % 2, t * D:(t + 1) * D], pwa,
                              start=True, stop=True)
                last.then_inc(S["xp_full"], 1)

            pe.wait_ge(S["wlo_ready"], 1)

            def attend(it, jts):
                for jt in jts:
                    mm(bank[it % (2 * TG)][:, 0:HI], adj8[:, it, jt, :], op0[:, jt, 0:HI], start=(jt == 0), stop=False)
                    last = mm(bank[it % (2 * TG)][:, 0:LO], adj8[:, it, jt, :], op0[:, jt, HI:OPW], start=False,
                              stop=(jt == NT - 1))
                return last

            def tile_is_in(it):
                pe.wait_ge(S["conv_v"], 2 * (it + 1))
                pe.wait_ge(S["conv_s"], 2 * (it + 1))

            for g in range(NG):
                pe.wait_ge(S["op0_ready"], g + 1)
                for it in range(2 * TG):
                    if g == 0:
                        tile_is_in(it)
                    last = attend(it, range(g * TG, (g + 1) * TG))
                    if g == NG - 1:
                        last.then_inc(S["acc_full"], 1)
            for it in range(2 * TG, NT):
                tile_is_in(it)
                if it % TG == 0:
                    pe.wait_ge(S["acc_read"], it // TG - 1)
                attend(it, range(NT)).then_inc(S["acc_full"], 1)

            def split_transposes(src):
                for part in range(2):
                    for t in range(TG):
                        last = nc.tensor.transpose(tr16[:, part, t * D:(t + 1) * D], src(part, t), ident16[:])
                return last

            def rows_times(srcT, m, dst):
                for t in range(TG):
                    for part, other in ((0, 0), (0, 1), (1, 0)):
                        last = mm(tile(dst, t), srcT[:, part, t * D:(t + 1) * D], w16[:, other, m, :],
                                  start=(part + other == 0), stop=(part == 1))
                return last

            def matrix_times(m, srcT, dst, stop=True):
                for other, part in ((0, 0), (0, 1), (1, 0)):
                    last = mm(dst, w16[:, other, m, :], srcT[:, part, :], start=(part + other == 0), stop=(stop and other == 1))
                return last

            def own_transposes(s):
                c = s % NG
                if s == 0:
                    pe.wait_ge(S["w16_ready"], 1)
                hs = hs_a if s < NG else hs_b
                split_transposes(lambda part, t: hs[:, c * TG + t, part, :]).then_inc(S["pre_tr"], 1)

            def own_self(s):
                pe.wait_ge(S["pre_hT"], s + 1)
                if s:
                    pe.wait_ge(S["xnew_ready"], s + NG)
                else:
                    pe.wait_ge(S["w16_ready"], 1)
                rows_times(hT16, M_SELF, bank[4]).then_inc(S["l1_self"], 1)

            def neighbours(s):
                pe.wait_ge(S["aT_ready"], s + 1)
                rows_times(aT16, M_NEIGH, bank[3]).then_inc(S["l1_neigh"], 1)

            def hidden_gates(s):
                pe.wait_ge(S["pre_hT"], s + 1)
                if s > NG:
                    pe.wait_ge(S["rz_ready"], s - NG)
                    pe.wait_ge(S["x3_ready"], s - NG)
                    if s > NG + 1:
                        pe.wait_ge(S["p1_ready"], s - NG - 1)
                else:
                    pe.wait_ge(S["hs_ready"], 2 * NG)
                matrix_times(M_HR, hT16, bank[4], stop=False)
                matrix_times(M_HZ, hT16, bank[5], stop=False)
                matrix_times(M_HN, hT16, bank[7])

            def message(s):
                pe.wait_ge(S["aT_ready"], s + 1)
                if s > NG:
                    pe.wait_ge(S["t_ready"], s - NG)
                matrix_times(M_MSG, aT16, bank[6]).then_inc(S["msg_full"], 1)

            def message_gates(s):
                pe.wait_ge(S["msg_ready"], s - NG + 1)
                mm(bank[4], tile(w_ih, 0), msgT, start=False, stop=True)
                mm(bank[5], tile(w_ih, 1), msgT, start=False, stop=True)
                mm(bank[6], tile(w_ih, 2), msgT, start=True, stop=True).then_inc(S["gates_full"], 1)

            def update_back(s):
                pe.wait_ge(S["u_ready"], s - NG + 1)
                for t in range(TG):
                    last = nc.tensor.transpose(tile(bank[7], t), tile(zT, t), ident[:])
                last.then_inc(S["uT_full"], 1)

            def new_transposes(s):
                pe.wait_ge(S["row16_ready"], s - NG + 1)
                split_transposes(lambda part, t: row16[:, part, t, :]).then_inc(S["h3_tr"], 1)

            def embed(s):
                pe.wait_ge(S["h3T_ready"], s - NG + 1)
                if s > NG:
                    pe.wait_ge(S["z_ready"], s - NG)
                rows_times(h3T16, M_EMB, bank[3]).then_inc(S["emb_full"], 1)

            def own_part(s):
                if s > NG:
                    pe.wait_ge(S["p1_ready"], s - NG)
                if s + 1 < 2 * NG:
                    pe.wait_ge(S["rz_ready"], s - NG + 2)
                rows_times(h3T16, M_TOP, bank[4]).then_inc(S["top_full"], 1)

            def norms(s):
                pe.wait_ge(S["aT_ready"], s + 1)
                for t in range(TG):
                    last = mm(bank[5][:, t:t + 1], tile(msgT, t), ones_col, start=True, stop=True)
                last.then_inc(S["norms_full"], 1)

            def bottom(s):
                pe.wait_ge(S["aT_ready"], s + 1)
                if s == 2 * NG:
                    pe.wait_ge(S["z_ready"], NG)
                rows_times(aT16, M_BOT, bank[3]).then_inc(S["p2_full"], 1)

            own = {1: {50: own_transposes, 60: own_self}, 2: {62: own_transposes}, 3: {}}
            after = {1: {8: neighbours},
                     2: {1: hidden_gates, 6: message, 11: message_gates},
                     3: {11: norms, 13: bottom}}
            late = {15: new_transposes, 26: embed, 32: own_part}
            back = {44: update_back}
            FIRST, SECOND, THIRD = 2 * NG, 2 * NG + 1, 2 * NG + 2
            both_zero = {10: own_transposes, 16: own_self, 24: neighbours}
            after_first = {8: norms, 9: bottom}
            after_second = {34: norms, 35: bottom}

            def aggregate(s, first, end):
                layer, c = s // NG + 1, s % NG
                hs = hs_b if layer == 2 else hs_a
                if s >= 2 and first == 0:
                    pe.wait_ge(S["aT_ready"], s - 1)
                dst = agg[:, s % 2, :].rearrange("p (a b) -> p a b", a=TG)
                for k in range(first, end):
                    jt, part = k // 2, k % 2
                    if s == THIRD and k in after_first:
                        after_first[k](FIRST)
                    if s == THIRD and k in after_second:
                        after_second[k](SECOND)
                    if s == 1 and k in both_zero:
                        both_zero[k](0)
                    if k and s not in (0, 1, SECOND, THIRD) and k in after[(s - 1) // NG + 1]:
                        after[(s - 1) // NG + 1][k](s - 1)
                    if k in late and NG <= s - 2 < 2 * NG - 1:
                        late[k](s - 2)
                    if k in back and NG <= s - 1 < 2 * NG - 1:
                        back[k](s - 1)
                    if s and k in own[layer]:
                        own[layer][k](s)
                    if (c == 0 or s == SECOND) and jt % TG == 0 and part == 0:
                        pe.wait_ge(S["hs_ready"], (layer - 1) * NG + jt // TG + 1)
                    last = mm(dst, hs[:, jt, part, :], adj8[:, c * TG:(c + 1) * TG, jt, :],
                              start=(k == 0), stop=(k == 2 * NT - 1))
                if end == 2 * NT:
                    last.then_inc(S["agg_full"], 1)

            aggregate(0, 0, 36)
            pe.wait_ge(S["acc_read"], NG)
            pe.wait_ge(S["odd_ready"], 1)
            mm(bank[4][0:1, 0:1], odd, ones_col, start=True, stop=True).then_inc(S["odd_sum"], 1)
            aggregate(0, 36, 56)
            pe.wait_ge(S["flag_ready"], 1)
            general = pe.value_load(flag, min_val=0, max_val=1)
            with pe.If(general > 0):
                mm(bank[0].rearrange("p (a b) -> p a b", a=TG), hs_a[:, 0, 0, :], adj8[:, 0:TG, 0, :], start=False, stop=True)
                turn = S["turn"]
                pe.wait_ge(turn, 1)
                mm(bank[0][:, 0:2 * HEADS], gw[:, D:2 * D], gw[:, 2 * D:2 * D + 2 * HEADS], start=True, stop=True).then_inc(turn, 1)
                with pe.Fori(0, NT) as i:
                    at = i * TURNS_ROWS + TURN_ROWS
                    pe.wait_ge(turn, at + 6)
                    nc.tensor.transpose(bank[0][:, 0:D], gxn, ident[:]).then_inc(turn, 1)
                    pe.wait_ge(turn, at + 9)
                    mm(bank[1][:, 0:D], tile(pT, 0), gw[:, 0:D], start=True, stop=True).then_inc(turn, 1)
                with pe.Fori(0, NT) as i:
                    at = i * TURNS_TILE + TURN_ATTEND
                    for c in range(CHUNKS):
                        pe.wait_ge(turn, at + (c * TURNS_MASK + 1))
                        for t in range(TG):
                            last = mm(tile(bank[0], t), a16[:, t * P:(t + 1) * P], ident16[:], start=True, stop=True)
                        last.then_inc(turn, 1)
                    for h in range(HEADS):
                        k = CHUNKS * TURNS_MASK + h * TURNS_HEAD
                        pe.wait_ge(turn, at + (k + 2))
                        mm(bank[1][:, 0:1], tile(pT, 0), wa[:, HEADS + h:HEADS + h + 1],
                           start=True, stop=True).then_inc(turn, 1)
                        for c in range(CHUNKS):
                            pe.wait_ge(turn, at + (k + 4 + c * TURNS_LOGITS))
                            mm(bank[2], wa_wide, hT_all[:, c * GW:(c + 1) * GW], start=True, stop=True).then_inc(turn, 1)
                        k += 4 + CHUNKS * TURNS_LOGITS + 5
                        for c in range(CHUNKS):
                            pe.wait_ge(turn, at + (k + c * TURNS_OUT))
                            transposes(lambda t: logits[:, (c * TG + t) * P:(c * TG + t + 1) * P], bank[3]).then_inc(turn, 1)
                            pe.wait_ge(turn, at + (k + c * TURNS_OUT + 2))
                            for t in range(TG):
                                last = mm(bank[4][:, 0:HD], tile(pT, t), xp[:, c * TG + t, h * HD:(h + 1) * HD],
                                          start=(t == 0), stop=(t == TG - 1))
                            last.then_inc(turn, 1)
                pe.wait_ge(turn, TURN_END + 1)
                aggregate(0, 0, 56)
            aggregate(0, 56, 2 * NT)
            for s in range(1, 2 * NG):
                aggregate(s, 0, 2 * NT)
            aggregate(FIRST, 0, 36)
            update_back(FIRST - 1)
            aggregate(SECOND, 0, 40)
            aggregate(FIRST, 36, 40)
            new_transposes(FIRST - 1)
            embed(FIRST - 1)
            own_part(FIRST - 1)
            for k in (40, 48, 56):
                aggregate(FIRST, k, k + 8)
                aggregate(SECOND, k, k + 8)
            for s in range(THIRD, 3 * NG):
                aggregate(s, 0, 2 * NT)
            norms(3 * NG - 1)
            bottom(3 * NG - 1)


def kernel(**inputs):
    import numpy as _np
    import concourse.bacc as _bacc
    from concourse import mybir as _mybir
    from concourse.bass_utils import run_bass_kernel_spmd as _run

    g = {k: _np.asarray(v) for k, v in inputs.items()}
    f = _np.float32
    rows = lambda b: _np.broadcast_to(b[None, :], (P, D))
    blocks = _np.zeros((D, 2 * HEADS), f)
    for h in range(HEADS):
        blocks[h * HD:(h + 1) * HD, h] = g["L0_gnn_a"][:HD]
        blocks[h * HD:(h + 1) * HD, HEADS + h] = g["L0_gnn_a"][HD:]
    arrays = {
        "x_rows": g["x"].reshape(NT, P, D).transpose(1, 0, 2),
        "adj_pieces": g["adj"].reshape(NT, P, 2, PIECE_T, P).transpose(0, 2, 4, 3, 1).reshape(NPIECE, P, PIECE),
        "proj": _np.concatenate([g["L0_gnn_W"], g["L0_gnn_W"].T, blocks], axis=1),
        "consts0": _np.eye(P, dtype=f),
        "matrices": _np.concatenate([
            g["L1_gnn_W_self"], g["L1_gnn_W_neigh"], g["L2_gnn_W_msg"].T, g["L2_gnn_W_hh"].T, g["L3_gnn_embed"],
            g["L3_gnn_layer"][:D], g["L3_gnn_layer"][D:], g["L2_gnn_W_ih"].T], axis=1),
        "vectors": _np.concatenate([
            rows(g["L3_gnn_embed_bias"]), rows(g["L3_gnn_layer_bias"]), g["L2_gnn_b_msg"][:, None],
            g["L2_gnn_b_ih"].reshape(3, D).T, g["L2_gnn_b_hh"].reshape(3, D).T, _np.zeros((P, 1), f)], axis=1),
    }
    arrays = {k: _np.ascontiguousarray(a) for k, a in arrays.items()}
    nc = _bacc.Bacc("TRN2", target_bir_lowering=False, num_devices=1)
    args = [nc.dram_tensor(k, a.shape, _mybir.dt.from_np(a.dtype), kind="ExternalInput").ap() for k, a in arrays.items()]
    p1 = nc.dram_tensor("p1_rows", (P, NT, D), _mybir.dt.float32, kind="Internal").ap()
    out = nc.dram_tensor("out_rows", (P, NT, D), _mybir.dt.float32, kind="ExternalOutput").ap()
    build_graph_stack(nc, *args, p1, out)
    r = _run(nc, [arrays], core_ids=[0])
    return r.results[0]["out_rows"].transpose(1, 0, 2).reshape(N, D)
```
